# Optimizing a Trainium2 kernel written in Bass

```python
import numpy as np
import jax
import jax.numpy as jnp

def _softmax(x, axis=-1):
    return jax.nn.softmax(x, axis=axis)

def _gelu(x):
    return jax.nn.gelu(x, approximate=True)

def _silu(x):
    return jax.nn.silu(x)

def _sigmoid(x):
    return jax.nn.sigmoid(x)

def _layernorm(x, axis=-1, eps=1e-05):
    m = jnp.mean(x, axis=axis, keepdims=True)
    v = jnp.var(x, axis=axis, keepdims=True)
    return (x - m) / jnp.sqrt(v + eps)

def _scatter_add(tgt, idx, src, axis=0):
    return tgt.at[idx].add(src)

def _segment_sum(src, seg, n):
    return jax.ops.segment_sum(src, seg, n)
kernel_name = 'mk_xattn_ffn_d4_seqx_r8_f45ad8'

def setup_inputs(seed: int=0):
    np.random.seed(seed)
    _w = jnp.asarray

    def _rec_inputs():
        import jax
        import jax.numpy as jnp
        _rk = jax.random.key(seed)
        x = 7.22e-05 + 1 * jax.random.normal(jax.random.fold_in(_rk, 1), (4, 256, 128), jnp.float32)
        _lenS = 256 - jax.random.randint(jax.random.fold_in(_rk, 7), (4,), 0, max(1, 256 // 4) + 1, jnp.int32)
        _lenS2 = 256 - jax.random.randint(jax.random.fold_in(_rk, 8), (4,), 0, max(1, 256 // 4) + 1, jnp.int32)
        _ctx_1024P = jax.random.normal(jax.random.fold_in(_rk, 11), (4, 16, 128), jnp.float32)
        _ctx_1024c = jax.random.dirichlet(jax.random.fold_in(_rk, 511), 0.3 * jnp.ones((16,), jnp.float32), (4, 256))
        _ctx_1024t = jnp.einsum('bsk,bkd->bsd', _ctx_1024c, _ctx_1024P)
        _ctx_1024t = _ctx_1024t * jax.lax.rsqrt(jnp.mean(jnp.square(_ctx_1024t)) + 1e-12) * 0.953939
        ctx_1024 = 4.13588e-05 + 0.999923 * (_ctx_1024t + 0.3 * jax.random.normal(jax.random.fold_in(_rk, 611), (4, 256, 128), jnp.float32))
        _validS = jnp.arange(256)[None, :] < _lenS[:, None]
        _validS2 = jnp.arange(256)[None, :] < _lenS2[:, None]
        _causal = jnp.tril(jnp.ones((256, 256), dtype=bool))
        mask_BxS2_bf1 = jnp.ones((4, 256), dtype=bool)
        mask_1x1xSxS2_if1 = jnp.where(jnp.ones((1, 1, 256, 256), dtype=bool), 1, 0).astype(jnp.int32)
        return (x, ctx_1024, _lenS2, mask_BxS2_bf1, mask_1x1xSxS2_if1)
    x, ctx_1024, _lenS2, mask_BxS2_bf1, mask_1x1xSxS2_if1 = _rec_inputs()

    def _L0_xattn_setup():
        import jax, jax.numpy as jnp
        import numpy as np
        B, L, D, H = (4, 256, 128, 8)
        DH = D // H
        NEG = float(-2 ** 32 + 1)
        key = jax.random.key(seed)
        ks = jax.random.split(key, 7)
        queries = jax.random.normal(ks[0], (B, L, D), dtype=jnp.float32)
        keys = jax.random.normal(ks[1], (B, L, D), dtype=jnp.float32)
        sequence_length = jax.random.randint(ks[2], (B,), 1, L + 1, dtype=jnp.int32)
        scale = 0.02
        W_q = jax.random.normal(ks[3], (D, D), dtype=jnp.float32) * scale
        W_k = jax.random.normal(ks[4], (D, D), dtype=jnp.float32) * scale
        W_v = jax.random.normal(ks[5], (D, D), dtype=jnp.float32) * scale
        W_o = jax.random.normal(ks[6], (D, D), dtype=jnp.float32) * scale
        return {'queries': queries, 'keys': keys, 'sequence_length': sequence_length, 'W_q': W_q, 'W_k': W_k, 'W_v': W_v, 'W_o': W_o}
    _L0_xattn_all = _L0_xattn_setup()
    _L0_xattn_in = {k: v for k, v in _L0_xattn_all.items() if k in ('W_q', 'W_k', 'W_v', 'W_o')}
    del _L0_xattn_all

    def _L0_ffn_setup():
        import jax, jax.numpy as jnp
        import numpy as np
        D_MODEL = 128
        D_FF = 512
        N_EXPERTS = 8
        TOP_K = 2

        def _ffn(x, w1, b1, w2, b2):
            h = jax.nn.gelu(x @ w1.T + b1)
            return h @ w2.T + b2
        key = jax.random.key(seed)
        ks = jax.random.split(key, 12)
        s = 0.02
        x = jax.random.normal(ks[0], (4, 256, D_MODEL), dtype=jnp.float32)
        shared_w1 = jax.random.normal(ks[1], (D_FF, D_MODEL), dtype=jnp.float32) * s
        shared_b1 = jnp.zeros((D_FF,), dtype=jnp.float32)
        shared_w2 = jax.random.normal(ks[2], (D_MODEL, D_FF), dtype=jnp.float32) * s
        shared_b2 = jnp.zeros((D_MODEL,), dtype=jnp.float32)
        router_w = jax.random.normal(ks[3], (N_EXPERTS, D_MODEL), dtype=jnp.float32) * s
        router_b = jnp.zeros((N_EXPERTS,), dtype=jnp.float32)
        spec_w1 = jax.random.normal(ks[4], (N_EXPERTS, D_FF, D_MODEL), dtype=jnp.float32) * s
        spec_b1 = jnp.zeros((N_EXPERTS, D_FF), dtype=jnp.float32)
        spec_w2 = jax.random.normal(ks[5], (N_EXPERTS, D_MODEL, D_FF), dtype=jnp.float32) * s
        spec_b2 = jnp.zeros((N_EXPERTS, D_MODEL), dtype=jnp.float32)
        return dict(x=x, shared_w1=shared_w1, shared_b1=shared_b1, shared_w2=shared_w2, shared_b2=shared_b2, router_w=router_w, router_b=router_b, spec_w1=spec_w1, spec_b1=spec_b1, spec_w2=spec_w2, spec_b2=spec_b2)
    _L0_ffn_all = _L0_ffn_setup()
    _L0_ffn_in = {k: v for k, v in _L0_ffn_all.items() if k in ('shared_w1', 'shared_b1', 'shared_w2', 'shared_b2', 'router_w', 'router_b', 'spec_w1', 'spec_b1', 'spec_w2', 'spec_b2')}
    del _L0_ffn_all

    def _L1_xattn_setup():
        import jax, jax.numpy as jnp
        import numpy as np
        B, T, M, E, H = (8, 64, 128, 128, 8)
        MAX_LEN = 128

        def sinusoidal_table(max_len, n_model):
            pos = jnp.concatenate([jnp.arange(-(max_len // 2), 0, dtype=jnp.float32), jnp.arange(0, max_len // 2, dtype=jnp.float32)])
            inv = 10000.0 ** ((jnp.arange(n_model) // 2 * 2).astype(jnp.float32) / n_model)
            w = pos[:, None] / inv[None, :]
            even = jnp.sin(w[:, 0::2])
            odd = jnp.cos(w[:, 1::2])
            out = jnp.zeros((max_len, n_model), jnp.float32)
            out = out.at[:, 0::2].set(even)
            out = out.at[:, 1::2].set(odd)
            return out
        key = jax.random.key(seed)
        ks = jax.random.split(key, 10)
        s = 0.02
        return {'q': jax.random.normal(ks[0], (B, T, M), jnp.float32), 'k': jax.random.normal(ks[1], (B, T, M), jnp.float32), 'v': jax.random.normal(ks[2], (B, T, M), jnp.float32), 'mask': jnp.ones((B, T), dtype=bool), 'wq': jax.random.normal(ks[3], (M, E, H), jnp.float32) * s, 'wk': jax.random.normal(ks[4], (M, E, H), jnp.float32) * s, 'wv': jax.random.normal(ks[5], (M, E, H), jnp.float32) * s, 'bu': jax.random.normal(ks[6], (E, H), jnp.float32) * s, 'bv': jax.random.normal(ks[7], (E, H), jnp.float32) * s, 'wo': jax.random.normal(ks[8], (E, H, M), jnp.float32) * s, 'pos_w': sinusoidal_table(MAX_LEN, E)}
    _L1_xattn_all = _L1_xattn_setup()
    _L1_xattn_in = {k: v for k, v in _L1_xattn_all.items() if k in ('wq', 'wk', 'wv', 'bu', 'bv', 'wo', 'pos_w')}
    del _L1_xattn_all

    def _L1_ffn_setup():
        import jax, jax.numpy as jnp
        import numpy as np
        TOP_K = 2
        EPS = 1e-05

        def layer_norm(x, g, b):
            mu = jnp.mean(x, axis=-1, keepdims=True)
            var = jnp.mean(jnp.square(x - mu), axis=-1, keepdims=True)
            return (x - mu) * jax.lax.rsqrt(var + EPS) * g + b
        key = jax.random.key(seed)
        ks = jax.random.split(key, 12)
        B, S, D, F, E = (2, 256, 128, 512, 8)
        std = 0.02
        return {'x': jax.random.normal(ks[0], (B, S, D), jnp.float32), 'g1': jnp.ones((D,), jnp.float32), 'be1': jnp.zeros((D,), jnp.float32), 'mix_w': jax.random.normal(ks[1], (D, D), jnp.float32) * std, 'mix_b': jnp.zeros((D,), jnp.float32), 'g2': jnp.ones((D,), jnp.float32), 'be2': jnp.zeros((D,), jnp.float32), 'router_w': jax.random.normal(ks[2], (D, E), jnp.float32) * std, 'w1': jax.random.normal(ks[3], (E, D, F), jnp.float32) * std, 'b1': jnp.zeros((E, F), jnp.float32), 'w2': jax.random.normal(ks[4], (E, F, D), jnp.float32) * std, 'b2': jnp.zeros((E, D), jnp.float32)}
    _L1_ffn_all = _L1_ffn_setup()
    _L1_ffn_in = {k: v for k, v in _L1_ffn_all.items() if k in ('g1', 'be1', 'mix_w', 'mix_b', 'g2', 'be2', 'router_w', 'w1', 'b1', 'w2', 'b2')}
    del _L1_ffn_all

    def _L2_xattn_setup():
        import jax, jax.numpy as jnp
        import numpy as np
        D_MODEL = 128
        H = 16
        D_K = D_MODEL // H
        NEG = -1000000000.0
        key = jax.random.key(seed)
        ks = jax.random.split(key, 8)
        B, S = (4, 256)
        q = jax.random.normal(ks[0], (B, S, D_MODEL), dtype=jnp.float32)
        k = jax.random.normal(ks[1], (B, S, D_MODEL), dtype=jnp.float32)
        v = jax.random.normal(ks[2], (B, S, D_MODEL), dtype=jnp.float32)
        mask = jnp.ones((1, 1, S, S), dtype=jnp.int32)
        scale = 1.0 / np.sqrt(D_MODEL)
        w_q = jax.random.normal(ks[3], (D_MODEL, D_MODEL), dtype=jnp.float32) * scale
        w_k = jax.random.normal(ks[4], (D_MODEL, D_MODEL), dtype=jnp.float32) * scale
        w_v = jax.random.normal(ks[5], (D_MODEL, D_MODEL), dtype=jnp.float32) * scale
        w_o = jax.random.normal(ks[6], (D_MODEL, D_MODEL), dtype=jnp.float32) * scale
        return {'q': q, 'k': k, 'v': v, 'mask': mask, 'w_q': w_q, 'w_k': w_k, 'w_v': w_v, 'w_o': w_o}
    _L2_xattn_all = _L2_xattn_setup()
    _L2_xattn_in = {k: v for k, v in _L2_xattn_all.items() if k in ('w_q', 'w_k', 'w_v', 'w_o')}
    del _L2_xattn_all

    def _L2_ffn_setup():
        import jax, jax.numpy as jnp
        import numpy as np
        B, S, H, E, F = (2, 256, 128, 8, 512)
        key = jax.random.key(seed)
        k1, k2, k3, k4 = jax.random.split(key, 4)
        h = jax.random.normal(k1, (B, S, H), dtype=jnp.float32)
        Wr = jax.random.normal(k2, (H, E), dtype=jnp.float32) / np.sqrt(H)
        W1 = jax.random.normal(k3, (E, H, F), dtype=jnp.float32) / np.sqrt(H)
        W2 = jax.random.normal(k4, (E, F, H), dtype=jnp.float32) / np.sqrt(F)
        return {'h': h, 'Wr': Wr, 'W1': W1, 'W2': W2}
    _L2_ffn_all = _L2_ffn_setup()
    _L2_ffn_in = {k: v for k, v in _L2_ffn_all.items() if k in ('Wr', 'W1', 'W2')}
    del _L2_ffn_all

    def _L3_xattn_setup():
        import jax, jax.numpy as jnp
        import numpy as np
        D_MODEL = 128
        NUM_HEADS = 16
        D_K = D_MODEL // NUM_HEADS
        key = jax.random.key(seed)
        ks = jax.random.split(key, 11)
        B, S, D = (2, 256, D_MODEL)
        scale = 1.0 / np.sqrt(D)
        inp = {'q': jax.random.normal(ks[0], (B, S, D), jnp.float32), 'k': jax.random.normal(ks[1], (B, S, D), jnp.float32), 'v': jax.random.normal(ks[2], (B, S, D), jnp.float32), 'Wq': jax.random.normal(ks[3], (D, D), jnp.float32) * scale, 'bq': jax.random.normal(ks[4], (D,), jnp.float32) * scale, 'Wk': jax.random.normal(ks[5], (D, D), jnp.float32) * scale, 'bk': jax.random.normal(ks[6], (D,), jnp.float32) * scale, 'Wv': jax.random.normal(ks[7], (D, D), jnp.float32) * scale, 'bv': jax.random.normal(ks[8], (D,), jnp.float32) * scale, 'Wo': jax.random.normal(ks[9], (D, D), jnp.float32) * scale, 'bo': jax.random.normal(ks[10], (D,), jnp.float32) * scale}
        return inp
    _L3_xattn_all = _L3_xattn_setup()
    _L3_xattn_in = {k: v for k, v in _L3_xattn_all.items() if k in ('Wq', 'bq', 'Wk', 'bk', 'Wv', 'bv', 'Wo', 'bo')}
    del _L3_xattn_all

    def _L3_ffn_setup():
        import jax, jax.numpy as jnp
        import numpy as np
        B, S, H, F, E = (4, 256, 128, 512, 8)
        key = jax.random.key(seed)
        ks = jax.random.split(key, 8)
        s = 1.0 / np.sqrt(H)
        sf = 1.0 / np.sqrt(F)
        return {'x': jax.random.normal(ks[0], (B, S, H), jnp.float32), 'wr': jax.random.uniform(ks[1], (H, E), jnp.float32, -s, s), 'br': jax.random.uniform(ks[2], (E,), jnp.float32, -s, s), 'w1': jax.random.uniform(ks[3], (E, H, F), jnp.float32, -s, s), 'b1': jax.random.uniform(ks[4], (E, F), jnp.float32, -s, s), 'w2': jax.random.uniform(ks[5], (E, F, H), jnp.float32, -sf, sf), 'b2': jax.random.uniform(ks[6], (E, H), jnp.float32, -sf, sf)}
    _L3_ffn_all = _L3_ffn_setup()
    _L3_ffn_in = {k: v for k, v in _L3_ffn_all.items() if k in ('wr', 'br', 'w1', 'b1', 'w2', 'b2')}
    del _L3_ffn_all
    return {'x': x, 'ctx_1024': ctx_1024, '_lenS2': _lenS2, 'mask_BxS2_bf1': mask_BxS2_bf1, 'mask_1x1xSxS2_if1': mask_1x1xSxS2_if1, 'L0_xattn_W_q': _L0_xattn_in['W_q'], 'L0_xattn_W_k': _L0_xattn_in['W_k'], 'L0_xattn_W_v': _L0_xattn_in['W_v'], 'L0_xattn_W_o': _L0_xattn_in['W_o'], 'L0_ffn_shared_w1': _L0_ffn_in['shared_w1'], 'L0_ffn_shared_b1': _L0_ffn_in['shared_b1'], 'L0_ffn_shared_w2': _L0_ffn_in['shared_w2'], 'L0_ffn_shared_b2': _L0_ffn_in['shared_b2'], 'L0_ffn_router_w': _L0_ffn_in['router_w'], 'L0_ffn_router_b': _L0_ffn_in['router_b'], 'L0_ffn_spec_w1': _L0_ffn_in['spec_w1'], 'L0_ffn_spec_b1': _L0_ffn_in['spec_b1'], 'L0_ffn_spec_w2': _L0_ffn_in['spec_w2'], 'L0_ffn_spec_b2': _L0_ffn_in['spec_b2'], 'L1_xattn_wq': _L1_xattn_in['wq'], 'L1_xattn_wk': _L1_xattn_in['wk'], 'L1_xattn_wv': _L1_xattn_in['wv'], 'L1_xattn_bu': _L1_xattn_in['bu'], 'L1_xattn_bv': _L1_xattn_in['bv'], 'L1_xattn_wo': _L1_xattn_in['wo'], 'L1_xattn_pos_w': _L1_xattn_in['pos_w'], 'L1_ffn_g1': _L1_ffn_in['g1'], 'L1_ffn_be1': _L1_ffn_in['be1'], 'L1_ffn_mix_w': _L1_ffn_in['mix_w'], 'L1_ffn_mix_b': _L1_ffn_in['mix_b'], 'L1_ffn_g2': _L1_ffn_in['g2'], 'L1_ffn_be2': _L1_ffn_in['be2'], 'L1_ffn_router_w': _L1_ffn_in['router_w'], 'L1_ffn_w1': _L1_ffn_in['w1'], 'L1_ffn_b1': _L1_ffn_in['b1'], 'L1_ffn_w2': _L1_ffn_in['w2'], 'L1_ffn_b2': _L1_ffn_in['b2'], 'L2_xattn_w_q': _L2_xattn_in['w_q'], 'L2_xattn_w_k': _L2_xattn_in['w_k'], 'L2_xattn_w_v': _L2_xattn_in['w_v'], 'L2_xattn_w_o': _L2_xattn_in['w_o'], 'L2_ffn_Wr': _L2_ffn_in['Wr'], 'L2_ffn_W1': _L2_ffn_in['W1'], 'L2_ffn_W2': _L2_ffn_in['W2'], 'L3_xattn_Wq': _L3_xattn_in['Wq'], 'L3_xattn_bq': _L3_xattn_in['bq'], 'L3_xattn_Wk': _L3_xattn_in['Wk'], 'L3_xattn_bk': _L3_xattn_in['bk'], 'L3_xattn_Wv': _L3_xattn_in['Wv'], 'L3_xattn_bv': _L3_xattn_in['bv'], 'L3_xattn_Wo': _L3_xattn_in['Wo'], 'L3_xattn_bo': _L3_xattn_in['bo'], 'L3_ffn_wr': _L3_ffn_in['wr'], 'L3_ffn_br': _L3_ffn_in['br'], 'L3_ffn_w1': _L3_ffn_in['w1'], 'L3_ffn_b1': _L3_ffn_in['b1'], 'L3_ffn_w2': _L3_ffn_in['w2'], 'L3_ffn_b2': _L3_ffn_in['b2']}

def reference(x, ctx_1024, _lenS2, mask_BxS2_bf1, mask_1x1xSxS2_if1, L0_xattn_W_q, L0_xattn_W_k, L0_xattn_W_v, L0_xattn_W_o, L0_ffn_shared_w1, L0_ffn_shared_b1, L0_ffn_shared_w2, L0_ffn_shared_b2, L0_ffn_router_w, L0_ffn_router_b, L0_ffn_spec_w1, L0_ffn_spec_b1, L0_ffn_spec_w2, L0_ffn_spec_b2, L1_xattn_wq, L1_xattn_wk, L1_xattn_wv, L1_xattn_bu, L1_xattn_bv, L1_xattn_wo, L1_xattn_pos_w, L1_ffn_g1, L1_ffn_be1, L1_ffn_mix_w, L1_ffn_mix_b, L1_ffn_g2, L1_ffn_be2, L1_ffn_router_w, L1_ffn_w1, L1_ffn_b1, L1_ffn_w2, L1_ffn_b2, L2_xattn_w_q, L2_xattn_w_k, L2_xattn_w_v, L2_xattn_w_o, L2_ffn_Wr, L2_ffn_W1, L2_ffn_W2, L3_xattn_Wq, L3_xattn_bq, L3_xattn_Wk, L3_xattn_bk, L3_xattn_Wv, L3_xattn_bv, L3_xattn_Wo, L3_xattn_bo, L3_ffn_wr, L3_ffn_br, L3_ffn_w1, L3_ffn_b1, L3_ffn_w2, L3_ffn_b2):
    import jax
    import jax.numpy as jnp

    def _L0_xattn_ref(queries, keys, sequence_length, W_q, W_k, W_v, W_o):
        import jax, jax.numpy as jnp
        import numpy as np
        B, L, D, H = (4, 256, 128, 8)
        DH = D // H
        NEG = float(-2 ** 32 + 1)
        b, lq, d = queries.shape
        lk = keys.shape[1]
        Q = (queries @ W_q.T).reshape(b, lq, H, DH).transpose(2, 0, 1, 3)
        K = (keys @ W_k.T).reshape(b, lk, H, DH).transpose(2, 0, 1, 3)
        V = (keys @ W_v.T).reshape(b, lk, H, DH).transpose(2, 0, 1, 3)
        scores = jnp.einsum('hbqd,hbkd->hbqk', Q, K) / jnp.sqrt(jnp.float32(DH))
        key_mask = jnp.arange(lk)[None, :] < sequence_length[:, None]
        scores = jnp.where(key_mask[None, :, None, :], scores, NEG)
        attn = jax.nn.softmax(scores, axis=-1)
        q_mask = (jnp.arange(lq)[None, :] < sequence_length[:, None]).astype(attn.dtype)
        attn = attn * q_mask[None, :, :, None]
        out = jnp.einsum('hbqk,hbkd->hbqd', attn, V)
        out = out.transpose(1, 2, 0, 3).reshape(b, lq, d)
        return out @ W_o.T

    def _L0_ffn_ref(x, shared_w1, shared_b1, shared_w2, shared_b2, router_w, router_b, spec_w1, spec_b1, spec_w2, spec_b2):
        import jax, jax.numpy as jnp
        import numpy as np
        D_MODEL = 128
        D_FF = 512
        N_EXPERTS = 8
        TOP_K = 2

        def _ffn(x, w1, b1, w2, b2):
            h = jax.nn.gelu(x @ w1.T + b1)
            return h @ w2.T + b2
        B, T, D = x.shape
        xf = x.reshape(-1, D)
        U = xf.shape[0]
        logits = xf @ router_w.T + router_b
        routing = jax.nn.softmax(logits, axis=-1)
        sel_w, sel_idx = jax.lax.top_k(routing, TOP_K)
        sel_w = sel_w / sel_w.sum(axis=-1, keepdims=True)
        comb = jnp.zeros_like(routing).at[jnp.arange(U)[:, None], sel_idx].set(sel_w)
        shared_out = _ffn(xf, shared_w1, shared_b1, shared_w2, shared_b2)

        def body(acc, params):
            w1, b1, w2, b2, we = params
            return (acc + we[:, None] * _ffn(xf, w1, b1, w2, b2), None)
        acc0 = jnp.zeros_like(shared_out)
        acc, _ = jax.lax.scan(body, acc0, (spec_w1, spec_b1, spec_w2, spec_b2, comb.T))
        return (shared_out + acc).reshape(B, T, D)

    def _L1_xattn_ref(q, k, v, mask, wq, wk, wv, bu, bv, wo, pos_w):
        import jax, jax.numpy as jnp
        import numpy as np
        B, T, M, E, H = (8, 64, 128, 128, 8)
        MAX_LEN = 128

        def sinusoidal_table(max_len, n_model):
            pos = jnp.concatenate([jnp.arange(-(max_len // 2), 0, dtype=jnp.float32), jnp.arange(0, max_len // 2, dtype=jnp.float32)])
            inv = 10000.0 ** ((jnp.arange(n_model) // 2 * 2).astype(jnp.float32) / n_model)
            w = pos[:, None] / inv[None, :]
            even = jnp.sin(w[:, 0::2])
            odd = jnp.cos(w[:, 1::2])
            out = jnp.zeros((max_len, n_model), jnp.float32)
            out = out.at[:, 0::2].set(even)
            out = out.at[:, 1::2].set(odd)
            return out
        scale = jnp.float32(E) ** 0.5
        qh = jnp.einsum('btm,meh->bteh', q, wq)
        kh = jnp.einsum('btm,meh->bteh', k, wk)
        vh = jnp.einsum('btm,meh->bteh', v, wv)
        t = q.shape[1]
        offset = MAX_LEN // 2 + MAX_LEN % 2
        pos = jnp.arange(t)
        idx = pos[None, :] - pos[:, None] + offset
        p = pos_w[idx]
        attn = jnp.einsum('bqeh,bkeh->bqkh', qh + bu, kh) + jnp.einsum('bqeh,qke->bqkh', qh + bv, p)
        attn = attn / scale
        attn = jnp.where(mask[:, None, :, None], attn, -jnp.inf)
        attn = jax.nn.softmax(attn, axis=-2)
        x = jnp.einsum('bqkh,bkeh->bqeh', attn, vh)
        return jnp.einsum('bqeh,ehm->bqm', x, wo)

    def _L1_ffn_ref(x, g1, be1, mix_w, mix_b, g2, be2, router_w, w1, b1, w2, b2):
        import jax, jax.numpy as jnp
        import numpy as np
        TOP_K = 2
        EPS = 1e-05

        def layer_norm(x, g, b):
            mu = jnp.mean(x, axis=-1, keepdims=True)
            var = jnp.mean(jnp.square(x - mu), axis=-1, keepdims=True)
            return (x - mu) * jax.lax.rsqrt(var + EPS) * g + b
        res = x
        n = layer_norm(x, g1, be1)
        x = res + n + (n @ mix_w + mix_b)
        res = x
        n = layer_norm(x, g2, be2)
        B, S, D = n.shape
        E = w1.shape[0]
        flat = n.reshape(-1, D)
        probs = jax.nn.softmax(flat @ router_w, axis=-1)
        topw, topi = jax.lax.top_k(probs, TOP_K)
        combine = jnp.sum(jax.nn.one_hot(topi, E, dtype=flat.dtype) * topw[..., None], axis=1)
        h = jax.nn.silu(jnp.einsum('td,edf->tef', flat, w1) + b1)
        y = jnp.einsum('tef,efd->ted', h, w2) + b2
        out = jnp.einsum('te,ted->td', combine, y)
        return res + out.reshape(B, S, D)

    def _L2_xattn_ref(q, k, v, mask, w_q, w_k, w_v, w_o):
        import jax, jax.numpy as jnp
        import numpy as np
        D_MODEL = 128
        H = 16
        D_K = D_MODEL // H
        NEG = -1000000000.0
        B, S, _ = q.shape
        query = (q @ w_q.T).reshape(B, S, H, D_K).transpose(0, 2, 1, 3)
        key_ = (k @ w_k.T).reshape(B, S, H, D_K).transpose(0, 2, 1, 3)
        value = (v @ w_v.T).reshape(B, S, H, D_K).transpose(0, 2, 1, 3)
        scores = jnp.einsum('bhqd,bhkd->bhqk', query, key_) / jnp.sqrt(jnp.asarray(D_K, dtype=query.dtype))
        scores = jnp.where(mask == 0, jnp.asarray(NEG, dtype=scores.dtype), scores)
        attn = jax.nn.softmax(scores, axis=-1)
        out = jnp.einsum('bhqk,bhkd->bhqd', attn, value)
        out = out.transpose(0, 2, 1, 3).reshape(B, S, H * D_K)
        return out @ w_o.T

    def _L2_ffn_ref(h, Wr, W1, W2):
        import jax, jax.numpy as jnp
        import numpy as np
        B, S, H, E, F = (2, 256, 128, 8, 512)
        g = jax.nn.softmax(h @ Wr, axis=-1)
        top2_w, top2_idx = jax.lax.top_k(g, 2)
        top2_w = top2_w / jnp.sum(top2_w, axis=-1, keepdims=True)
        hid = jax.nn.relu(jnp.einsum('bsh,ehf->bsef', h, W1))
        expert_out = jnp.einsum('bsef,efh->bseh', hid, W2)
        top2_out = jnp.take_along_axis(expert_out, top2_idx[..., None], axis=2)
        return jnp.sum(top2_out * top2_w[..., None], axis=2)

    def _L3_xattn_ref(q, k, v, Wq, bq, Wk, bk, Wv, bv, Wo, bo):
        import jax, jax.numpy as jnp
        import numpy as np
        D_MODEL = 128
        NUM_HEADS = 16
        D_K = D_MODEL // NUM_HEADS
        B, S, D = q.shape
        H, dk = (NUM_HEADS, D_K)

        def proj(x, W, b):
            y = jnp.einsum('bsd,ed->bse', x, W) + b
            return y.reshape(B, S, H, dk).transpose(0, 2, 1, 3)
        Q = proj(q, Wq, bq)
        K = proj(k, Wk, bk)
        V = proj(v, Wv, bv)
        scores = jnp.einsum('bhqd,bhkd->bhqk', Q, K)
        attn = jax.nn.softmax(scores, axis=-1)
        out = jnp.einsum('bhqk,bhkd->bhqd', attn, V)
        out = out.transpose(0, 2, 1, 3).reshape(B, S, D)
        return jnp.einsum('bsd,ed->bse', out, Wo) + bo

    def _L3_ffn_ref(x, wr, br, w1, b1, w2, b2):
        import jax, jax.numpy as jnp
        import numpy as np
        B, S, H, F, E = (4, 256, 128, 512, 8)
        scores = jnp.einsum('bsh,he->bse', x, wr) + br
        expert_id = jnp.argmax(scores, axis=-1)
        h = jnp.einsum('bsh,ehf->ebsf', x, w1) + b1[:, None, None, :]
        h = jax.nn.gelu(h, approximate=False)
        y = jnp.einsum('ebsf,efh->ebsh', h, w2) + b2[:, None, None, :]
        one_hot = jax.nn.one_hot(expert_id, E, dtype=x.dtype)
        out = jnp.einsum('ebsh,bse->bsh', y, one_hot)
        return out
    x = x + _L0_xattn_ref(_layernorm(x, axis=-1), ctx_1024, _lenS2, L0_xattn_W_q, L0_xattn_W_k, L0_xattn_W_v, L0_xattn_W_o)
    x = x + _L0_ffn_ref(_layernorm(x, axis=-1), L0_ffn_shared_w1, L0_ffn_shared_b1, L0_ffn_shared_w2, L0_ffn_shared_b2, L0_ffn_router_w, L0_ffn_router_b, L0_ffn_spec_w1, L0_ffn_spec_b1, L0_ffn_spec_w2, L0_ffn_spec_b2)
    x = x + _L1_xattn_ref(_layernorm(x, axis=-1), ctx_1024, ctx_1024, mask_BxS2_bf1, L1_xattn_wq, L1_xattn_wk, L1_xattn_wv, L1_xattn_bu, L1_xattn_bv, L1_xattn_wo, L1_xattn_pos_w)
    x = x + _L1_ffn_ref(_layernorm(x, axis=-1), L1_ffn_g1, L1_ffn_be1, L1_ffn_mix_w, L1_ffn_mix_b, L1_ffn_g2, L1_ffn_be2, L1_ffn_router_w, L1_ffn_w1, L1_ffn_b1, L1_ffn_w2, L1_ffn_b2)
    x = x + _L2_xattn_ref(_layernorm(x, axis=-1), ctx_1024, ctx_1024, mask_1x1xSxS2_if1, L2_xattn_w_q, L2_xattn_w_k, L2_xattn_w_v, L2_xattn_w_o)
    x = x + _L2_ffn_ref(_layernorm(x, axis=-1), L2_ffn_Wr, L2_ffn_W1, L2_ffn_W2)
    x = x + _L3_xattn_ref(_layernorm(x, axis=-1), ctx_1024, ctx_1024, L3_xattn_Wq, L3_xattn_bq, L3_xattn_Wk, L3_xattn_bk, L3_xattn_Wv, L3_xattn_bv, L3_xattn_Wo, L3_xattn_bo)
    x = x + _L3_ffn_ref(_layernorm(x, axis=-1), L3_ffn_wr, L3_ffn_br, L3_ffn_w1, L3_ffn_b1, L3_ffn_w2, L3_ffn_b2)
    return x

_drawn_inputs = setup_inputs


def setup_inputs(seed=0):
    import zlib

    import numpy as np

    out = dict(_drawn_inputs(seed))
    spreads = {'L0_ffn_shared_b1': (0.0, 0.269),
     'L0_ffn_shared_b2': (0.0, 0.1),
     'L0_ffn_router_b': (0.0, 0.1),
     'L0_ffn_spec_b1': (0.0, 0.294),
     'L0_ffn_spec_b2': (0.0, 0.1),
     'L1_ffn_g1': (1.0, 0.2),
     'L1_ffn_be1': (0.0, 0.1),
     'L1_ffn_mix_b': (0.0, 0.1),
     'L1_ffn_g2': (1.0, 0.6),
     'L1_ffn_be2': (0.0, 0.8),
     'L1_ffn_b1': (0.0, 0.8),
     'L1_ffn_b2': (0.0, 0.473)}
    factors = {'L0_xattn_W_q': 8.0,
     'L0_xattn_W_k': 8.0,
     'L1_xattn_wq': 8.0,
     'L1_xattn_wk': 8.0,
     'L1_xattn_bu': 8.0,
     'L1_xattn_bv': 8.0,
     'L1_xattn_pos_w': 8.0,
     'L1_ffn_router_w': 4.276,
     'L1_ffn_w1': 7.545,
     'L1_ffn_w2': 7.45,
     'L3_xattn_bk': 64.0,
     'L3_ffn_br': 3.154,
     'L3_ffn_b1': 8.0,
     'L3_ffn_b2': 6.988,
     'L3_xattn_bq': 3.198}
    for name, (base, spread) in spreads.items():
        noise = np.random.default_rng([zlib.crc32(name.encode()), seed]).standard_normal(out[name].shape)
        drawn = base * np.exp(spread * noise) if base else spread * noise
        out[name] = jnp.asarray(drawn.astype(out[name].dtype))
    for name, factor in factors.items():
        out[name] = (out[name] * factor).astype(out[name].dtype)
    return out
```

```python
import concourse.bass as bass
from concourse import mybir
from contextlib import ExitStack

B, S, D = 4, 256, 128
TOK = B * S
NT = TOK // 128
F, E = 512, 8
FC = F // 128
H1 = 8
BH1 = B * H1
POS = 128
WIN = 2 * S - 1
LN_EPS = 1e-5
BIG_NEG = -float(2 ** 30)
L0_NEG = -float(2 ** 32)
L1_NEG = -3.0e38

NARROW = {"a0": (8, 16, 0.25), "a2": (16, 8, float(8 ** -0.5)), "a3": (16, 8, 1.0)}
LAYER_OF = {"a0": 0, "a2": 1, "a3": 2}
PAIRS = ((0, 0), (0, 1), (1, 0), (1, 1), (0, 2), (2, 0))
MASK_ROW = 96
ROWS = {"a0": 128, "a2": 96, "a3": 96}
FFN = {"f0": (9, 2), "f1": (8, 2), "f2": (8, 2), "f3": (8, 1)}


def build(nc, A, out):
    fp32, bf16, i32, u8 = mybir.dt.float32, mybir.dt.bfloat16, mybir.dt.int32, mybir.dt.uint8
    ALU, ACT, AX = mybir.AluOpType, mybir.ActivationFunctionType, mybir.AxisListType
    ctx = ExitStack()
    with ctx:
        def sb(name, shape, dt=fp32):
            return ctx.enter_context(nc.sbuf_tensor(name, shape, dt))

        made = {}

        def sem(name):
            if name not in made:
                made[name] = ctx.enter_context(nc.semaphore(name.replace(".", "_")))
            return made[name]

        narrow = {k: B * h for k, (h, _, _) in NARROW.items()}
        COUNTS = {n: [("a0", c("a0")), ("a2", c("a2")), ("a3", c("a3"))] for n, c in {
            **dict.fromkeys(("k", "kt", "v", "va", "q", "qt", "qp"), lambda k: 2), "kp": lambda k: 1,
            **dict.fromkeys(("S", "nm", "e", "T", "pte", "pv"), lambda k: narrow[k]),
            **dict.fromkeys(("oe", "ot", "att"), lambda k: narrow[k] // 4),
            **dict.fromkeys(("attT", "ate", "out"), lambda k: B)}.items()}
        COUNTS |= {n: [(k, c(k)) for k in ("f0", "f1", "f2", "f3")] for n, c in {
            **dict.fromkeys(("lg", "comb"), lambda k: 1), **dict.fromkeys(("d", "ex"), lambda k: int(FFN[k][1] == 2)),
            **dict.fromkeys(("up", "h"), lambda k: 2 * FC * FFN[k][0]), **dict.fromkeys(("down", "acc"), lambda k: 2 * FFN[k][0]),
            **dict.fromkeys(("cT", "cTe", "b2", "b2a"), lambda k: 0 if k == "f2" else 2)}.items()}
        norms = ("a0", "f0", "a1", "f1", "f1b", "f1c", "a2", "f2", "a3", "f3")
        COUNTS |= {"mv": [(k, 1) for k in norms], "rstd": [(k, 1) for k in norms], "xn": [(k, NT) for k in norms]}
        COUNTS |= {n: [(k, 2) for k in ("ctx", "a0", "f0", "a1", "f1", "f1n", "a2", "f2", "a3", "f3")] for n in ("tr", "nT")}
        COUNTS["x"] = [("a0", B), ("a1", NT), ("a2", B), ("a3", B)]

        def at(key, name, v):
            base = 0
            for k, total in COUNTS[name]:
                if k == key:
                    assert 0 < v <= total, (key, name, v)
                    return sem(name), base + v
                base += total
            raise KeyError(key)

        x = sb("x_res", [128, NT, D])
        xn = sb("xn", [128, NT, D])
        xm = sb("xm", [128, NT, D])
        nT = [sb("nT0", [128, TOK]), sb("nT1", [128, TOK])]
        cx = sb("cx", [128, NT, D])
        cT = sb("cT", [128, TOK])
        W = sb("W", [128, 9, 2 * F])
        aw = sb("aw", [128, 12, D])
        big = sb("big", [128, 18432])
        late = sb("late", [128, 8192])
        P = [sb("P0", [128, 2, S]), sb("P1", [128, 2, S])]
        PTs = [sb("PTs0", [128, 2, S]), sb("PTs1", [128, 2, S])]
        ident = sb("ident", [128, 128])
        identb = sb("identb", [128, 128], bf16)
        lowert = sb("lowert", [128, E, E])
        half = sb("half", [128, NT])
        stats = sb("stats", [128, NT, 6])
        mv = sb("mv", [128, NT, 2])
        rstd = sb("rstd", [128, NT])
        negmax = sb("negmax", [128, 4, 2])
        QT = sb("QT", [128, TOK])
        KT = sb("KT", [128, TOK])
        Os = [sb("Os0", [128, S]), sb("Os1", [128, S])]
        att = [sb("att0", [128, 2, D]), sb("att1", [128, 2, D])]
        attT = [sb("attT0", [128, S]), sb("attT1", [128, S])]
        rc = sb("rc", [128, 2, 4])
        madd2 = sb("madd2", [128, 2, S], bf16)
        leni = sb("leni", [128, B], i32)
        lenf = sb("lenf", [128, B])
        qpos = sb("qpos", [128, NT])
        qmask = sb("qmask", [128, NT])
        m1u = sb("m1u", [128, 2 * B], u8)
        m1f = sb("m1f", [128, 2 * B])
        m1bh = sb("m1bh", [128, 2, BH1])
        qkb = sb("qkb", [128, 2])
        rows = sb("rows", [128, 7, D])
        rb = sb("rb", [128, 2, E])
        rw = sb("rw", [128, 4, E])
        b1 = sb("b1", [128, 3, 9 * FC])
        b2 = sb("b2", [9, 3, D])
        mixw = sb("mixw", [128, D])
        lg = sb("lg", [128, NT, E])
        sel = sb("sel", [128, NT, E])
        ex = sb("ex", [128, NT, E])
        tmax = sb("tmax", [128, NT])
        tsum = sb("tsum", [128, NT])
        comb = sb("comb", [128, NT, 9])
        bub = sb("bub", [128, 2, H1])
        bst = sb("bst", [128, 2, H1])
        r1 = sb("r1", [128, 4])
        r2 = sb("r2", [128, 4])

        keyrow = big[:, 17920:18176]
        combT = KT[0:9, :]
        m2i = xm[:, 0:4, :].rearrange("p t d -> p (t d)").bitcast(i32).rearrange("p (t k) -> p t k", t=2)
        cmp_a, cmp_b = (QT[:, 512 * i:512 * (i + 1)].rearrange("p (t e f) -> p t e f", t=NT, e=E) for i in range(2))
        Qs, Ks = (big[:, 8192 * i:8192 * (i + 1)].bitcast(bf16).rearrange("p (h t) -> p h t", h=16) for i in range(2))
        parts = big[:, 16384:17920].bitcast(bf16).rearrange("p (c t) -> p c t", c=3)
        T1 = big[:, 0:4096].rearrange("p (q n) -> p q n", n=BH1)
        Q1 = [big[:, 4096 + 2048 * i:6144 + 2048 * i].bitcast(bf16).rearrange("p (q n) -> p q n", n=BH1)
              for i in range(3)]
        ST = big[:, 10240:18432].rearrange("p (c n q) -> p c n q", c=2, n=BH1)
        Va = late[:, 0:4096].rearrange("p (t h w) -> p t h w", t=NT, w=32)
        hid = [late[:, 4096 + 2048 * i:6144 + 2048 * i].rearrange("p (c t) -> p c t", c=FC) for i in range(2)]
        wide = late[:, :].rearrange("p (w h m) -> p w h m", w=8, h=H1)
        WQT, WKT, WVT, WO, WQ, AQK, CVO = (wide[:, i] for i in range(7))
        QF = late[:, 7168:8192].rearrange("p (s t) -> p s t", s=2)
        PWf = QT
        PW = [KT[:, 256 * i:256 * (i + 1)].bitcast(bf16) for i in range(3)]
        QR = [Os[i][:, :] for i in range(2)]
        GT = [att[i][:, 0, :] for i in range(2)]

        scratch = nc.dram_tensor("parts_scratch", [2, 128, 3, TOK], bf16, kind="Internal").ap()

        bank = [ctx.enter_context(nc.psum_tensor(f"bank{i}", [128, 512], fp32)) for i in range(8)]
        M = [6, 7]

        block = ctx.enter_context(nc.Block())

        SMALL = 16 * 16
        nexp = lambda key: FFN[key][0]
        ORDER = ["a0", "f0", "a1", "f1", "a2", "f2", "a3", "f3"]
        NEXT = {"f1": "a2", "f2": "a3"}
        SLOTLOAD = {"f0": 1, "f1": 2, "f2": 3, "f3": 4}

        def x_ready(eng, key):
            n = len(ORDER) if key == "out" else ORDER.index(key)
            if n == 0:
                eng.wait_ge(sem("ld.x"), 16)
            elif ORDER[n - 1] in FFN:
                eng.wait_ge(*at(ORDER[n - 1], "acc", 2 * FFN[ORDER[n - 1]][0]))
            else:
                eng.wait_ge(*at(ORDER[n - 1], "x", dict(COUNTS["x"])[ORDER[n - 1]]))

        loads = {"ld.ctx": 16, "ld.x": 16, "ld.aw": 16, "ld.small": 16 * 18}

        @block.sync
        def _(sp):
            sp.dma_start(cx[:, :, :], A["ctx"].rearrange("(t p) d -> p t d", p=128)).then_inc(sem("ld.ctx"), 16)
            sp.dma_start(x[:, :, :], A["x"].rearrange("(t p) d -> p t d", p=128)).then_inc(sem("ld.x"), 16)
            sp.dma_start(aw[:, :, :], A["aw"].rearrange("w i o -> i w o")).then_inc(sem("ld.aw"), 16)

            def expert(key, e):
                prev = {"f1": "f0", "f2": "f1", "f3": "f2"}.get(key)
                if prev and e < FFN[prev][0]:
                    sp.wait_ge(*at(prev, "down", FFN[prev][0] + e + 1))
                sp.dma_start(W[:, e, 0:F], A[f"{key}.w1"][e]).then_inc(sem(f"w.slot{e}"), 16)
                sp.dma_start(W[:, e, F:2 * F].rearrange("p (c d) -> p c d", c=FC),
                             A[f"{key}.w2"][e].rearrange("(c p) d -> p c d", p=128)).then_inc(sem(f"w.slot{e}"), 16)

            small = [(m2i[:, :, :], A["mask2"].rearrange("(t p) k -> p t k", p=128)),
                     (m1u[:, :], A["mask1"]),
                     (leni[:, :], bass.AP(A["lens"].tensor, 0, [[0, 128], [1, B]])),
                     (qkb[:, :], A["qkb"]),
                     (rows[:, :, :], bass.AP(A["rows"].tensor, 0, [[0, 128], [D, 7], [1, D]])),
                     (rb[:, :, :], bass.AP(A["rb"].tensor, 0, [[0, 128], [E, 2], [1, E]])),
                     (rw[:, :, :], A["rw"].rearrange("l d e -> d l e")),
                     (b1[:, 0, :], A["f0.b1"]),
                     (b1[:, 1, 0:8 * FC], A["f1.b1"]),
                     (b1[:, 2, 0:8 * FC], A["f3.b1"]),
                     (b2[:, 0, :], A["f0.b2"]), (b2[0:8, 1, :], A["f1.b2"]), (b2[0:8, 2, :], A["f3.b2"]),
                     (mixw[:, :], A["mixw"]),
                     (bub[:, 0, :], A["bu"]), (bub[:, 1, :], A["bv"])]
            for dst, src in small:
                sp.dma_start(dst, src).then_inc(sem("ld.small"), 16)
            loads["ld.small"] = 16 * len(small)
            def stack(key, side, half=None):
                H, d, _ = NARROW[key]
                n = LAYER_OF[key]
                cols = slice(0, TOK) if half is None else slice(512 * half, 512 * (half + 1))
                dst = (Qs, Ks)[side]
                if side:
                    sp.wait_ge(*at(key, "kp", 1))
                    if key == "a3":
                        sp.wait_ge(*at("a2", "S", narrow["a2"]))
                    elif key == "a2":
                        sp.wait_ge(sem("c.zero"), 2)
                else:
                    sp.wait_ge(*at(key, "qp", half + 1))
                done = 16 * (3 * n + (1 if side else 2 + half))
                sp.dma_start(scratch[side, :, :, cols], parts[:, :, cols]).then_inc(sem("st.w"), 16)
                sp.wait_ge(sem("st.w"), done)
                src = scratch[side].rearrange("(h i) c t -> i h c t", i=d)
                for r, pair in enumerate(PAIRS):
                    sp.dma_start(dst[r * d:(r + 1) * d, 0:H, cols], src[:, :, pair[side], cols])\
                      .then_inc(sem("st.k" if side else f"st.q{half}"), 16)

            stack("a0", 1)
            stack("a0", 0, 0)
            stack("a0", 0, 1)
            for e in range(9):
                expert("f0", e)
            sp.wait_ge(*at("f0", "down", 2 * FFN["f0"][0]))
            for i, n in enumerate(("wqT", "wkT", "wvT", "wo", "wq")):
                sp.dma_start(wide[:, i], A[f"a1.{n}"]).then_inc(sem("ld.wide"), 16)
            sp.dma_start(PWf[:, 0:WIN], A["a1.pos"]).then_inc(sem("ld.pos"), 16)
            for e in range(8):
                expert("f1", e)
            for key, nxt in (("a2", "f2"), ("a3", "f3")):
                stack(key, 1)
                for e in range(8):
                    expert(nxt, e)
                stack(key, 0, 0)
                stack(key, 0, 1)
            x_ready(sp, "out")
            sp.dma_start(out.rearrange("(t p) d -> p t d", p=128), x[:, :, :]).then_inc(sem("stored"), 16)
            sp.wait_ge(sem("stored"), 16)

        @block.gpsimd
        def _(pool):
            chain = [0]

            def link(ins):
                chain[0] += 1
                ins.then_inc(sem("pool.chain"), 1)
                pool.wait_ge(sem("pool.chain"), chain[0])

            link(pool.memset(ident[:, :], 0.0))
            link(pool.affine_select(out=ident[:, :], in_=ident[:, :], compare_op=ALU.not_equal, fill=1.0, base=0,
                                    pattern=[[-1, 128]], channel_multiplier=1))
            pool.tensor_copy(identb[:, :], ident[:, :]).then_inc(sem("c.ident"), 1)
            pool.wait_ge(sem("c.ident"), 1)
            link(pool.memset(half[:, :], -0.5))
            link(pool.memset(Qs[96:128, 0:8, :], 0.0))
            pool.memset(Ks[96:128, 0:8, :], 0.0).then_inc(sem("c.zero"), 1)
            pool.wait_ge(sem("c.zero"), 1)
            link(pool.iota(keyrow[:, :], pattern=[[1, S]], base=0, channel_multiplier=0, allow_small_or_imprecise_dtypes=True))
            link(pool.iota(qpos[:, :].rearrange("p (b t) -> p b t", t=2), pattern=[[0, B], [128, 2]], base=0,
                           channel_multiplier=1, allow_small_or_imprecise_dtypes=True))
            link(pool.memset(lowert[:, :, :], 1.0))
            pool.affine_select(out=lowert[:, :, :], in_=lowert[:, :, :], compare_op=ALU.is_gt, fill=0.0, base=0,
                               pattern=[[1, E], [-1, E]], channel_multiplier=0).then_inc(sem("c.rest"), 1)
            pool.wait_ge(sem("c.rest"), 1)
            link(pool.memset(comb[:, :, :], 1.0))
            pool.memset(Va[:, :, :, :], 0.0).then_inc(sem("c.Va"), 1)

            def layer_norm_rstd(key):
                pool.wait_ge(*at(key, "mv", 1))
                link(pool.tensor_scalar(rstd[:, :], mv[:, :, 1], LN_EPS, None, ALU.add))
                pool.tensor_tensor(rstd[:, :], rstd[:, :], half[:, :], ALU.pow).then_inc(sem("rstd"), 1)

            layer_norm_rstd("a0")
            layer_norm_rstd("f0")
            layer_norm_rstd("a1")
            for n in ("f1", "f1b", "f1c"):
                layer_norm_rstd(n)
            pool.wait_ge(sem("a1.o"), 2 * BH1)
            link(pool.memset(Va[:, :, :, :], 0.0))
            pool.memset(big[:, 0:16384], 0.0).then_inc(sem("c.zero"), 1)
            for key in ("a2", "f2", "a3", "f3"):
                layer_norm_rstd(key)

        @block.vector
        def _(dve):
            chain = [0]
            v = nc.vector

            def link(ins):
                chain[0] += 1
                ins.then_inc(sem("dve.chain"), 1)
                dve.wait_ge(sem("dve.chain"), chain[0])

            def layer_norm(key, src, dst):
                n = norms.index(key)
                if n:
                    dve.wait_ge(*at(norms[n - 1], "xn", NT))
                for t in range(NT):
                    ins = v.bn_stats(stats[:, t, :], src[:, t, :])
                link(ins)
                for t in range(NT):
                    ins = v.bn_aggr(mv[:, t, :], stats[:, t, :])
                ins.then_inc(sem("mv"), 1)
                dve.wait_ge(*at(key, "rstd", 1))
                for t in range(NT):
                    v.tensor_scalar(dst[:, t, :], src[:, t, :], mv[:, t, 0:1], rstd[:, t:t + 1],
                                    ALU.subtract, ALU.mult).then_inc(sem("xn"), 1)

            def row(i, n=NT):
                return rows[:, i:i + 1, :].broadcast_to([128, n, D])

            dve.wait_ge(sem("ld.small"), SMALL)
            dve.wait_ge(sem("c.rest"), 1)
            v.tensor_scalar(madd2[:, :, :], m2i[:, :, :], 0.0, BIG_NEG, ALU.is_equal, ALU.mult)
            link(v.tensor_copy(lenf[:, :], leni[:, :]))
            dve.wait_ge(sem("c.zero"), 1)
            v.memset(Qs[MASK_ROW:MASK_ROW + 1, 0:8, :], 1.0)
            for b in range(B):
                r = MASK_ROW
                v.tensor_scalar(Ks[r:r + 1, 0:8, S * b:S * (b + 1)], keyrow[r:r + 1, :].unsqueeze(1).broadcast_to([1, 8, S]),
                                lenf[r:r + 1, b:b + 1], L0_NEG, ALU.is_ge, ALU.mult)
                v.tensor_scalar(qmask[:, 2 * b:2 * b + 2], qpos[:, 2 * b:2 * b + 2], lenf[:, b:b + 1], None, ALU.is_lt)
            link(v.tensor_copy(m1f[:, :], m1u[:, :]))
            link(v.tensor_scalar(m1f[:, :], m1f[:, :], 1.0, -L1_NEG, ALU.subtract, ALU.mult))
            for c in range(2):
                ins = v.tensor_copy(m1bh[:, c, :].rearrange("p (b h) -> p b h", h=H1),
                                    m1f[:, :].rearrange("p (b c) -> p b c", c=2)[:, :, c:c + 1].broadcast_to([128, B, H1]))
            link(v.tensor_scalar(bst[:, 1, :], bub[:, 1, :], float(D) ** -0.5, None, ALU.mult))
            ins = v.memset(r1[:, :], 0.0)
            ins.then_inc(sem("c.masks"), 1)

            def split(src, cols, done):
                f, (p0, p1, p2) = src[:, cols], (parts[:, c, cols] for c in range(3))
                link(v.tensor_copy(p0, f))
                link(v.tensor_tensor(f, f, p0, ALU.subtract))
                link(v.tensor_copy(p1, f))
                v.tensor_tensor(p2, f, p1, ALU.subtract).then_inc(sem(done), 1)

            def keys_parts(key):
                n = LAYER_OF[key]
                dve.wait_ge(*at(key, "kt", 2))
                if n:
                    dve.wait_ge(sem("st.w"), 16 * 3 * n)
                split(KT, slice(0, TOK), "kp")

            def values(key):
                H, d, _ = NARROW[key]
                dve.wait_ge(*((sem("c.Va"), 1) if key == "a0" else (sem("c.zero"), 2)))
                Vk = Va[:, :, 0:H, :]
                v.memset(Vk[:, :, :, d:d + 1], 1.0)
                for c in range(2):
                    dve.wait_ge(*at(key, "v", c + 1))
                    src = bank[M[c]][:, :].rearrange("p (t h w) -> p t h w", t=4, w=d)
                    dst = Vk[:, 4 * c:4 * c + 4, :, 0:d]
                    for t in range(4):
                        if key == "a3":
                            ins = v.tensor_tensor(dst[:, t], src[:, t], rows[:, 5, :].rearrange("p (h w) -> p h w", w=d), ALU.add)
                        else:
                            ins = v.tensor_copy(dst[:, t], src[:, t])
                    ins.then_inc(sem("va"), 1)

            def attention(key):
                H, d, _ = NARROW[key]
                G = H // 4
                n = B * H
                if key == "a0":
                    keys_parts(key)
                    values(key)
                x_ready(dve, key)
                layer_norm(key, x, xn)
                dve.wait_ge(sem("st.w"), 16 * (3 * LAYER_OF[key] + 1))
                for c in range(2):
                    dve.wait_ge(*at(key, "qt", c + 1))
                    split(QT, slice(512 * c, 512 * (c + 1)), "qp")

                def evacuate(i):
                    dve.wait_ge(*at(key, "T", i + 1))
                    if i >= 2:
                        dve.wait_ge(*at(key, "pv", i - 1))
                    v.tensor_copy(PTs[i % 2][:, :, :], bank[2 + i % 2][:, :].rearrange("p (c q) -> p c q", c=2))\
                        .then_inc(sem("pte"), 1)

                def normalise(g):
                    b, j = g // G, g % G
                    src = bank[4 + g % 2][:, 256:512].rearrange("p (t h w) -> p t h w", t=2, w=32)
                    dve.wait_ge(*at(key, "ot", g + 1))
                    if g:
                        dve.wait_ge(*at(key, "att", g))
                    link(v.reciprocal(rc[:, :, :], src[:, :, :, d]))
                    if key == "a0":
                        link(v.tensor_tensor(rc[:, :, :], rc[:, :, :],
                                             qmask[:, 2 * b:2 * b + 2].unsqueeze(2).broadcast_to([128, 2, 4]), ALU.mult))
                    for t in range(2):
                        if t == 0 and b >= 2 and j == 0:
                            dve.wait_ge(*at(key, "attT", b - 1))
                        ins = v.tensor_tensor(att[b % 2][:, t, 4 * d * j:4 * d * (j + 1)].rearrange("p (h w) -> p h w", w=d),
                                              src[:, t, :, 0:d], rc[:, t, :].unsqueeze(2).broadcast_to([128, 4, d]), ALU.mult)
                    ins.then_inc(sem("att"), 1)

                def residual(b):
                    dve.wait_ge(*at(key, "out", b + 1))
                    xs = x[:, 2 * b:2 * b + 2, :]
                    ins = v.tensor_tensor(xs, xs, bank[7][:, 0:256].rearrange("p (t d) -> p t d", t=2), ALU.add)
                    if key == "a3":
                        link(ins)
                        ins = v.tensor_tensor(xs, xs, row(6, 2), ALU.add)
                    ins.then_inc(sem("x"), 1)

                for i in range(n + 14):
                    if i < n:
                        dve.wait_ge(*at(key, "S", i + 1))
                        v.tensor_reduce(negmax[:, i % 4, :], bank[i % 2][:, :].rearrange("p (t k) -> p t k", t=2),
                                        AX.X, ALU.max, negate=True).then_inc(sem("nm"), 1)
                    if 1 <= i <= n:
                        evacuate(i - 1)
                    if i >= 8 and (i - 8) % 4 == 0 and (i - 8) // 4 < n // 4:
                        normalise((i - 8) // 4)
                    if i >= H + 9 and (i - H - 9) % H == 0 and (i - H - 9) // H < B:
                        residual((i - H - 9) // H)

            def router(key):
                li = int(key[1])
                nE, keep = FFN[key]
                dve.wait_ge(*at(key, "lg", 1))
                src = bank[6][:, 0:NT * E].rearrange("p (t e) -> p t e", e=E)
                if key in ("f0", "f3"):
                    link(v.tensor_tensor(lg[:, :, :], src, rb[:, (0 if key == "f0" else 1):(1 if key == "f0" else 2), :].broadcast_to([128, NT, E]), ALU.add))
                else:
                    link(v.tensor_copy(lg[:, :, :], src))
                if keep == 2:
                    link(v.tensor_reduce(tmax[:, :], lg[:, :, :], AX.X, ALU.max))
                    v.tensor_tensor(ex[:, :, :], lg[:, :, :], tmax[:, :].unsqueeze(2).broadcast_to([128, NT, E]), ALU.subtract)\
                        .then_inc(sem("d"), 1)
                other = lg[:, :, :].unsqueeze(2).broadcast_to([128, NT, E, E])
                own = lg[:, :, :].unsqueeze(3).broadcast_to([128, NT, E, E])
                v.tensor_tensor(cmp_a[:, :, :, :], other, own, ALU.is_gt)
                link(v.tensor_tensor(cmp_b[:, :, :, :], other, own, ALU.is_equal))
                link(v.tensor_tensor(cmp_b[:, :, :, :], cmp_b[:, :, :, :], lowert[:, :, :].unsqueeze(1).broadcast_to([128, NT, E, E]), ALU.mult))
                link(v.tensor_tensor(cmp_a[:, :, :, :], cmp_a[:, :, :, :], cmp_b[:, :, :, :], ALU.add))
                link(v.tensor_reduce(sel[:, :, :], cmp_a[:, :, :, :], AX.X, ALU.add))
                dst = comb[:, :, 0:E]
                if keep == 1:
                    v.tensor_scalar(dst, sel[:, :, :], float(keep), None, ALU.is_lt).then_inc(sem("comb"), 1)
                    return
                link(v.tensor_scalar(sel[:, :, :], sel[:, :, :], float(keep), None, ALU.is_lt))
                dve.wait_ge(*at(key, "ex", 1))
                if key == "f1":
                    link(v.tensor_reduce(tsum[:, :], ex[:, :, :], AX.X, ALU.add))
                link(v.tensor_tensor(sel[:, :, :], sel[:, :, :], ex[:, :, :], ALU.mult))
                if key != "f1":
                    link(v.tensor_reduce(tsum[:, :], sel[:, :, :], AX.X, ALU.add))
                link(v.reciprocal(tsum[:, :], tsum[:, :]))
                v.tensor_tensor(dst, sel[:, :, :], tsum[:, :].unsqueeze(2).broadcast_to([128, NT, E]), ALU.mult)\
                    .then_inc(sem("comb"), 1)

            def ffn(key):
                nE, keep = FFN[key]
                router(key)
                dve.wait_ge(*at(key, "comb", 1))
                last = 2 * nE - 1
                for u in range(2 * nE):
                    hf, e = divmod(u, nE)
                    dve.wait_ge(*at(key, "down", u + 1))
                    if u:
                        dve.wait_ge(*at(key, "acc", u))
                    if u == 4 and key != "f2":
                        dve.wait_ge(*at(key, "b2a", 2))
                    for i in range(4):
                        t = 4 * hf + i
                        ins = v.scalar_tensor_tensor(x[:, t, :], bank[4 + u % 2][:, 128 * i:128 * (i + 1)], comb[:, t, e:e + 1],
                                                     x[:, t, :], ALU.mult, ALU.add)
                    ins.then_inc(sem("acc"), 1)
                    if u == 3 and key != "f2":
                        dve.wait_ge(*at(key, "acc", 4))
                        for c in range(2):
                            dve.wait_ge(*at(key, "b2", c + 1))
                            xs = x[:, 4 * c:4 * c + 4, :]
                            v.tensor_tensor(xs, xs, bank[M[c]][:, :].rearrange("p (t d) -> p t d", t=4), ALU.add)\
                                .then_inc(sem("b2a"), 1)
                    if u == 7 and key in NEXT:
                        keys_parts(NEXT[key])
                    if u == 8 and key in NEXT:
                        values(NEXT[key])

            def wide_attention():
                key = "a1"
                x_ready(dve, key)
                layer_norm(key, x, xn)
                dve.wait_ge(sem("ld.pos"), 16)
                pw = PWf[:, 0:WIN]
                res = PTs[0][:, :, :].rearrange("p c q -> p (c q)")[:, 0:WIN]
                link(v.tensor_copy(PW[0][:, 0:WIN], pw))
                link(v.tensor_tensor(res, pw, PW[0][:, 0:WIN], ALU.subtract))
                link(v.tensor_copy(PW[1][:, 0:WIN], res))
                v.tensor_tensor(PW[2][:, 0:WIN], res, PW[1][:, 0:WIN], ALU.subtract).then_inc(sem("a1.pw"), 1)
                for qh in range(2):
                    for h in range(H1):
                        k = qh * H1 + h
                        dve.wait_ge(sem("a1.qf"), k + 1)
                        if h == 0 and qh:
                            dve.wait_ge(sem("a1.st"), 16)
                        qf = QF[:, k % 2, :]
                        parts = [q.rearrange("p q (b h) -> p b q h", h=H1)[:, :, :, h] for q in Q1]
                        qs = qf.rearrange("p (b q) -> p b q", b=B)
                        rs = P[0][:, :, :].rearrange("p c (b q) -> p (c b) q", q=128)
                        link(v.tensor_copy(parts[0], qs))
                        link(v.tensor_tensor(rs, qs, parts[0], ALU.subtract))
                        link(v.tensor_copy(parts[1], rs))
                        v.tensor_tensor(parts[2], rs, parts[1], ALU.subtract).then_inc(sem("a1.q"), 1)
                    for u in range(16):
                        n = qh * 16 + u
                        qb, c = divmod(u, 2)
                        dve.wait_ge(sem("a1.S"), n + 1)
                        if u == 0 and qh:
                            dve.wait_ge(sem("a1.T0"), 32)
                        v.tensor_tensor(ST[:, c, :, 16 * qb:16 * qb + 16].rearrange("p n q -> p q n"),
                                        bank[n % 4][:, :].rearrange("p (q n) -> p q n", n=BH1),
                                        m1bh[:, c:c + 1, :].broadcast_to([128, 16, BH1]), ALU.add).then_inc(sem("a1.st"), 1)

                    def head_max(i):
                        dve.wait_ge(sem("a1.T0"), i + 1)
                        v.tensor_reduce(r1[:, i % 4:i % 4 + 1], bank[i % 2][:, 0:256], AX.X, ALU.max, negate=True)\
                            .then_inc(sem("a1.nm"), 1)

                    def head_scale(i):
                        dve.wait_ge(sem("a1.e"), i + 1)
                        link(v.reciprocal(r2[:, i % 4:i % 4 + 1], r2[:, i % 4:i % 4 + 1]))
                        p = P[i % 2][:, 0, :]
                        v.tensor_scalar(p, p, r2[:, i % 4:i % 4 + 1], None, ALU.mult).then_inc(sem("a1.p"), 1)

                    def head_out(i):
                        dve.wait_ge(sem("a1.G"), i + 1)
                        if i >= 2:
                            dve.wait_ge(sem("a1.o"), i - 1)
                        v.tensor_copy(GT[i % 2], bank[4 + i % 2][:, 0:128]).then_inc(sem("a1.g"), 1)

                    i0 = qh * 32
                    for i in range(32 + 5):
                        if i < 32:
                            head_max(i0 + i)
                        if 1 <= i <= 32:
                            head_scale(i0 + i - 1)
                        if 3 <= i <= 34:
                            head_out(i0 + i - 3)
                        if i >= 11 + 1 and (i - 12) % 8 == 0 and (i - 12) // 8 < B:
                            b = (i - 12) // 8
                            dve.wait_ge(sem("a1.o"), i0 + 8 * b + 8)
                            t = 2 * b + qh
                            v.tensor_tensor(x[:, t, :], x[:, t, :], bank[6 + b % 2][:, 0:128], ALU.add).then_inc(sem("x"), 1)

            def inner_layer():
                x_ready(dve, "f1")
                layer_norm("f1", x, xn)
                dve.wait_ge(*at("f1", "xn", NT))
                layer_norm("f1b", xn, xm)
                dve.wait_ge(*at("f1b", "xn", NT))
                link(v.tensor_tensor(xm[:, :, :], xm[:, :, :], row(0), ALU.mult))
                v.tensor_tensor(xm[:, :, :], xm[:, :, :], row(1), ALU.add).then_inc(sem("f1.n"), 1)
                dve.wait_ge(*at("f1", "nT", 2))
                link(v.tensor_tensor(xn[:, :, :], xn[:, :, :], xm[:, :, :], ALU.add))
                for c in range(2):
                    dve.wait_ge(sem("f1.mix"), c + 1)
                    ins = v.tensor_tensor(xm[:, 4 * c:4 * c + 4, :], xn[:, 4 * c:4 * c + 4, :],
                                          bank[M[c]][:, :].rearrange("p (t d) -> p t d", t=4), ALU.add)
                    ins.then_inc(sem("f1.m"), 1)
                dve.wait_ge(sem("f1.m"), 2)
                link(v.tensor_tensor(xm[:, :, :], xm[:, :, :], row(2), ALU.add))
                link(v.tensor_tensor(x[:, :, :], x[:, :, :], xm[:, :, :], ALU.add))
                layer_norm("f1c", xm, xn)
                dve.wait_ge(*at("f1c", "xn", NT))
                link(v.tensor_tensor(xn[:, :, :], xn[:, :, :], row(3), ALU.mult))
                v.tensor_tensor(xn[:, :, :], xn[:, :, :], row(4), ALU.add).then_inc(sem("f1.n2"), 1)

            for key in ORDER:
                if key in NARROW:
                    attention(key)
                elif key == "a1":
                    wide_attention()
                elif key == "f1":
                    inner_layer()
                    ffn(key)
                else:
                    x_ready(dve, key)
                    layer_norm(key, x, xn)
                    ffn(key)

        @block.scalar
        def _(act):
            a = nc.scalar

            def copy_T(key, dst):
                for c in range(2):
                    act.wait_ge(*at(key, "tr", c + 1))
                    a.activation(dst[:, 512 * c:512 * (c + 1)], bank[M[c]][:, :], ACT.Copy).then_inc(sem("nT"), 1)

            copy_T("ctx", cT)
            act.wait_ge(sem("ld.small"), SMALL)

            def project(key):
                for c in range(2):
                    act.wait_ge(*at(key, "k", c + 1))
                    kt = KT[:, 512 * c:512 * (c + 1)]
                    if key == "a3":
                        ins = a.activation(kt, bank[M[c]][:, :], ACT.Identity, bias=qkb[:, 1:2])
                    else:
                        ins = a.activation(kt, bank[M[c]][:, :], ACT.Copy)
                    ins.then_inc(sem("kt"), 1)

            def attention(key):
                H, d, scale = NARROW[key]
                n = B * H
                if key == "a0":
                    project(key)
                copy_T(key, nT[0])
                for c in range(2):
                    act.wait_ge(*at(key, "q", c + 1))
                    qt = QT[:, 512 * c:512 * (c + 1)]
                    if c == 0 and key != "a0":
                        act.wait_ge(*at({"a2": "a0", "a3": "a2"}[key], "qp", 2))
                    if key == "a3":
                        ins = a.activation(qt, bank[M[c]][:, :], ACT.Identity, bias=qkb[:, 0:1])
                    else:
                        ins = a.activation(qt, bank[M[c]][:, :], ACT.Copy, scale=scale)
                    ins.then_inc(sem("qt"), 1)
                for i in range(n + 14):
                    if i < n:
                        act.wait_ge(*at(key, "nm", i + 1))
                        if i >= 2:
                            act.wait_ge(*at(key, "T", i - 1))
                        for t in range(2):
                            ins = a.activation(P[i % 2][:, t, :], bank[i % 2][:, 256 * t:256 * (t + 1)], ACT.Exp,
                                               bias=negmax[:, i % 4, t:t + 1])
                        ins.then_inc(sem("e"), 1)
                    if i >= 6 and (i - 6) % 4 == 0 and (i - 6) // 4 < n // 4:
                        g = (i - 6) // 4
                        act.wait_ge(*at(key, "pv", 4 * g + 4))
                        if g >= 2:
                            act.wait_ge(*at(key, "ot", g - 1))
                        a.activation(Os[g % 2][:, :], bank[4 + g % 2][:, 0:256], ACT.Copy).then_inc(sem("oe"), 1)
                    if i >= H + 7 and (i - H - 7) % H == 0 and (i - H - 7) // H < B:
                        b = (i - H - 7) // H
                        act.wait_ge(*at(key, "attT", b + 1))
                        if b >= 2:
                            act.wait_ge(*at(key, "out", b - 1))
                        a.activation(attT[b % 2][:, :], bank[6][:, 0:256], ACT.Copy).then_inc(sem("ate"), 1)

            def ffn(key, nTk):
                nE, keep = FFN[key]
                bi = {"f0": 0, "f1": 1, "f3": 2}.get(key)
                func = {"f0": ACT.Gelu_apprx_tanh, "f1": ACT.Silu, "f2": ACT.Relu, "f3": ACT.Gelu}[key]
                if keep == 2:
                    act.wait_ge(*at(key, "d", 1))
                    a.activation(ex[:, :, :], ex[:, :, :], ACT.Exp).then_inc(sem("ex"), 1)
                for u in range(2 * nE):
                    e = u % nE
                    for c in range(FC):
                        act.wait_ge(*at(key, "up", FC * u + c + 1))
                        if c == 0 and u >= 2:
                            act.wait_ge(*at(key, "down", u - 1))
                        dst = hid[u % 2][:, c, :]
                        if bi is None:
                            ins = a.activation(dst, bank[c][:, :], func)
                        else:
                            ins = a.activation(dst, bank[c][:, :], func, bias=b1[:, bi, FC * e + c:FC * e + c + 1])
                        ins.then_inc(sem("h"), 1)
                    if u == 1 and key != "f2":
                        for c in range(2):
                            act.wait_ge(*at(key, "cT", c + 1))
                            a.activation(combT[0:nE, 512 * c:512 * (c + 1)], bank[M[c]][0:nE, :], ACT.Copy)\
                                .then_inc(sem("cTe"), 1)
                    if u == 5 and key in NEXT:
                        project(NEXT[key])

            def wide_attention():
                scale = float(D) ** -0.5
                copy_T("a1", nT[0])
                for i in range(4):
                    act.wait_ge(sem("a1.pre"), i + 1)
                    dst = (AQK, CVO)[i // 2][:, 4 * (i % 2):4 * (i % 2) + 4, :]
                    a.activation(dst, bank[M[i % 2]][:, :].rearrange("p (h m) -> p h m", h=4), ACT.Copy).then_inc(sem("a1.w"), 1)
                act.wait_ge(sem("a1.pre"), 5)
                a.activation(bst[:, 0, :], bank[5][:, 0:H1], ACT.Copy, scale=scale).then_inc(sem("a1.w"), 1)
                act.wait_ge(sem("a1.w"), 5)
                act.wait_ge(sem("c.masks"), 1)
                for qh in range(2):
                    for h in range(H1):
                        k = qh * H1 + h
                        act.wait_ge(sem("a1.t"), 2 * k + 1)
                        if h == 0 and qh:
                            act.wait_ge(sem("a1.S"), 16)
                        a.activation(T1.rearrange("p q (b h) -> p b q h", h=H1)[:, :, :, h],
                                     bank[4 + 2 * (k % 2)][:, :].rearrange("p (b q) -> p b q", b=B), ACT.Identity,
                                     bias=bst[:, 0, h:h + 1], scale=scale).then_inc(sem("a1.te"), 1)
                        act.wait_ge(sem("a1.t"), 2 * k + 2)
                        if k >= 2:
                            act.wait_ge(sem("a1.q"), k - 1)
                        a.activation(QF[:, k % 2, :], bank[5 + 2 * (k % 2)][:, :], ACT.Identity,
                                     bias=bst[:, 1, h:h + 1], scale=scale).then_inc(sem("a1.qf"), 1)
                    i0 = qh * 32
                    for j in range(33):
                        i = i0 + j
                        if j < 32:
                            act.wait_ge(sem("a1.nm"), i + 1)
                            if i >= 2:
                                act.wait_ge(sem("a1.T1"), i - 1)
                            elif i == 0:
                                act.wait_ge(sem("a1.q"), 8)
                            a.activation(P[i % 2][:, 0, :], bank[i % 2][:, 0:256], ACT.Exp, bias=r1[:, i % 4:i % 4 + 1],
                                         accum_out=r2[:, i % 4:i % 4 + 1]).then_inc(sem("a1.e"), 1)
                        if j >= 1:
                            k = i - 1
                            act.wait_ge(sem("a1.T1"), k + 1)
                            if k >= 2:
                                act.wait_ge(sem("a1.G"), k - 1)
                            a.activation(PTs[k % 2][:, 0, :], bank[2 + k % 2][:, 0:256], ACT.Copy).then_inc(sem("a1.pte"), 1)

            for key in ORDER:
                if key in NARROW:
                    attention(key)
                elif key == "a1":
                    wide_attention()
                else:
                    if key == "f1":
                        copy_T("f1", nT[0])
                        copy_T("f1n", nT[1])
                    else:
                        copy_T(key, nT[1])
                    ffn(key, nT[1])

        @block.tensor
        def _(pe):
            mm, tr = nc.tensor.matmul, nc.tensor.transpose
            reader = {}

            def take(k):
                if k in reader:
                    pe.wait_ge(*reader.pop(k))
                return bank[k]

            def transpose_all(key, src, ready):
                for c in range(2):
                    dst = take(M[c])
                    for i in range(4):
                        t = 4 * c + i
                        pe.wait_ge(*ready(t))
                        ins = tr(dst[:, 128 * i:128 * (i + 1)], src[:, t, :], ident[:, :])
                    ins.then_inc(sem("tr"), 1)
                    reader[M[c]] = at(key, "nT", c + 1)

            pe.wait_ge(sem("c.ident"), 1)
            transpose_all("ctx", cx, lambda t: (sem("ld.ctx"), 16))
            pe.wait_ge(sem("ld.aw"), 16)
            pe.wait_ge(*at("ctx", "nT", 2))

            def keys(key):
                w = 4 * LAYER_OF[key]
                for c in range(2):
                    dst = take(M[c])
                    mm(dst[:, :], aw[:, w + 1, :], cT[:, 512 * c:512 * (c + 1)], start=True, stop=True).then_inc(sem("k"), 1)
                    reader[M[c]] = at(key, "kt", c + 1)

            def values(key):
                w = 4 * LAYER_OF[key]
                for c in range(2):
                    dst = take(M[c])
                    for i in range(4):
                        t = 4 * c + i
                        ins = mm(dst[:, 128 * i:128 * (i + 1)], cT[:, 128 * t:128 * (t + 1)], aw[:, w + 2, :], start=True, stop=True)
                    ins.then_inc(sem("v"), 1)
                    reader[M[c]] = at(key, "va", c + 1)

            def attention(key):
                H, d, _ = NARROW[key]
                G = H // 4
                n = B * H
                w = 4 * LAYER_OF[key]
                R = ROWS[key]
                if key == "a0":
                    keys(key)
                    values(key)
                transpose_all(key, xn, lambda t: at(key, "xn", t + 1))
                for c in range(2):
                    pe.wait_ge(*at(key, "nT", c + 1))
                    dst = take(M[c])
                    mm(dst[:, :], aw[:, w, :], nT[0][:, 512 * c:512 * (c + 1)], start=True, stop=True).then_inc(sem("q"), 1)
                    reader[M[c]] = at(key, "qt", c + 1)
                pe.wait_ge(sem("st.k"), 16 * len(PAIRS) * (LAYER_OF[key] + 1))
                pe.wait_ge(sem("c.masks"), 1)

                def scores(i):
                    b, h = divmod(i, H)
                    if h == 0 and b % 2 == 0:
                        pe.wait_ge(sem(f"st.q{b // 2}"), 16 * len(PAIRS) * (LAYER_OF[key] + 1))
                    dst = take(i % 2)
                    for t in range(2):
                        o = dst[:, 256 * t:256 * (t + 1)]
                        ins = mm(o, Qs[0:R, h, S * b + 128 * t:S * b + 128 * (t + 1)], Ks[0:R, h, S * b:S * (b + 1)],
                                 start=True, stop=key != "a2")
                        if key == "a2":
                            ins = mm(o, identb[:, :], madd2[:, t, :], start=False, stop=True)
                    ins.then_inc(sem("S"), 1)
                    reader[i % 2] = at(key, "e", i + 1)

                def transpose_p(i):
                    pe.wait_ge(*at(key, "e", i + 1))
                    dst = take(2 + i % 2)
                    for c in range(2):
                        for t in range(2):
                            ins = tr(dst[:, 256 * c + 128 * t:256 * c + 128 * (t + 1)], P[i % 2][:, t, 128 * c:128 * (c + 1)], ident[:, :])
                    ins.then_inc(sem("T"), 1)
                    reader[2 + i % 2] = at(key, "pte", i + 1)

                def probs_v(i):
                    b, h = divmod(i, H)
                    g, j = divmod(i, 4)
                    pe.wait_ge(*at(key, "pte", i + 1))
                    if i == 0:
                        pe.wait_ge(*at(key, "va", 2))
                    dst = take(4 + g % 2) if j == 0 else bank[4 + g % 2]
                    for c in range(2):
                        ins = mm(dst[32 * j:32 * (j + 1), 0:256], Va[:, 2 * b + c, h, :], PTs[i % 2][:, c, :],
                                 start=c == 0, stop=c == 1)
                    ins.then_inc(sem("pv"), 1)

                def token_major(g):
                    pe.wait_ge(*at(key, "oe", g + 1))
                    for t in range(2):
                        ins = tr(bank[4 + g % 2][:, 256 + 128 * t:384 + 128 * t], Os[g % 2][:, 128 * t:128 * (t + 1)], ident[:, :])
                    ins.then_inc(sem("ot"), 1)
                    reader[4 + g % 2] = at(key, "att", g + 1)

                def out_transpose(b):
                    pe.wait_ge(*at(key, "att", G * (b + 1)))
                    dst = take(6)
                    for t in range(2):
                        ins = tr(dst[:, 128 * t:128 * (t + 1)], att[b % 2][:, t, :], ident[:, :])
                    ins.then_inc(sem("attT"), 1)
                    reader[6] = at(key, "ate", b + 1)

                def out_project(b):
                    pe.wait_ge(*at(key, "ate", b + 1))
                    dst = take(7)
                    for t in range(2):
                        ins = mm(dst[:, 128 * t:128 * (t + 1)], attT[b % 2][:, 128 * t:128 * (t + 1)], aw[:, w + 3, :], start=True, stop=True)
                    ins.then_inc(sem("out"), 1)
                    reader[7] = at(key, "x", b + 1)

                for i in range(n + 14):
                    if i < n:
                        scores(i)
                    if 1 <= i <= n:
                        transpose_p(i - 1)
                    if 2 <= i <= n + 1:
                        probs_v(i - 2)
                    if i >= 7 and (i - 7) % 4 == 0 and (i - 7) // 4 < n // 4:
                        token_major((i - 7) // 4)
                    if i >= H + 6 and (i - H - 6) % H == 0 and (i - H - 6) // H < B:
                        out_transpose((i - H - 6) // H)
                    if i >= H + 8 and (i - H - 8) % H == 0 and (i - H - 8) // H < B:
                        out_project((i - H - 8) // H)

            def ffn(key, nTk):
                nE, keep = FFN[key]
                li = int(key[1])
                pe.wait_ge(sem("ld.small"), SMALL)
                pe.wait_ge(*at("f1n" if key == "f1" else key, "nT", 2))
                dst = take(6)
                for t in range(NT):
                    ins = mm(dst[:, E * t:E * (t + 1)], nTk[:, 128 * t:128 * (t + 1)], rw[:, li, :], start=True, stop=True)
                ins.then_inc(sem("lg"), 1)
                reader[6] = at(key, "comb", 1)

                def up(u):
                    hf, e = divmod(u, nE)
                    pe.wait_ge(sem(f"w.slot{e}"), 32 * SLOTLOAD[key] if e < 8 else 32)
                    for c in range(FC):
                        dst = take(c)
                        mm(dst[:, :], W[:, e, 128 * c:128 * (c + 1)], nTk[:, 512 * hf:512 * (hf + 1)], start=True, stop=True)\
                            .then_inc(sem("up"), 1)
                        reader[c] = at(key, "h", FC * u + c + 1)

                def down(u):
                    e = u % nE
                    pe.wait_ge(*at(key, "h", FC * (u + 1)))
                    dst = take(4 + u % 2)
                    for i in range(4):
                        for c in range(FC):
                            ins = mm(dst[:, 128 * i:128 * (i + 1)], hid[u % 2][:, c, 128 * i:128 * (i + 1)],
                                     W[:, e, F + 128 * c:F + 128 * (c + 1)], start=c == 0, stop=c == FC - 1)
                    ins.then_inc(sem("down"), 1)
                    reader[4 + u % 2] = at(key, "acc", u + 1)

                def biases():
                    bi = {"f0": 0, "f1": 1, "f3": 2}[key]
                    pe.wait_ge(*at(key, "comb", 1))
                    for c in range(2):
                        dst = take(M[c])
                        for i in range(4):
                            ins = tr(dst[0:nE, 128 * i:128 * (i + 1)], comb[:, 4 * c + i, 0:nE], ident[:, :])
                        ins.then_inc(sem("cT"), 1)
                        reader[M[c]] = at(key, "cTe", c + 1)

                def biases2():
                    bi = {"f0": 0, "f1": 1, "f3": 2}[key]
                    for c in range(2):
                        dst = take(M[c])
                        for i in range(4):
                            t = 4 * c + i
                            ins = mm(dst[:, 128 * i:128 * (i + 1)], combT[0:nE, 128 * t:128 * (t + 1)], b2[0:nE, bi, :], start=True, stop=True)
                        ins.then_inc(sem("b2"), 1)
                        reader[M[c]] = at(key, "b2a", c + 1)

                up(0)
                for u in range(2 * nE):
                    if u + 1 < 2 * nE:
                        up(u + 1)
                    down(u)
                    if u == 0 and key != "f2":
                        biases()
                    if u == 2 and key != "f2":
                        biases2()
                    if u == 5 and key in NEXT:
                        keys(NEXT[key])
                    if u == 7 and key in NEXT:
                        values(NEXT[key])

            def wide_attention():
                transpose_all("a1", xn, lambda t: at("a1", "xn", t + 1))
                pe.wait_ge(sem("ld.wide"), 16 * 5)
                for i in range(4):
                    dst = take(M[i % 2])
                    l, r = ((WQT, WKT), (WVT, WO))[i // 2]
                    for j in range(4):
                        h = 4 * (i % 2) + j
                        ins = mm(dst[:, 128 * j:128 * (j + 1)], l[:, h, :], r[:, h, :], start=True, stop=True)
                    ins.then_inc(sem("a1.pre"), 1)
                    reader[M[i % 2]] = (sem("a1.w"), i + 1)
                dst = take(5)
                for h in range(H1):
                    ins = mm(dst[:, h:h + 1], WKT[:, h, :], bub[:, 0, h:h + 1], start=True, stop=True)
                ins.then_inc(sem("a1.pre"), 1)
                reader[5] = (sem("a1.w"), 5)
                pe.wait_ge(sem("a1.w"), 5)
                pe.wait_ge(*at("a1", "nT", 2))
                xq = nT[0][:, :].rearrange("p (b s q) -> p b s q", b=B, s=2)
                for qh in range(2):
                    for h in range(H1):
                        k = qh * H1 + h
                        for j, wt in ((0, AQK), (1, WQ)):
                            kb = 4 + 2 * (k % 2) + j
                            dst = take(kb)
                            mm(dst[:, :].rearrange("p (b q) -> p b q", b=B), wt[:, h, :], xq[:, :, qh, :], start=True, stop=True)\
                                .then_inc(sem("a1.t"), 1)
                            reader[kb] = (sem("a1.qf" if j else "a1.te"), k + 1)
                    pe.wait_ge(sem("a1.te"), 8 * (qh + 1))
                    pe.wait_ge(sem("a1.q"), 8 * (qh + 1))
                    pe.wait_ge(sem("a1.pw"), 1)
                    for u in range(16):
                        n = qh * 16 + u
                        qb, c = divmod(u, 2)
                        dst = take(n % 4)[:, :].rearrange("p (q n) -> p q n", n=BH1)
                        for b in range(B):
                            mm(dst[:, :, H1 * b:H1 * (b + 1)], cT[:, S * b + 128 * c:S * b + 128 * (c + 1)],
                               T1[:, 16 * qb:16 * qb + 16, H1 * b:H1 * (b + 1)], start=b == 0, stop=False, skip_group_check=True)
                        for qi in range(16):
                            off = S - 1 - (128 * qh + 16 * qb + qi) + 128 * c
                            for pj, qj in ((0, 0), (0, 1), (0, 2), (1, 0), (1, 1), (2, 0)):
                                ins = mm(dst[:, qi, :], PW[pj][:, off:off + 128], Q1[qj][:, 16 * qb + qi, :],
                                         start=False, stop=qi == 15 and pj == 2, skip_group_check=True)
                        ins.then_inc(sem("a1.S"), 1)
                        reader[n % 4] = (sem("a1.st"), n + 1)
                    pe.wait_ge(sem("a1.st"), 16 * (qh + 1))

                    def scores_q(i, j):
                        b, h = divmod(j, H1)
                        dst = take(i % 2)
                        for c in range(2):
                            ins = tr(dst[:, 128 * c:128 * (c + 1)], ST[:, c, j, :], ident[:, :])
                        ins.then_inc(sem("a1.T0"), 1)
                        reader[i % 2] = (sem("a1.e"), i + 1)

                    def probs_t(i, j):
                        pe.wait_ge(sem("a1.p"), i + 1)
                        dst = take(2 + i % 2)
                        for c in range(2):
                            ins = tr(dst[:, 128 * c:128 * (c + 1)], P[i % 2][:, 0, 128 * c:128 * (c + 1)], ident[:, :])
                        ins.then_inc(sem("a1.T1"), 1)
                        reader[2 + i % 2] = (sem("a1.pte"), i + 1)

                    def probs_ctx(i, j):
                        b = j // H1
                        pe.wait_ge(sem("a1.pte"), i + 1)
                        dst = take(4 + i % 2)
                        for c in range(2):
                            ins = mm(dst[:, 0:128], cx[:, 2 * b + c, :], PTs[i % 2][:, 0, 128 * c:128 * (c + 1)], start=c == 0, stop=c == 1)
                        ins.then_inc(sem("a1.G"), 1)
                        reader[4 + i % 2] = (sem("a1.g"), i + 1)

                    def out_head(i, j):
                        b, h = divmod(j, H1)
                        pe.wait_ge(sem("a1.g"), i + 1)
                        dst = take(6 + b % 2) if h == 0 else bank[6 + b % 2]
                        mm(dst[:, 0:128], GT[i % 2], CVO[:, h, :], start=h == 0, stop=h == H1 - 1).then_inc(sem("a1.o"), 1)
                        if h == H1 - 1:
                            reader[6 + b % 2] = at("a1", "x", B * qh + b + 1)

                    i0 = qh * 32
                    for j in range(32 + 4):
                        if j < 32:
                            scores_q(i0 + j, j)
                        if 2 <= j <= 33:
                            probs_t(i0 + j - 2, j - 2)
                        if 3 <= j <= 34:
                            probs_ctx(i0 + j - 3, j - 3)
                        if 4 <= j <= 35:
                            out_head(i0 + j - 4, j - 4)

            for key in ORDER:
                if key in NARROW:
                    attention(key)
                elif key == "a1":
                    wide_attention()
                elif key == "f1":
                    transpose_all("f1", xm, lambda t: (sem("f1.n"), 1))
                    pe.wait_ge(*at("f1", "nT", 2))
                    for c in range(2):
                        dst = take(M[c])
                        for i in range(4):
                            t = 4 * c + i
                            ins = mm(dst[:, 128 * i:128 * (i + 1)], nT[0][:, 128 * t:128 * (t + 1)], mixw[:, :], start=True, stop=True)
                        ins.then_inc(sem("f1.mix"), 1)
                        reader[M[c]] = (sem("f1.m"), c + 1)
                    transpose_all("f1n", xn, lambda t: (sem("f1.n2"), 1))
                    ffn(key, nT[1])
                else:
                    transpose_all(key, xn, lambda t: at(key, "xn", t + 1))
                    ffn(key, nT[1])


def kernel(**inputs):
    import numpy as np
    import concourse.bacc as bacc
    from concourse.bass_utils import run_bass_kernel_spmd

    g = {k: np.asarray(v) for k, v in inputs.items()}
    T = lambda a, *p: np.ascontiguousarray(np.transpose(a, p or None))
    row = np.arange(WIN) - (S - 1) + POS // 2
    row = np.clip(np.where(row < 0, row + POS, row), 0, POS - 1)
    cols = lambda a: np.ascontiguousarray(a.reshape(-1, 128).T)
    aw = []
    for n in ("L0_xattn_W_", "L2_xattn_w_", "L3_xattn_W"):
        aw += [T(g[n + s]) for s in "qkvo"]
    a = {
        "x": g["x"].reshape(TOK, D), "ctx": g["ctx_1024"].reshape(TOK, D), "lens": g["_lenS2"],
        "mask1": np.ascontiguousarray(g["mask_BxS2_bf1"].reshape(2 * B, 128).T).view(np.uint8),
        "mask2": g["mask_1x1xSxS2_if1"].reshape(S, S),
        "aw": np.stack(aw),
        "qkb": T(np.stack([g["L3_xattn_bq"], g["L3_xattn_bk"]])),
        "rows": np.stack([g["L1_ffn_g1"], g["L1_ffn_be1"], g["L1_ffn_mix_b"], g["L1_ffn_g2"], g["L1_ffn_be2"],
                          g["L3_xattn_bv"], g["L3_xattn_bo"]]),
        "rb": np.stack([g["L0_ffn_router_b"], g["L3_ffn_br"]]),
        "rw": np.stack([T(g["L0_ffn_router_w"]), g["L1_ffn_router_w"], g["L2_ffn_Wr"], g["L3_ffn_wr"]]),
        "mixw": g["L1_ffn_mix_w"],
        "bu": g["L1_xattn_bu"], "bv": g["L1_xattn_bv"],
        "a1.wqT": T(g["L1_xattn_wq"], 1, 2, 0), "a1.wkT": T(g["L1_xattn_wk"], 1, 2, 0),
        "a1.wvT": T(g["L1_xattn_wv"], 1, 2, 0), "a1.wo": g["L1_xattn_wo"], "a1.wq": T(g["L1_xattn_wq"], 0, 2, 1),
        "a1.pos": T(g["L1_xattn_pos_w"][row]),
        "f0.w1": np.concatenate([T(g["L0_ffn_spec_w1"], 0, 2, 1), T(g["L0_ffn_shared_w1"])[None]]),
        "f0.w2": np.concatenate([T(g["L0_ffn_spec_w2"], 0, 2, 1), T(g["L0_ffn_shared_w2"])[None]]),
        "f0.b1": cols(np.concatenate([g["L0_ffn_spec_b1"], g["L0_ffn_shared_b1"][None]])),
        "f0.b2": np.concatenate([g["L0_ffn_spec_b2"], g["L0_ffn_shared_b2"][None]]),
        "f1.w1": g["L1_ffn_w1"], "f1.w2": g["L1_ffn_w2"], "f1.b1": cols(g["L1_ffn_b1"]), "f1.b2": g["L1_ffn_b2"],
        "f2.w1": g["L2_ffn_W1"], "f2.w2": g["L2_ffn_W2"],
        "f3.w1": g["L3_ffn_w1"], "f3.w2": g["L3_ffn_w2"], "f3.b1": cols(g["L3_ffn_b1"]), "f3.b2": g["L3_ffn_b2"],
    }
    nc = bacc.Bacc("TRN2", target_bir_lowering=False, num_devices=1)
    arrays, handles = {}, {}
    for name, v in a.items():
        dram = "in_" + name.replace(".", "_")
        arrays[dram] = np.ascontiguousarray(v)
        handles[name] = nc.dram_tensor(dram, v.shape, mybir.dt.from_np(v.dtype), kind="ExternalInput").ap()
    o = nc.dram_tensor("out_x", (TOK, D), mybir.dt.float32, kind="ExternalOutput").ap()
    build(nc, handles, o)
    r = run_bass_kernel_spmd(nc, [arrays], core_ids=[0])
    return r.results[0]["out_x"].reshape(B, S, D)
```

```python
import concourse.bass as bass
from concourse import mybir
from contextlib import ExitStack

B, S, D = 4, 256, 128
TOK = B * S
NT = TOK // 128
F, E = 512, 8
FC = F // 128
H1 = 8
BH1 = B * H1
POS = 128
WIN = 2 * S - 1
LN_EPS = 1e-5
BIG_NEG = -float(2 ** 30)
L0_NEG = -float(2 ** 32)
L1_NEG = -3.0e38

NARROW = {"a0": (8, 16, 0.25), "a2": (16, 8, float(8 ** -0.5)), "a3": (16, 8, 1.0)}
LAYER_OF = {"a0": 0, "a2": 1, "a3": 2}
PAIRS = ((0, 0), (0, 1), (1, 0), (1, 1), (0, 2), (2, 0))
MASK_ROW = 96
ROWS = {"a0": 128, "a2": 96, "a3": 96}
FFN = {"f0": (9, 2), "f1": (8, 2), "f2": (8, 2), "f3": (8, 1)}


def build(nc, A, out):
    fp32, bf16, i32, u8 = mybir.dt.float32, mybir.dt.bfloat16, mybir.dt.int32, mybir.dt.uint8
    fp32r = mybir.dt.float32r
    ALU, ACT, AX = mybir.AluOpType, mybir.ActivationFunctionType, mybir.AxisListType
    ctx = ExitStack()
    with ctx:
        def sb(name, shape, dt=fp32):
            return ctx.enter_context(nc.sbuf_tensor(name, shape, dt))

        made = {}

        def sem(name):
            if name not in made:
                made[name] = ctx.enter_context(nc.semaphore(name.replace(".", "_")))
            return made[name]

        narrow = {k: B * h for k, (h, _, _) in NARROW.items()}
        COUNTS = {n: [("a0", c("a0")), ("a2", c("a2")), ("a3", c("a3"))] for n, c in {
            **dict.fromkeys(("k", "kt", "v", "va", "q", "qt", "qp"), lambda k: 2), "kp": lambda k: 1,
            **dict.fromkeys(("S", "nm", "e", "T", "pv"), lambda k: narrow[k]),
            "pte": lambda k: narrow[k] - narrow[k] // 4, "pta": lambda k: narrow[k] // 4,
            **dict.fromkeys(("oe", "ot", "att"), lambda k: narrow[k] // 4),
            **dict.fromkeys(("attT", "ate", "out"), lambda k: B)}.items()}
        COUNTS |= {n: [(k, c(k)) for k in ("f0", "f1", "f2", "f3")] for n, c in {
            **dict.fromkeys(("lg", "lgc", "comb"), lambda k: 2), **dict.fromkeys(("d", "ex"), lambda k: 2 * int(FFN[k][1] == 2)),
            **dict.fromkeys(("up", "h"), lambda k: 2 * FC * FFN[k][0]), **dict.fromkeys(("down", "acc", "wp"), lambda k: 2 * FFN[k][0]), "np": lambda k: 2,
            **dict.fromkeys(("cT", "cTe", "b2", "b2a"), lambda k: 0 if k == "f2" else 2)}.items()}
        halves = lambda keys: [f"{k}.{hf}" for k in keys for hf in range(2)]
        inner = lambda keys: [f"{k}.{hf}" for hf in range(2) for k in keys]
        norms = halves(("a0", "f0", "a1")) + inner(("f1", "f1b", "f1c")) + halves(("a2", "f2", "a3", "f3"))
        COUNTS |= {"mv": [(k, 1) for k in norms], "rstd": [(k, 1) for k in norms], "xn": [(k, 4) for k in norms]}
        turns = halves(("ctx", "a0", "f0", "a1")) + inner(("f1", "f1n")) + halves(("a2", "f2", "a3", "f3"))
        COUNTS |= {n: [(k, 1) for k in turns] for n in ("tr", "nT")}
        COUNTS["x"] = [("a0", B), ("a1", NT), ("a2", B), ("a3", B)]

        def at(key, name, v):
            base = 0
            for k, total in COUNTS[name]:
                if k == key:
                    assert 0 < v <= total, (key, name, v)
                    return sem(name), base + v
                base += total
            raise KeyError(key)

        def on_act(i):
            return i % 4 == 2

        def probs_in_sbuf(key, i):
            return at(key, "pta", (i + 2) // 4) if on_act(i) else at(key, "pte", i + 1 - (i + 2) // 4)

        arena = -(-nc.sbuf_base // 32) * 32
        sb("arena", [128, 4096])

        def place(name, at_byte, shape, dt=fp32):
            return nc.alloc_sbuf_tensor_at(name, shape, dt, offset=arena + at_byte)

        x = sb("x_res", [128, NT, D])
        xn = place("xn", 0, [128, NT, D])
        xm = sb("xm", [128, NT, D])
        nT = [place("nT0", 4096, [128, TOK]), sb("nT1", [128, TOK])]
        cx = sb("cx", [128, NT, D])
        cT = sb("cT", [128, TOK])
        W = sb("W", [128, 9, 2 * F])
        aw = sb("aw", [128, 12, D])
        big = sb("big", [128, 18432])
        late = sb("late", [128, 8192])
        P = [place(f"P{i}", 8192 + 2048 * i, [128, 2, S]) for i in range(2)]
        PTs = [place(f"PTs{i}", 12288 + 2048 * i, [128, 2, S]) for i in range(2)]
        ident = sb("ident", [128, 128])
        identb = sb("identb", [128, 128], bf16)
        lowert = sb("lowert", [128, E, E])
        half = sb("half", [128, NT])
        stats = sb("stats", [128, NT, 6])
        mv = sb("mv", [128, NT, 2])
        rstd = sb("rstd", [128, NT])
        negmax = sb("negmax", [128, 4, 2])
        QT = sb("QT", [128, TOK])
        KT = sb("KT", [128, TOK])
        Os = [sb("Os0", [128, S]), sb("Os1", [128, S])]
        att = [sb("att0", [128, 2, D]), sb("att1", [128, 2, D])]
        attT = [sb("attT0", [128, S]), sb("attT1", [128, S])]
        rc = sb("rc", [128, 2, 4])
        madd2 = sb("madd2", [128, 2, S], bf16)
        leni = sb("leni", [128, B], i32)
        lenf = sb("lenf", [128, B])
        qpos = sb("qpos", [128, NT])
        qmask = sb("qmask", [128, NT])
        m1u = sb("m1u", [128, 2 * B], u8)
        m1f = sb("m1f", [128, 2 * B])
        m1bh = sb("m1bh", [128, 2, BH1])
        qkb = sb("qkb", [128, 2])
        rows = sb("rows", [128, 7, D])
        rb = sb("rb", [128, 2, E])
        rw = sb("rw", [128, 4, E])
        b1 = sb("b1", [128, 3, 9 * FC])
        b2 = sb("b2", [9, 3, D])
        mixw = sb("mixw", [128, D])
        lg = sb("lg", [128, NT, E])
        sel = sb("sel", [128, NT, E])
        ex = sb("ex", [128, NT, E])
        tmax = sb("tmax", [128, NT])
        tsum = sb("tsum", [128, NT])
        comb = sb("comb", [128, NT, 9])
        bub = sb("bub", [128, 2, H1])
        bst = sb("bst", [128, 2, H1])
        r1 = sb("r1", [128, 4])
        r2 = sb("r2", [128, 4])

        keyrow = big[:, 17920:18176]
        combT = KT[0:9, :]
        m2i = xm[:, 0:4, :].rearrange("p t d -> p (t d)").bitcast(i32).rearrange("p (t k) -> p t k", t=2)
        cmp_a, cmp_b = (QT[:, 512 * i:512 * (i + 1)].rearrange("p (t e f) -> p t e f", t=NT, e=E) for i in range(2))
        Qs, Ks = (big[:, 8192 * i:8192 * (i + 1)].bitcast(bf16).rearrange("p (h t) -> p h t", h=16) for i in range(2))
        parts = big[:, 16384:17920].bitcast(bf16).rearrange("p (c t) -> p c t", c=3)
        T1 = big[:, 0:4096].rearrange("p (q n) -> p q n", n=BH1)
        Q1 = [big[:, 4096 + 2048 * i:6144 + 2048 * i].bitcast(bf16).rearrange("p (q n) -> p q n", n=BH1)
              for i in range(3)]
        ST = big[:, 10240:18432].rearrange("p (c n q) -> p c n q", c=2, n=BH1)
        Va = late[:, 0:4096].rearrange("p (t h w) -> p t h w", t=NT, w=32)
        hid = [late[:, 4096 + 2048 * i:6144 + 2048 * i].rearrange("p (c t) -> p c t", c=FC) for i in range(2)]
        PTs.append(late[:, 4096:4608].rearrange("p (c q) -> p c q", c=2))
        wide = late[:, :].rearrange("p (w h m) -> p w h m", w=8, h=H1)
        WQT, WKT, WVT, WO, WQ, AQK, CVO = (wide[:, i] for i in range(7))
        QF = late[:, 7168:8192].rearrange("p (s t) -> p s t", s=2)
        PWf = QT
        PW = [KT[:, 256 * i:256 * (i + 1)].bitcast(bf16) for i in range(3)]
        QR = [Os[i][:, :] for i in range(2)]
        GT = [att[i][:, 0, :] for i in range(2)]

        nL, nH = (place(n, 4096 * i, [128, TOK], fp32r) for i, n in enumerate(("nL", "nH")))
        wH, wL = ([place(f"{n}{i}", o + 2048 * i, [128, F], fp32r) for i in range(2)] for n, o in (("wH", 8192), ("wL", 12288)))

        scratch = nc.dram_tensor("parts_scratch", [2, 128, 3, TOK], bf16, kind="Internal").ap()

        bank = [ctx.enter_context(nc.psum_tensor(f"bank{i}", [128, 512], fp32)) for i in range(8)]
        M = [6, 7]

        PVB = [4, 5, M[1]]

        block = ctx.enter_context(nc.Block())

        SMALL = 16 * 16
        nexp = lambda key: FFN[key][0]
        ORDER = ["a0", "f0", "a1", "f1", "a2", "f2", "a3", "f3"]
        NEXT = {"f1": "a2", "f2": "a3"}
        KV_STEP = {"f1": 8, "f2": 5}

        def bias_step(key, hf):
            return 5 if (key, hf) == ("f1", 0) else 3

        AFTER = dict(zip(ORDER, ORDER[1:]))
        SLOTLOAD = {"f0": 1, "f1": 2, "f2": 3, "f3": 4}

        def x_ready(eng, key, hf=1):
            n = len(ORDER) if key == "out" else ORDER.index(key)
            if n == 0:
                eng.wait_ge(sem("ld.x"), 16)
            elif ORDER[n - 1] in FFN:
                eng.wait_ge(*at(ORDER[n - 1], "acc", (hf + 1) * FFN[ORDER[n - 1]][0]))
            elif ORDER[n - 1] == "a1":
                eng.wait_ge(*at("a1", "x", B + 2 * (hf + 1)))
            else:
                eng.wait_ge(*at(ORDER[n - 1], "x", 2 * (hf + 1)))

        loads = {"ld.ctx": 16, "ld.x": 16, "ld.aw": 16, "ld.small": 16 * 18}

        @block.sync
        def _(sp):
            sp.dma_start(cx[:, :, :], A["ctx"].rearrange("(t p) d -> p t d", p=128)).then_inc(sem("ld.ctx"), 16)
            sp.dma_start(x[:, :, :], A["x"].rearrange("(t p) d -> p t d", p=128)).then_inc(sem("ld.x"), 16)
            sp.dma_start(aw[:, :, :], A["aw"].rearrange("w i o -> i w o")).then_inc(sem("ld.aw"), 16)

            def expert(key, e):
                prev = {"f1": "f0", "f2": "f1", "f3": "f2"}.get(key)
                if prev and e < FFN[prev][0]:
                    sp.wait_ge(*at(prev, "down", FFN[prev][0] + e + 1))
                sp.dma_start(W[:, e, 0:F], A[f"{key}.w1"][e]).then_inc(sem(f"w.slot{e}"), 16)
                sp.dma_start(W[:, e, F:2 * F].rearrange("p (c d) -> p c d", c=FC),
                             A[f"{key}.w2"][e].rearrange("(c p) d -> p c d", p=128)).then_inc(sem(f"w.slot{e}"), 16)

            small = [(m2i[:, :, :], A["mask2"].rearrange("(t p) k -> p t k", p=128)),
                     (m1u[:, :], A["mask1"]),
                     (leni[:, :], bass.AP(A["lens"].tensor, 0, [[0, 128], [1, B]])),
                     (qkb[:, :], A["qkb"]),
                     (rows[:, :, :], bass.AP(A["rows"].tensor, 0, [[0, 128], [D, 7], [1, D]])),
                     (rb[:, :, :], bass.AP(A["rb"].tensor, 0, [[0, 128], [E, 2], [1, E]])),
                     (rw[:, :, :], A["rw"].rearrange("l d e -> d l e")),
                     (b1[:, 0, :], A["f0.b1"]),
                     (b1[:, 1, 0:8 * FC], A["f1.b1"]),
                     (b1[:, 2, 0:8 * FC], A["f3.b1"]),
                     (b2[:, 0, :], A["f0.b2"]), (b2[0:8, 1, :], A["f1.b2"]), (b2[0:8, 2, :], A["f3.b2"]),
                     (mixw[:, :], A["mixw"]),
                     (bub[:, 0, :], A["bu"]), (bub[:, 1, :], A["bv"])]
            for dst, src in small:
                sp.dma_start(dst, src).then_inc(sem("ld.small"), 16)
            loads["ld.small"] = 16 * len(small)
            def stack(key, side, half=None):
                H, d, _ = NARROW[key]
                n = LAYER_OF[key]
                cols = slice(0, TOK) if half is None else slice(512 * half, 512 * (half + 1))
                dst = (Qs, Ks)[side]
                if side:
                    sp.wait_ge(*at(key, "kp", 1))
                    if key == "a3":
                        sp.wait_ge(*at("a2", "S", narrow["a2"]))
                    elif key == "a2":
                        sp.wait_ge(sem("c.zero"), 2)
                else:
                    sp.wait_ge(*at(key, "qp", half + 1))
                done = 16 * (3 * n + (1 if side else 2 + half))
                sp.dma_start(scratch[side, :, :, cols], parts[:, :, cols]).then_inc(sem("st.w"), 16)
                sp.wait_ge(sem("st.w"), done)
                src = scratch[side].rearrange("(h i) c t -> i h c t", i=d)
                for r, pair in enumerate(PAIRS):
                    sp.dma_start(dst[r * d:(r + 1) * d, 0:H, cols], src[:, :, pair[side], cols])\
                      .then_inc(sem("st.k" if side else f"st.q{half}"), 16)

            stack("a0", 1)
            stack("a0", 0, 0)
            stack("a0", 0, 1)
            for e in range(9):
                expert("f0", e)
            sp.wait_ge(*at("f0", "down", 2 * FFN["f0"][0]))
            for i, n in enumerate(("wqT", "wkT", "wvT", "wo", "wq")):
                sp.dma_start(wide[:, i], A[f"a1.{n}"]).then_inc(sem("ld.wide"), 16)
            sp.dma_start(PWf[:, 0:WIN], A["a1.pos"]).then_inc(sem("ld.pos"), 16)
            for e in range(8):
                expert("f1", e)
            for key, nxt in (("a2", "f2"), ("a3", "f3")):
                stack(key, 1)
                for e in range(8):
                    if e == 4:
                        stack(key, 0, 0)
                    expert(nxt, e)
                stack(key, 0, 1)
            x_ready(sp, "out")
            sp.dma_start(out.rearrange("(t p) d -> p t d", p=128), x[:, :, :]).then_inc(sem("stored"), 16)
            sp.wait_ge(sem("stored"), 16)

        @block.gpsimd
        def _(pool):
            chain = [0]

            def link(ins):
                chain[0] += 1
                ins.then_inc(sem("pool.chain"), 1)
                pool.wait_ge(sem("pool.chain"), chain[0])

            link(pool.memset(ident[:, :], 0.0))
            link(pool.affine_select(out=ident[:, :], in_=ident[:, :], compare_op=ALU.not_equal, fill=1.0, base=0,
                                    pattern=[[-1, 128]], channel_multiplier=1))
            pool.tensor_copy(identb[:, :], ident[:, :]).then_inc(sem("c.ident"), 1)
            pool.wait_ge(sem("c.ident"), 1)
            link(pool.memset(half[:, :], -0.5))
            link(pool.memset(Qs[96:128, 0:8, :], 0.0))
            pool.memset(Ks[96:128, 0:8, :], 0.0).then_inc(sem("c.zero"), 1)
            pool.wait_ge(sem("c.zero"), 1)
            link(pool.iota(keyrow[:, :], pattern=[[1, S]], base=0, channel_multiplier=0, allow_small_or_imprecise_dtypes=True))
            link(pool.iota(qpos[:, :].rearrange("p (b t) -> p b t", t=2), pattern=[[0, B], [128, 2]], base=0,
                           channel_multiplier=1, allow_small_or_imprecise_dtypes=True))
            link(pool.memset(lowert[:, :, :], 1.0))
            pool.affine_select(out=lowert[:, :, :], in_=lowert[:, :, :], compare_op=ALU.is_gt, fill=0.0, base=0,
                               pattern=[[1, E], [-1, E]], channel_multiplier=0).then_inc(sem("c.rest"), 1)
            pool.wait_ge(sem("c.rest"), 1)
            link(pool.memset(comb[:, :, :], 1.0))
            pool.memset(Va[:, :, :, :], 0.0).then_inc(sem("c.Va"), 1)

            def layer_norm_rstd(name):
                ts = slice(4 * int(name[-1]), 4 * int(name[-1]) + 4)
                pool.wait_ge(*at(name, "mv", 1))
                link(pool.tensor_scalar(rstd[:, ts], mv[:, ts, 1], LN_EPS, None, ALU.add))
                pool.tensor_tensor(rstd[:, ts], rstd[:, ts], half[:, ts], ALU.pow).then_inc(sem("rstd"), 1)
                pool.wait_ge(*at(name, "rstd", 1))

            for name in norms:
                layer_norm_rstd(name)
                if name == "f1c.1":
                    pool.wait_ge(sem("a1.o"), 2 * BH1)
                    link(pool.memset(Va[:, :, :, :], 0.0))
                    pool.memset(big[:, 0:16384], 0.0).then_inc(sem("c.zero"), 1)
                    pool.wait_ge(sem("c.zero"), 2)

        @block.vector
        def _(dve):
            chain = [0]
            v = nc.vector

            def link(ins):
                chain[0] += 1
                ins.then_inc(sem("dve.chain"), 1)
                dve.wait_ge(sem("dve.chain"), chain[0])

            def norm_stats(key, hf, src):
                n = norms.index(f"{key}.{hf}")
                if n:
                    dve.wait_ge(*at(norms[n - 1], "xn", 4))
                for t in range(4 * hf, 4 * hf + 4):
                    ins = v.bn_stats(stats[:, t, :], src[:, t, :])
                link(ins)
                for t in range(4 * hf, 4 * hf + 4):
                    ins = v.bn_aggr(mv[:, t, :], stats[:, t, :])
                ins.then_inc(sem("mv"), 1)

            def norm_apply(key, hf, src, dst):
                dve.wait_ge(*at(f"{key}.{hf}", "rstd", 1))
                for t in range(4 * hf, 4 * hf + 4):
                    v.tensor_scalar(dst[:, t, :], src[:, t, :], mv[:, t, 0:1], rstd[:, t:t + 1],
                                    ALU.subtract, ALU.mult).then_inc(sem("xn"), 1)

            def query_parts(key, hf):
                dve.wait_ge(sem("st.w"), 16 * (3 * LAYER_OF[key] + 1))
                dve.wait_ge(*at(key, "qt", hf + 1))
                split(QT, slice(512 * hf, 512 * (hf + 1)), "qp")

            def row(i, n=NT):
                return rows[:, i:i + 1, :].broadcast_to([128, n, D])

            dve.wait_ge(sem("ld.small"), SMALL)
            dve.wait_ge(sem("c.rest"), 1)
            v.tensor_scalar(madd2[:, :, :], m2i[:, :, :], 0.0, BIG_NEG, ALU.is_equal, ALU.mult)
            link(v.tensor_copy(lenf[:, :], leni[:, :]))
            dve.wait_ge(sem("c.zero"), 1)
            v.memset(Qs[MASK_ROW:MASK_ROW + 1, 0:8, :], 1.0)
            for b in range(B):
                r = MASK_ROW
                v.tensor_scalar(Ks[r:r + 1, 0:8, S * b:S * (b + 1)], keyrow[r:r + 1, :].unsqueeze(1).broadcast_to([1, 8, S]),
                                lenf[r:r + 1, b:b + 1], L0_NEG, ALU.is_ge, ALU.mult)
                v.tensor_scalar(qmask[:, 2 * b:2 * b + 2], qpos[:, 2 * b:2 * b + 2], lenf[:, b:b + 1], None, ALU.is_lt)
            link(v.tensor_copy(m1f[:, :], m1u[:, :]))
            link(v.tensor_scalar(m1f[:, :], m1f[:, :], 1.0, -L1_NEG, ALU.subtract, ALU.mult))
            for c in range(2):
                ins = v.tensor_copy(m1bh[:, c, :].rearrange("p (b h) -> p b h", h=H1),
                                    m1f[:, :].rearrange("p (b c) -> p b c", c=2)[:, :, c:c + 1].broadcast_to([128, B, H1]))
            link(v.tensor_scalar(bst[:, 1, :], bub[:, 1, :], float(D) ** -0.5, None, ALU.mult))
            ins = v.memset(r1[:, :], 0.0)
            ins.then_inc(sem("c.masks"), 1)

            def split(src, cols, done):
                f, (p0, p1, p2) = src[:, cols], (parts[:, c, cols] for c in range(3))
                link(v.tensor_copy(p0, f))
                link(v.tensor_tensor(f, f, p0, ALU.subtract))
                link(v.tensor_copy(p1, f))
                v.tensor_tensor(p2, f, p1, ALU.subtract).then_inc(sem(done), 1)

            def keys_parts(key):
                n = LAYER_OF[key]
                dve.wait_ge(*at(key, "kt", 2))
                if n:
                    dve.wait_ge(sem("st.w"), 16 * 3 * n)
                split(KT, slice(0, TOK), "kp")

            def values(key):
                H, d, _ = NARROW[key]
                dve.wait_ge(*((sem("c.Va"), 1) if key == "a0" else (sem("c.zero"), 2)))
                Vk = Va[:, :, 0:H, :]
                v.memset(Vk[:, :, :, d:d + 1], 1.0)
                for c in range(2):
                    dve.wait_ge(*at(key, "v", c + 1))
                    src = bank[M[c]][:, :].rearrange("p (t h w) -> p t h w", t=4, w=d)
                    dst = Vk[:, 4 * c:4 * c + 4, :, 0:d]
                    for t in range(4):
                        if key == "a3":
                            ins = v.tensor_tensor(dst[:, t], src[:, t], rows[:, 5, :].rearrange("p (h w) -> p h w", w=d), ALU.add)
                        else:
                            ins = v.tensor_copy(dst[:, t], src[:, t])
                    ins.then_inc(sem("va"), 1)

            def attention(key):
                H, d, _ = NARROW[key]
                G = H // 4
                n = B * H
                if key == "a0":
                    keys_parts(key)
                    values(key)
                    x_ready(dve, key, 0)
                    norm_stats(key, 0, x)
                    norm_apply(key, 0, x, xn)
                    query_parts(key, 0)
                x_ready(dve, key, 1)
                norm_stats(key, 1, x)
                ffn_key = AFTER[key]

                def evacuate(i):
                    dve.wait_ge(*at(key, "T", i + 1))
                    if i >= 3:
                        dve.wait_ge(*at(key, "pv", i - 2))
                    v.tensor_copy(PTs[i % 3][:, :, :], bank[2 + i % 2][:, :].rearrange("p (c q) -> p c q", c=2))\
                        .then_inc(sem("pte"), 1)

                def normalise(g):
                    b, j = g // G, g % G
                    src = bank[PVB[g % 3]][:, 256:512].rearrange("p (t h w) -> p t h w", t=2, w=32)
                    dve.wait_ge(*at(key, "ot", g + 1))
                    if g:
                        dve.wait_ge(*at(key, "att", g))
                    link(v.reciprocal(rc[:, :, :], src[:, :, :, d]))
                    if key == "a0":
                        link(v.tensor_tensor(rc[:, :, :], rc[:, :, :],
                                             qmask[:, 2 * b:2 * b + 2].unsqueeze(2).broadcast_to([128, 2, 4]), ALU.mult))
                    for t in range(2):
                        if t == 0 and b >= 2 and j == 0:
                            dve.wait_ge(*at(key, "attT", b - 1))
                        ins = v.tensor_tensor(att[b % 2][:, t, 4 * d * j:4 * d * (j + 1)].rearrange("p (h w) -> p h w", w=d),
                                              src[:, t, :, 0:d], rc[:, t, :].unsqueeze(2).broadcast_to([128, 4, d]), ALU.mult)
                    ins.then_inc(sem("att"), 1)

                def residual(b):
                    dve.wait_ge(*at(key, "out", b + 1))
                    xs = x[:, 2 * b:2 * b + 2, :]
                    ins = v.tensor_tensor(xs, xs, bank[M[0]][:, 0:256].rearrange("p (t d) -> p t d", t=2), ALU.add)
                    if key == "a3":
                        link(ins)
                        ins = v.tensor_tensor(xs, xs, row(6, 2), ALU.add)
                    ins.then_inc(sem("x"), 1)

                for i in range(n + 17):
                    if i < n:
                        dve.wait_ge(*at(key, "S", i + 1))
                        v.tensor_reduce(negmax[:, i % 4, :], bank[i % 2][:, :].rearrange("p (t k) -> p t k", t=2),
                                        AX.X, ALU.max, negate=True).then_inc(sem("nm"), 1)
                    if 2 <= i <= n + 1 and not on_act(i - 2):
                        evacuate(i - 2)
                    if i >= 11 and (i - 11) % 4 == 0 and (i - 11) // 4 < n // 4:
                        normalise((i - 11) // 4)
                    if i >= H + 12 and (i - H - 12) % H == 0 and (i - H - 12) // H < B:
                        residual((i - H - 12) // H)
                    if i == 2:
                        norm_apply(key, 1, x, xn)
                    if i == 8:
                        query_parts(key, 1)
                    if i == 2 * H + 13:
                        x_ready(dve, ffn_key, 0)
                        norm_stats(ffn_key, 0, x)
                    if i == 2 * H + 14:
                        norm_apply(ffn_key, 0, x, xn)
                    if i == 2 * H + 18:
                        split_input(ffn_key, 0)
                        router(ffn_key, 0)

            def split_input(key, hf):
                cols = slice(512 * hf, 512 * (hf + 1))
                dve.wait_ge(*at(f"{'f1n' if key == 'f1' else key}.{hf}", "nT", 1))
                link(v.tensor_copy(nH[:, cols], nT[1][:, cols]))
                v.tensor_tensor(nL[:, cols], nT[1][:, cols], nH[:, cols].bitcast(fp32), ALU.subtract).then_inc(sem("np"), 1)

            def split_weights(key, u):
                e = u % FFN[key][0]
                if u >= 2:
                    dve.wait_ge(*at(key, "up", FC * (u - 1)))
                elif key == "f1":
                    dve.wait_ge(sem("a1.o"), 2 * BH1)
                else:
                    before = ORDER[ORDER.index(key) - 1]
                    dve.wait_ge(*at(before, "pv", narrow[before]))
                dve.wait_ge(sem(f"w.slot{e}"), 32 * SLOTLOAD[key] if e < 8 else 32)
                link(v.tensor_copy(wH[u % 2][:, :], W[:, e, 0:F]))
                v.tensor_tensor(wL[u % 2][:, :], W[:, e, 0:F], wH[u % 2][:, :].bitcast(fp32), ALU.subtract).then_inc(sem("wp"), 1)

            def router(key, hf):
                nE, keep = FFN[key]
                ts = slice(4 * hf, 4 * hf + 4)
                n = [4, E]
                lgh, exh, selh, combh = lg[:, ts, :], ex[:, ts, :], sel[:, ts, :], comb[:, ts, 0:E]
                tmaxh, tsumh = tmax[:, ts], tsum[:, ts]
                ca, cb = cmp_a[:, ts], cmp_b[:, ts]
                dve.wait_ge(*at(key, "lg", hf + 1))
                src = bank[M[0]][:, 0:4 * E].rearrange("p (t e) -> p t e", e=E)
                if key in ("f0", "f3"):
                    r = int(key == "f3")
                    v.tensor_tensor(lgh, src, rb[:, r:r + 1, :].broadcast_to([128, 4, E]), ALU.add).then_inc(sem("lgc"), 1)
                else:
                    v.tensor_copy(lgh, src).then_inc(sem("lgc"), 1)
                dve.wait_ge(*at(key, "lgc", hf + 1))
                if keep == 2:
                    link(v.tensor_reduce(tmaxh, lgh, AX.X, ALU.max))
                    v.tensor_tensor(exh, lgh, tmaxh.unsqueeze(2).broadcast_to([128, 4, E]), ALU.subtract).then_inc(sem("d"), 1)
                other = lgh.unsqueeze(2).broadcast_to([128, 4, E, E])
                own = lgh.unsqueeze(3).broadcast_to([128, 4, E, E])
                v.tensor_tensor(ca, other, own, ALU.is_gt)
                link(v.tensor_tensor(cb, other, own, ALU.is_equal))
                link(v.tensor_tensor(cb, cb, lowert[:, :, :].unsqueeze(1).broadcast_to([128, 4, E, E]), ALU.mult))
                link(v.tensor_tensor(ca, ca, cb, ALU.add))
                link(v.tensor_reduce(selh, ca, AX.X, ALU.add))
                if keep == 1:
                    v.tensor_scalar(combh, selh, float(keep), None, ALU.is_lt).then_inc(sem("comb"), 1)
                    return
                link(v.tensor_scalar(selh, selh, float(keep), None, ALU.is_lt))
                dve.wait_ge(*at(key, "ex", hf + 1))
                if key == "f1":
                    link(v.tensor_reduce(tsumh, exh, AX.X, ALU.add))
                link(v.tensor_tensor(selh, selh, exh, ALU.mult))
                if key != "f1":
                    link(v.tensor_reduce(tsumh, selh, AX.X, ALU.add))
                link(v.reciprocal(tsumh, tsumh))
                v.tensor_tensor(combh, selh, tsumh.unsqueeze(2).broadcast_to([128, 4, E]), ALU.mult).then_inc(sem("comb"), 1)

            def ffn(key):
                nE, keep = FFN[key]
                nxt = AFTER.get(key)
                split_weights(key, 0)
                split_weights(key, 1)
                if key != "f1":
                    x_ready(dve, key, 1)
                    norm_stats(key, 1, x)
                    norm_apply(key, 1, x, xn)
                for u in range(2 * nE):
                    hf, e = divmod(u, nE)
                    if u + 2 < 2 * nE:
                        split_weights(key, u + 2)
                    if key == "f1" and u in (0, 1, 2, 4, 5):
                        inner_layer(1, (0, 1, 2, 4, 5).index(u))
                    if u == (6 if key == "f1" else 3):
                        split_input(key, 1)
                    if u == (7 if key == "f1" else 2):
                        router(key, 1)
                    dve.wait_ge(*at(key, "comb", hf + 1))
                    dve.wait_ge(*at(key, "down", u + 1))
                    if u:
                        dve.wait_ge(*at(key, "acc", u))
                    if e == bias_step(key, hf) + 2 and key != "f2":
                        dve.wait_ge(*at(key, "b2a", hf + 1))
                    for i in range(4):
                        t = 4 * hf + i
                        ins = v.scalar_tensor_tensor(x[:, t, :], bank[4 + u % 2][:, 128 * i:128 * (i + 1)], comb[:, t, e:e + 1],
                                                     x[:, t, :], ALU.mult, ALU.add)
                    ins.then_inc(sem("acc"), 1)
                    if e == bias_step(key, hf) + 1 and key != "f2":
                        dve.wait_ge(*at(key, "acc", u + 1))
                        dve.wait_ge(*at(key, "b2", hf + 1))
                        xs = x[:, 4 * hf:4 * hf + 4, :]
                        v.tensor_tensor(xs, xs, bank[M[1]][:, :].rearrange("p (t d) -> p t d", t=4), ALU.add)\
                            .then_inc(sem("b2a"), 1)
                    if u == KV_STEP.get(key, 99) + 1:
                        keys_parts(NEXT[key])
                    if u == KV_STEP.get(key, 99) + 2:
                        values(NEXT[key])
                    if u == nE and nxt:
                        x_ready(dve, nxt, 0)
                        norm_stats(nxt, 0, x)
                    if u == nE + 1 and nxt:
                        norm_apply(nxt, 0, x, xn)
                    if u == nE + 4 and nxt in NARROW:
                        query_parts(nxt, 0)

            def wide_attention():
                x_ready(dve, "a1", 1)
                norm_stats("a1", 1, x)
                norm_apply("a1", 1, x, xn)
                dve.wait_ge(sem("ld.pos"), 16)
                pw = PWf[:, 0:WIN]
                res = PTs[0][:, :, :].rearrange("p c q -> p (c q)")[:, 0:WIN]
                link(v.tensor_copy(PW[0][:, 0:WIN], pw))
                link(v.tensor_tensor(res, pw, PW[0][:, 0:WIN], ALU.subtract))
                link(v.tensor_copy(PW[1][:, 0:WIN], res))
                v.tensor_tensor(PW[2][:, 0:WIN], res, PW[1][:, 0:WIN], ALU.subtract).then_inc(sem("a1.pw"), 1)
                for qh in range(2):
                    for h in range(H1):
                        k = qh * H1 + h
                        dve.wait_ge(sem("a1.qf"), k + 1)
                        if h == 0 and qh:
                            dve.wait_ge(sem("a1.st"), 16)
                        qf = QF[:, k % 2, :]
                        parts = [q.rearrange("p q (b h) -> p b q h", h=H1)[:, :, :, h] for q in Q1]
                        qs = qf.rearrange("p (b q) -> p b q", b=B)
                        rs = P[0][:, :, :].rearrange("p c (b q) -> p (c b) q", q=128)
                        link(v.tensor_copy(parts[0], qs))
                        link(v.tensor_tensor(rs, qs, parts[0], ALU.subtract))
                        link(v.tensor_copy(parts[1], rs))
                        v.tensor_tensor(parts[2], rs, parts[1], ALU.subtract).then_inc(sem("a1.q"), 1)
                    for u in range(16):
                        n = qh * 16 + u
                        qb, c = divmod(u, 2)
                        dve.wait_ge(sem("a1.S"), n + 1)
                        if u == 0 and qh:
                            dve.wait_ge(sem("a1.T0"), 32)
                        v.tensor_tensor(ST[:, c, :, 16 * qb:16 * qb + 16].rearrange("p n q -> p q n"),
                                        bank[n % 4][:, :].rearrange("p (q n) -> p q n", n=BH1),
                                        m1bh[:, c:c + 1, :].broadcast_to([128, 16, BH1]), ALU.add).then_inc(sem("a1.st"), 1)

                    def head_max(i):
                        dve.wait_ge(sem("a1.T0"), i + 1)
                        v.tensor_reduce(r1[:, i % 4:i % 4 + 1], bank[i % 2][:, 0:256], AX.X, ALU.max, negate=True)\
                            .then_inc(sem("a1.nm"), 1)

                    def head_scale(i):
                        dve.wait_ge(sem("a1.e"), i + 1)
                        link(v.reciprocal(r2[:, i % 4:i % 4 + 1], r2[:, i % 4:i % 4 + 1]))
                        p = P[i % 2][:, 0, :]
                        v.tensor_scalar(p, p, r2[:, i % 4:i % 4 + 1], None, ALU.mult).then_inc(sem("a1.p"), 1)

                    def head_out(i):
                        dve.wait_ge(sem("a1.G"), i + 1)
                        if i >= 2:
                            dve.wait_ge(sem("a1.o"), i - 1)
                        v.tensor_copy(GT[i % 2], bank[4 + i % 2][:, 0:128]).then_inc(sem("a1.g"), 1)

                    i0 = qh * 32
                    for i in range(32 + 5):
                        if i < 32:
                            head_max(i0 + i)
                        if 1 <= i <= 32:
                            head_scale(i0 + i - 1)
                        if 3 <= i <= 34:
                            head_out(i0 + i - 3)
                        if i >= 11 + 1 and (i - 12) % 8 == 0 and (i - 12) // 8 < B:
                            b = (i - 12) // 8
                            dve.wait_ge(sem("a1.o"), i0 + 8 * b + 8)
                            t = 2 * b + qh
                            v.tensor_tensor(x[:, t, :], x[:, t, :], bank[6 + b % 2][:, 0:128], ALU.add).then_inc(sem("x"), 1)

            def inner_layer(hf, stage):
                ts = slice(4 * hf, 4 * hf + 4)
                if stage == 0:
                    x_ready(dve, "f1", hf)
                    norm_stats("f1", hf, x)
                elif stage == 1:
                    norm_apply("f1", hf, x, xn)
                    dve.wait_ge(*at(f"f1.{hf}", "xn", 4))
                    norm_stats("f1b", hf, xn)
                elif stage == 2:
                    norm_apply("f1b", hf, xn, xm)
                    dve.wait_ge(*at(f"f1b.{hf}", "xn", 4))
                    link(v.tensor_tensor(xm[:, ts, :], xm[:, ts, :], row(0, 4), ALU.mult))
                    v.tensor_tensor(xm[:, ts, :], xm[:, ts, :], row(1, 4), ALU.add).then_inc(sem("f1.n"), 1)
                    dve.wait_ge(sem("f1.n"), hf + 1)
                    link(v.tensor_tensor(xn[:, ts, :], xn[:, ts, :], xm[:, ts, :], ALU.add))
                    link(v.tensor_tensor(xn[:, ts, :], xn[:, ts, :], row(2, 4), ALU.add))
                elif stage == 3:
                    dve.wait_ge(sem("f1.mix"), hf + 1)
                    v.tensor_tensor(xm[:, ts, :], xn[:, ts, :], bank[M[1]][:, :].rearrange("p (t d) -> p t d", t=4), ALU.add)\
                        .then_inc(sem("f1.m"), 1)
                    dve.wait_ge(sem("f1.m"), hf + 1)
                    norm_stats("f1c", hf, xm)
                    link(v.tensor_tensor(x[:, ts, :], x[:, ts, :], xm[:, ts, :], ALU.add))
                elif stage == 4:
                    norm_apply("f1c", hf, xm, xn)
                    dve.wait_ge(*at(f"f1c.{hf}", "xn", 4))
                    link(v.tensor_tensor(xn[:, ts, :], xn[:, ts, :], row(3, 4), ALU.mult))
                    v.tensor_tensor(xn[:, ts, :], xn[:, ts, :], row(4, 4), ALU.add).then_inc(sem("f1.n2"), 1)

            for key in ORDER:
                if key in NARROW:
                    attention(key)
                elif key == "a1":
                    wide_attention()
                else:
                    if key == "f1":
                        for stage in range(5):
                            inner_layer(0, stage)
                        split_input(key, 0)
                        router(key, 0)
                    ffn(key)

        @block.scalar
        def _(act):
            a = nc.scalar

            def copy_T(key, hf, dst):
                act.wait_ge(*at(f"{key}.{hf}", "tr", 1))
                a.activation(dst[:, 512 * hf:512 * (hf + 1)], bank[M[hf if key == "ctx" else 0]][:, :], ACT.Copy).then_inc(sem("nT"), 1)

            def queries(key, hf):
                scale = NARROW[key][2]
                act.wait_ge(*at(key, "q", hf + 1))
                qt = QT[:, 512 * hf:512 * (hf + 1)]
                if key == "a3":
                    ins = a.activation(qt, bank[M[1 - hf]][:, :], ACT.Identity, bias=qkb[:, 0:1])
                else:
                    ins = a.activation(qt, bank[M[1 - hf]][:, :], ACT.Copy, scale=scale)
                ins.then_inc(sem("qt"), 1)

            def router(key, hf):
                if FFN[key][1] == 2:
                    act.wait_ge(*at(key, "d", hf + 1))
                    exh = ex[:, 4 * hf:4 * hf + 4, :]
                    a.activation(exh, exh, ACT.Exp).then_inc(sem("ex"), 1)

            copy_T("ctx", 0, cT)
            copy_T("ctx", 1, cT)
            act.wait_ge(sem("ld.small"), SMALL)

            def project(key):
                for c in range(2):
                    act.wait_ge(*at(key, "k", c + 1))
                    kt = KT[:, 512 * c:512 * (c + 1)]
                    if key == "a3":
                        ins = a.activation(kt, bank[M[c]][:, :], ACT.Identity, bias=qkb[:, 1:2])
                    else:
                        ins = a.activation(kt, bank[M[c]][:, :], ACT.Copy)
                    ins.then_inc(sem("kt"), 1)

            def attention(key):
                H, d, scale = NARROW[key]
                n = B * H
                if key == "a0":
                    project(key)
                    copy_T(key, 0, nT[0])
                    queries(key, 0)
                ffn_key = AFTER[key]
                for i in range(n + 17):
                    if i < n:
                        act.wait_ge(*at(key, "nm", i + 1))
                        if i >= 2:
                            act.wait_ge(*at(key, "T", i - 1))
                        for t in range(2):
                            ins = a.activation(P[i % 2][:, t, :], bank[i % 2][:, 256 * t:256 * (t + 1)], ACT.Exp,
                                               bias=negmax[:, i % 4, t:t + 1])
                        ins.then_inc(sem("e"), 1)
                    if 2 <= i <= n + 1 and on_act(i - 2):
                        act.wait_ge(*at(key, "T", i - 1))
                        if i >= 5:
                            act.wait_ge(*at(key, "pv", i - 4))
                        a.activation(PTs[(i - 2) % 3][:, :, :], bank[2 + i % 2][:, :].rearrange("p (c q) -> p c q", c=2), ACT.Copy)\
                            .then_inc(sem("pta"), 1)
                    if i >= 8 and (i - 8) % 4 == 0 and (i - 8) // 4 < n // 4:
                        g = (i - 8) // 4
                        act.wait_ge(*at(key, "pv", 4 * g + 4))
                        if g >= 2:
                            act.wait_ge(*at(key, "ot", g - 1))
                        a.activation(Os[g % 2][:, :], bank[PVB[g % 3]][:, 0:256], ACT.Copy).then_inc(sem("oe"), 1)
                    if i >= H + 10 and (i - H - 10) % H == 0 and (i - H - 10) // H < B:
                        b = (i - H - 10) // H
                        act.wait_ge(*at(key, "attT", b + 1))
                        if b >= 2:
                            act.wait_ge(*at(key, "out", b - 1))
                        a.activation(attT[b % 2][:, :], bank[6][:, 0:256], ACT.Copy).then_inc(sem("ate"), 1)
                    if i == 5:
                        copy_T(key, 1, nT[0])
                    if i == 7:
                        queries(key, 1)
                    if i == 2 * H + 17:
                        copy_T(ffn_key, 0, nT[1])
                    if i == 2 * H + 18:
                        router(ffn_key, 0)

            def ffn(key, nTk):
                nE, keep = FFN[key]
                bi = {"f0": 0, "f1": 1, "f3": 2}.get(key)
                func = {"f0": ACT.Gelu_apprx_tanh, "f1": ACT.Silu, "f2": ACT.Relu, "f3": ACT.Gelu}[key]
                nxt = AFTER.get(key)
                for u in range(2 * nE):
                    hf, e = divmod(u, nE)
                    for c in range(FC):
                        act.wait_ge(*at(key, "up", FC * u + c + 1))
                        if c == 0 and u >= 2:
                            act.wait_ge(*at(key, "down", u - 1))
                        dst = hid[u % 2][:, c, :]
                        if bi is None:
                            ins = a.activation(dst, bank[c][:, :], func)
                        else:
                            ins = a.activation(dst, bank[c][:, :], func, bias=b1[:, bi, FC * e + c:FC * e + c + 1])
                        ins.then_inc(sem("h"), 1)
                    if key == "f1":
                        if u == 3:
                            copy_T("f1", 1, nT[0])
                        if u == 6:
                            copy_T("f1n", 1, nT[1])
                    elif u == 2:
                        copy_T(key, 1, nT[1])
                    if u == (7 if key == "f1" else 3):
                        router(key, 1)
                    if e == bias_step(key, hf) + 1 and key != "f2":
                        act.wait_ge(*at(key, "cT", hf + 1))
                        a.activation(combT[0:nE, 512 * hf:512 * (hf + 1)], bank[M[1]][0:nE, :], ACT.Copy)\
                            .then_inc(sem("cTe"), 1)
                    if u == KV_STEP.get(key, 99) + 1:
                        project(NEXT[key])
                    if u == nE + 3 and nxt:
                        copy_T(nxt, 0, nT[0])
                    if u == nE + 4 and nxt in NARROW:
                        queries(nxt, 0)

            def wide_attention():
                scale = float(D) ** -0.5
                for i in range(4):
                    act.wait_ge(sem("a1.pre"), i + 1)
                    dst = (AQK, CVO)[i // 2][:, 4 * (i % 2):4 * (i % 2) + 4, :]
                    a.activation(dst, bank[M[i % 2]][:, :].rearrange("p (h m) -> p h m", h=4), ACT.Copy).then_inc(sem("a1.w"), 1)
                act.wait_ge(sem("a1.pre"), 5)
                a.activation(bst[:, 0, :], bank[5][:, 0:H1], ACT.Copy, scale=scale).then_inc(sem("a1.w"), 1)
                act.wait_ge(sem("a1.w"), 5)
                act.wait_ge(sem("c.masks"), 1)
                copy_T("a1", 1, nT[0])
                for qh in range(2):
                    for h in range(H1):
                        k = qh * H1 + h
                        act.wait_ge(sem("a1.t"), 2 * k + 1)
                        if h == 0 and qh:
                            act.wait_ge(sem("a1.S"), 16)
                        a.activation(T1.rearrange("p q (b h) -> p b q h", h=H1)[:, :, :, h],
                                     bank[4 + 2 * (k % 2)][:, :].rearrange("p (b q) -> p b q", b=B), ACT.Identity,
                                     bias=bst[:, 0, h:h + 1], scale=scale).then_inc(sem("a1.te"), 1)
                        act.wait_ge(sem("a1.t"), 2 * k + 2)
                        if k >= 2:
                            act.wait_ge(sem("a1.q"), k - 1)
                        a.activation(QF[:, k % 2, :], bank[5 + 2 * (k % 2)][:, :], ACT.Identity,
                                     bias=bst[:, 1, h:h + 1], scale=scale).then_inc(sem("a1.qf"), 1)
                    i0 = qh * 32
                    for j in range(33):
                        i = i0 + j
                        if j < 32:
                            act.wait_ge(sem("a1.nm"), i + 1)
                            if i >= 2:
                                act.wait_ge(sem("a1.T1"), i - 1)
                            elif i == 0:
                                act.wait_ge(sem("a1.q"), 8)
                            a.activation(P[i % 2][:, 0, :], bank[i % 2][:, 0:256], ACT.Exp, bias=r1[:, i % 4:i % 4 + 1],
                                         accum_out=r2[:, i % 4:i % 4 + 1]).then_inc(sem("a1.e"), 1)
                        if j >= 1:
                            k = i - 1
                            act.wait_ge(sem("a1.T1"), k + 1)
                            if k >= 2:
                                act.wait_ge(sem("a1.G"), k - 1)
                            a.activation(PTs[k % 2][:, 0, :], bank[2 + k % 2][:, 0:256], ACT.Copy).then_inc(sem("a1.pte"), 1)

            for key in ORDER:
                if key in NARROW:
                    attention(key)
                elif key == "a1":
                    wide_attention()
                else:
                    if key == "f1":
                        copy_T("f1", 0, nT[0])
                        copy_T("f1n", 0, nT[1])
                        router(key, 0)
                    ffn(key, nT[1])

        @block.tensor
        def _(pe):
            mm, tr = nc.tensor.matmul, nc.tensor.transpose
            reader = {}

            def take(k):
                if k in reader:
                    pe.wait_ge(*reader.pop(k))
                return bank[k]

            def turn(key, hf, src, ready):
                k = M[hf if key == "ctx" else 0]
                dst = take(k)
                for i in range(4):
                    t = 4 * hf + i
                    pe.wait_ge(*ready(t))
                    ins = tr(dst[:, 128 * i:128 * (i + 1)], src[:, t, :], ident[:, :])
                ins.then_inc(sem("tr"), 1)
                reader[k] = at(f"{key}.{hf}", "nT", 1)

            def turn_norm(key, hf):
                turn(key, hf, xn, lambda t: at(f"{key}.{hf}", "xn", t - 4 * hf + 1))

            def queries(key, hf):
                pe.wait_ge(*at(f"{key}.{hf}", "nT", 1))
                dst = take(M[1 - hf])
                mm(dst[:, :], aw[:, 4 * LAYER_OF[key], :], nT[0][:, 512 * hf:512 * (hf + 1)], start=True, stop=True).then_inc(sem("q"), 1)
                reader[M[1 - hf]] = at(key, "qt", hf + 1)

            def logits(key, hf):
                nTk = nT[1]
                pe.wait_ge(sem("ld.small"), SMALL)
                pe.wait_ge(*at(f"{'f1n' if key == 'f1' else key}.{hf}", "nT", 1))
                dst = take(M[0])
                for i in range(4):
                    t = 4 * hf + i
                    ins = mm(dst[:, E * i:E * (i + 1)], nTk[:, 128 * t:128 * (t + 1)], rw[:, int(key[1]), :], start=True, stop=True)
                ins.then_inc(sem("lg"), 1)
                reader[M[0]] = at(key, "lgc", hf + 1)

            pe.wait_ge(sem("c.ident"), 1)
            turn("ctx", 0, cx, lambda t: (sem("ld.ctx"), 16))
            turn("ctx", 1, cx, lambda t: (sem("ld.ctx"), 16))
            pe.wait_ge(sem("ld.aw"), 16)
            pe.wait_ge(*at("ctx.1", "nT", 1))

            def keys(key):
                w = 4 * LAYER_OF[key]
                for c in range(2):
                    dst = take(M[c])
                    mm(dst[:, :], aw[:, w + 1, :], cT[:, 512 * c:512 * (c + 1)], start=True, stop=True).then_inc(sem("k"), 1)
                    reader[M[c]] = at(key, "kt", c + 1)

            def values(key):
                w = 4 * LAYER_OF[key]
                for c in range(2):
                    dst = take(M[c])
                    for i in range(4):
                        t = 4 * c + i
                        ins = mm(dst[:, 128 * i:128 * (i + 1)], cT[:, 128 * t:128 * (t + 1)], aw[:, w + 2, :], start=True, stop=True)
                    ins.then_inc(sem("v"), 1)
                    reader[M[c]] = at(key, "va", c + 1)

            def attention(key):
                H, d, _ = NARROW[key]
                G = H // 4
                n = B * H
                w = 4 * LAYER_OF[key]
                R = ROWS[key]
                if key == "a0":
                    keys(key)
                    values(key)
                    turn_norm(key, 0)
                    queries(key, 0)
                ffn_key = AFTER[key]
                pe.wait_ge(sem("st.k"), 16 * len(PAIRS) * (LAYER_OF[key] + 1))
                pe.wait_ge(sem("c.masks"), 1)

                def scores(i):
                    b, h = divmod(i, H)
                    if h == 0 and b % 2 == 0:
                        pe.wait_ge(sem(f"st.q{b // 2}"), 16 * len(PAIRS) * (LAYER_OF[key] + 1))
                    dst = take(i % 2)
                    for t in range(2):
                        o = dst[:, 256 * t:256 * (t + 1)]
                        ins = mm(o, Qs[0:R, h, S * b + 128 * t:S * b + 128 * (t + 1)], Ks[0:R, h, S * b:S * (b + 1)],
                                 start=True, stop=key != "a2")
                        if key == "a2":
                            ins = mm(o, identb[:, :], madd2[:, t, :], start=False, stop=True)
                    ins.then_inc(sem("S"), 1)
                    reader[i % 2] = at(key, "e", i + 1)

                def transpose_p(i):
                    pe.wait_ge(*at(key, "e", i + 1))
                    dst = take(2 + i % 2)
                    for c in range(2):
                        for t in range(2):
                            ins = tr(dst[:, 256 * c + 128 * t:256 * c + 128 * (t + 1)], P[i % 2][:, t, 128 * c:128 * (c + 1)], ident[:, :])
                    ins.then_inc(sem("T"), 1)
                    reader[2 + i % 2] = probs_in_sbuf(key, i)

                def probs_v(i):
                    b, h = divmod(i, H)
                    g, j = divmod(i, 4)
                    pe.wait_ge(*probs_in_sbuf(key, i))
                    if i == 0:
                        pe.wait_ge(*at(key, "va", 2))
                    dst = take(PVB[g % 3]) if j == 0 else bank[PVB[g % 3]]
                    for c in range(2):
                        ins = mm(dst[32 * j:32 * (j + 1), 0:256], Va[:, 2 * b + c, h, :], PTs[i % 3][:, c, :],
                                 start=c == 0, stop=c == 1)
                    ins.then_inc(sem("pv"), 1)

                def token_major(g):
                    pe.wait_ge(*at(key, "oe", g + 1))
                    for t in range(2):
                        ins = tr(bank[PVB[g % 3]][:, 256 + 128 * t:384 + 128 * t], Os[g % 2][:, 128 * t:128 * (t + 1)], ident[:, :])
                    ins.then_inc(sem("ot"), 1)
                    reader[PVB[g % 3]] = at(key, "att", g + 1)

                def out_transpose(b):
                    pe.wait_ge(*at(key, "att", G * (b + 1)))
                    dst = take(M[0])
                    for t in range(2):
                        ins = tr(dst[:, 128 * t:128 * (t + 1)], att[b % 2][:, t, :], ident[:, :])
                    ins.then_inc(sem("attT"), 1)
                    reader[M[0]] = at(key, "ate", b + 1)

                def out_project(b):
                    pe.wait_ge(*at(key, "ate", b + 1))
                    dst = take(M[0])
                    for t in range(2):
                        ins = mm(dst[:, 128 * t:128 * (t + 1)], attT[b % 2][:, 128 * t:128 * (t + 1)], aw[:, w + 3, :], start=True, stop=True)
                    ins.then_inc(sem("out"), 1)
                    reader[M[0]] = at(key, "x", b + 1)

                for i in range(n + 17):
                    if i < n:
                        scores(i)
                    if 2 <= i <= n + 1:
                        transpose_p(i - 2)
                    if 4 <= i <= n + 3:
                        probs_v(i - 4)
                    if i >= 10 and (i - 10) % 4 == 0 and (i - 10) // 4 < n // 4:
                        token_major((i - 10) // 4)
                    if i >= H + 9 and (i - H - 9) % H == 0 and (i - H - 9) // H < B:
                        out_transpose((i - H - 9) // H)
                    if i >= H + 11 and (i - H - 11) % H == 0 and (i - H - 11) // H < B:
                        out_project((i - H - 11) // H)
                    if i == 5:
                        turn_norm(key, 1)
                    if i == 7:
                        queries(key, 1)
                    if i == 2 * H + 16:
                        turn_norm(ffn_key, 0)
                    if i == 2 * H + 18:
                        logits(ffn_key, 0)

            def ffn(key, nTk):
                nE, keep = FFN[key]
                nxt = AFTER.get(key)

                def up(u):
                    hf, e = divmod(u, nE)
                    if e == 0:
                        pe.wait_ge(*at(key, "np", hf + 1))
                    pe.wait_ge(*at(key, "wp", u + 1))
                    for c in range(FC):
                        dst = take(c)
                        for n, (w, act_in) in enumerate(((wH, nH), (wH, nL), (wL, nH))):
                            ins = mm(dst[:, :], w[u % 2][:, 128 * c:128 * (c + 1)], act_in[:, 512 * hf:512 * (hf + 1)],
                                     start=n == 0, stop=n == 2)
                        ins.then_inc(sem("up"), 1)
                        reader[c] = at(key, "h", FC * u + c + 1)

                def down(u):
                    e = u % nE
                    if u < nE:
                        pe.wait_ge(sem(f"w.slot{e}"), 32 * SLOTLOAD[key] if e < 8 else 32)
                    pe.wait_ge(*at(key, "h", FC * (u + 1)))
                    dst = take(4 + u % 2)
                    for i in range(4):
                        for c in range(FC):
                            ins = mm(dst[:, 128 * i:128 * (i + 1)], hid[u % 2][:, c, 128 * i:128 * (i + 1)],
                                     W[:, e, F + 128 * c:F + 128 * (c + 1)], start=c == 0, stop=c == FC - 1)
                    ins.then_inc(sem("down"), 1)
                    reader[4 + u % 2] = at(key, "acc", u + 1)

                def weights_turned(hf):
                    pe.wait_ge(*at(key, "comb", hf + 1))
                    dst = take(M[1])
                    for i in range(4):
                        ins = tr(dst[0:nE, 128 * i:128 * (i + 1)], comb[:, 4 * hf + i, 0:nE], ident[:, :])
                    ins.then_inc(sem("cT"), 1)
                    reader[M[1]] = at(key, "cTe", hf + 1)

                def biases(hf):
                    dst = take(M[1])
                    for i in range(4):
                        t = 4 * hf + i
                        ins = mm(dst[:, 128 * i:128 * (i + 1)], combT[0:nE, 128 * t:128 * (t + 1)],
                                 b2[0:nE, {"f0": 0, "f1": 1, "f3": 2}[key], :], start=True, stop=True)
                    ins.then_inc(sem("b2"), 1)
                    reader[M[1]] = at(key, "b2a", hf + 1)

                up(0)
                for u in range(2 * nE):
                    hf, e = divmod(u, nE)
                    if u + 1 < 2 * nE:
                        up(u + 1)
                    down(u)
                    if key == "f1" and u in (2, 3, 5):
                        inner_layer(1, (2, 3, 5).index(u))
                    if key != "f1" and u == 1:
                        turn_norm(key, 1)
                    if u == (6 if key == "f1" else 2):
                        logits(key, 1)
                    if e == bias_step(key, hf) and key != "f2":
                        weights_turned(hf)
                    if e == bias_step(key, hf) + 1 and key != "f2":
                        biases(hf)
                    if u == KV_STEP.get(key, 99):
                        keys(NEXT[key])
                    if u == KV_STEP.get(key, 99) + 1:
                        values(NEXT[key])
                    if u == nE + 2 and nxt:
                        turn_norm(nxt, 0)
                    if u == nE + 3 and nxt in NARROW:
                        queries(nxt, 0)

            def inner_layer(hf, stage):
                if stage == 0:
                    turn("f1", hf, xm, lambda t: (sem("f1.n"), hf + 1))
                elif stage == 1:
                    pe.wait_ge(*at(f"f1.{hf}", "nT", 1))
                    dst = take(M[1])
                    for i in range(4):
                        t = 4 * hf + i
                        ins = mm(dst[:, 128 * i:128 * (i + 1)], nT[0][:, 128 * t:128 * (t + 1)], mixw[:, :], start=True, stop=True)
                    ins.then_inc(sem("f1.mix"), 1)
                    reader[M[1]] = (sem("f1.m"), hf + 1)
                else:
                    turn("f1n", hf, xn, lambda t: (sem("f1.n2"), hf + 1))

            def wide_attention():
                pe.wait_ge(sem("ld.wide"), 16 * 5)
                for i in range(4):
                    dst = take(M[i % 2])
                    l, r = ((WQT, WKT), (WVT, WO))[i // 2]
                    for j in range(4):
                        h = 4 * (i % 2) + j
                        ins = mm(dst[:, 128 * j:128 * (j + 1)], l[:, h, :], r[:, h, :], start=True, stop=True)
                    ins.then_inc(sem("a1.pre"), 1)
                    reader[M[i % 2]] = (sem("a1.w"), i + 1)
                dst = take(5)
                for h in range(H1):
                    ins = mm(dst[:, h:h + 1], WKT[:, h, :], bub[:, 0, h:h + 1], start=True, stop=True)
                ins.then_inc(sem("a1.pre"), 1)
                reader[5] = (sem("a1.w"), 5)
                pe.wait_ge(sem("a1.w"), 5)
                turn_norm("a1", 1)
                pe.wait_ge(*at("a1.1", "nT", 1))
                xq = nT[0][:, :].rearrange("p (b s q) -> p b s q", b=B, s=2)
                for qh in range(2):
                    for h in range(H1):
                        k = qh * H1 + h
                        for j, wt in ((0, AQK), (1, WQ)):
                            kb = 4 + 2 * (k % 2) + j
                            dst = take(kb)
                            mm(dst[:, :].rearrange("p (b q) -> p b q", b=B), wt[:, h, :], xq[:, :, qh, :], start=True, stop=True)\
                                .then_inc(sem("a1.t"), 1)
                            reader[kb] = (sem("a1.qf" if j else "a1.te"), k + 1)
                    pe.wait_ge(sem("a1.te"), 8 * (qh + 1))
                    pe.wait_ge(sem("a1.q"), 8 * (qh + 1))
                    pe.wait_ge(sem("a1.pw"), 1)
                    for u in range(16):
                        n = qh * 16 + u
                        qb, c = divmod(u, 2)
                        dst = take(n % 4)[:, :].rearrange("p (q n) -> p q n", n=BH1)
                        for b in range(B):
                            mm(dst[:, :, H1 * b:H1 * (b + 1)], cT[:, S * b + 128 * c:S * b + 128 * (c + 1)],
                               T1[:, 16 * qb:16 * qb + 16, H1 * b:H1 * (b + 1)], start=b == 0, stop=False, skip_group_check=True)
                        for qi in range(16):
                            off = S - 1 - (128 * qh + 16 * qb + qi) + 128 * c
                            for pj, qj in ((0, 0), (0, 1), (0, 2), (1, 0), (1, 1), (2, 0)):
                                ins = mm(dst[:, qi, :], PW[pj][:, off:off + 128], Q1[qj][:, 16 * qb + qi, :],
                                         start=False, stop=qi == 15 and pj == 2, skip_group_check=True)
                        ins.then_inc(sem("a1.S"), 1)
                        reader[n % 4] = (sem("a1.st"), n + 1)
                    pe.wait_ge(sem("a1.st"), 16 * (qh + 1))

                    def scores_q(i, j):
                        b, h = divmod(j, H1)
                        dst = take(i % 2)
                        for c in range(2):
                            ins = tr(dst[:, 128 * c:128 * (c + 1)], ST[:, c, j, :], ident[:, :])
                        ins.then_inc(sem("a1.T0"), 1)
                        reader[i % 2] = (sem("a1.e"), i + 1)

                    def probs_t(i, j):
                        pe.wait_ge(sem("a1.p"), i + 1)
                        dst = take(2 + i % 2)
                        for c in range(2):
                            ins = tr(dst[:, 128 * c:128 * (c + 1)], P[i % 2][:, 0, 128 * c:128 * (c + 1)], ident[:, :])
                        ins.then_inc(sem("a1.T1"), 1)
                        reader[2 + i % 2] = (sem("a1.pte"), i + 1)

                    def probs_ctx(i, j):
                        b = j // H1
                        pe.wait_ge(sem("a1.pte"), i + 1)
                        dst = take(4 + i % 2)
                        for c in range(2):
                            ins = mm(dst[:, 0:128], cx[:, 2 * b + c, :], PTs[i % 2][:, 0, 128 * c:128 * (c + 1)], start=c == 0, stop=c == 1)
                        ins.then_inc(sem("a1.G"), 1)
                        reader[4 + i % 2] = (sem("a1.g"), i + 1)

                    def out_head(i, j):
                        b, h = divmod(j, H1)
                        pe.wait_ge(sem("a1.g"), i + 1)
                        dst = take(6 + b % 2) if h == 0 else bank[6 + b % 2]
                        mm(dst[:, 0:128], GT[i % 2], CVO[:, h, :], start=h == 0, stop=h == H1 - 1).then_inc(sem("a1.o"), 1)
                        if h == H1 - 1:
                            reader[6 + b % 2] = at("a1", "x", B * qh + b + 1)

                    i0 = qh * 32
                    for j in range(32 + 4):
                        if j < 32:
                            scores_q(i0 + j, j)
                        if 2 <= j <= 33:
                            probs_t(i0 + j - 2, j - 2)
                        if 3 <= j <= 34:
                            probs_ctx(i0 + j - 3, j - 3)
                        if 4 <= j <= 35:
                            out_head(i0 + j - 4, j - 4)

            for key in ORDER:
                if key in NARROW:
                    attention(key)
                elif key == "a1":
                    wide_attention()
                else:
                    if key == "f1":
                        for stage in range(3):
                            inner_layer(0, stage)
                        logits(key, 0)
                    ffn(key, nT[1])


def kernel(**inputs):
    import numpy as np
    import concourse.bacc as bacc
    from concourse.bass_utils import run_bass_kernel_spmd

    g = {k: np.asarray(v) for k, v in inputs.items()}
    T = lambda a, *p: np.ascontiguousarray(np.transpose(a, p or None))
    row = np.arange(WIN) - (S - 1) + POS // 2
    row = np.clip(np.where(row < 0, row + POS, row), 0, POS - 1)
    cols = lambda a: np.ascontiguousarray(a.reshape(-1, 128).T)
    aw = []
    for n in ("L0_xattn_W_", "L2_xattn_w_", "L3_xattn_W"):
        aw += [T(g[n + s]) for s in "qkvo"]
    a = {
        "x": g["x"].reshape(TOK, D), "ctx": g["ctx_1024"].reshape(TOK, D), "lens": g["_lenS2"],
        "mask1": np.ascontiguousarray(g["mask_BxS2_bf1"].reshape(2 * B, 128).T).view(np.uint8),
        "mask2": g["mask_1x1xSxS2_if1"].reshape(S, S),
        "aw": np.stack(aw),
        "qkb": T(np.stack([g["L3_xattn_bq"], g["L3_xattn_bk"]])),
        "rows": np.stack([g["L1_ffn_g1"], g["L1_ffn_be1"], g["L1_ffn_mix_b"], g["L1_ffn_g2"], g["L1_ffn_be2"],
                          g["L3_xattn_bv"], g["L3_xattn_bo"]]),
        "rb": np.stack([g["L0_ffn_router_b"], g["L3_ffn_br"]]),
        "rw": np.stack([T(g["L0_ffn_router_w"]), g["L1_ffn_router_w"], g["L2_ffn_Wr"], g["L3_ffn_wr"]]),
        "mixw": g["L1_ffn_mix_w"],
        "bu": g["L1_xattn_bu"], "bv": g["L1_xattn_bv"],
        "a1.wqT": T(g["L1_xattn_wq"], 1, 2, 0), "a1.wkT": T(g["L1_xattn_wk"], 1, 2, 0),
        "a1.wvT": T(g["L1_xattn_wv"], 1, 2, 0), "a1.wo": g["L1_xattn_wo"], "a1.wq": T(g["L1_xattn_wq"], 0, 2, 1),
        "a1.pos": T(g["L1_xattn_pos_w"][row]),
        "f0.w1": np.concatenate([T(g["L0_ffn_spec_w1"], 0, 2, 1), T(g["L0_ffn_shared_w1"])[None]]),
        "f0.w2": np.concatenate([T(g["L0_ffn_spec_w2"], 0, 2, 1), T(g["L0_ffn_shared_w2"])[None]]),
        "f0.b1": cols(np.concatenate([g["L0_ffn_spec_b1"], g["L0_ffn_shared_b1"][None]])),
        "f0.b2": np.concatenate([g["L0_ffn_spec_b2"], g["L0_ffn_shared_b2"][None]]),
        "f1.w1": g["L1_ffn_w1"], "f1.w2": g["L1_ffn_w2"], "f1.b1": cols(g["L1_ffn_b1"]), "f1.b2": g["L1_ffn_b2"],
        "f2.w1": g["L2_ffn_W1"], "f2.w2": g["L2_ffn_W2"],
        "f3.w1": g["L3_ffn_w1"], "f3.w2": g["L3_ffn_w2"], "f3.b1": cols(g["L3_ffn_b1"]), "f3.b2": g["L3_ffn_b2"],
    }
    nc = bacc.Bacc("TRN2", target_bir_lowering=False, num_devices=1)
    arrays, handles = {}, {}
    for name, v in a.items():
        dram = "in_" + name.replace(".", "_")
        arrays[dram] = np.ascontiguousarray(v)
        handles[name] = nc.dram_tensor(dram, v.shape, mybir.dt.from_np(v.dtype), kind="ExternalInput").ap()
    o = nc.dram_tensor("out_x", (TOK, D), mybir.dt.float32, kind="ExternalOutput").ap()
    build(nc, handles, o)
    r = run_bass_kernel_spmd(nc, [arrays], core_ids=[0])
    return r.results[0]["out_x"].reshape(B, S, D)
```

```python
import concourse.bass as bass
from concourse import mybir
from contextlib import ExitStack

B, S, D = 4, 256, 128
TOK = B * S
NT = TOK // 128
F, E = 512, 8
FC = F // 128
H1 = 8
BH1 = B * H1
POS = 128
WIN = 2 * S - 1
LN_EPS = 1e-5
BIG_NEG = -float(2 ** 30)
L0_NEG = -float(2 ** 32)
L1_NEG = -3.0e38

NARROW = {"a0": (8, 16, 0.25), "a2": (16, 8, float(8 ** -0.5)), "a3": (16, 8, 1.0)}
LAYER_OF = {"a0": 0, "a2": 1, "a3": 2}
PAIRS = ((0, 0), (0, 1), (1, 0), (1, 1), (0, 2), (2, 0))
MASK_ROW = 96
ROWS = {"a0": 128, "a2": 96, "a3": 96}
FFN = {"f0": (9, 2), "f1": (8, 2), "f2": (8, 2), "f3": (8, 1)}


def build(nc, A, out):
    fp32, bf16, i32, u8 = mybir.dt.float32, mybir.dt.bfloat16, mybir.dt.int32, mybir.dt.uint8
    fp32r = mybir.dt.float32r
    ALU, ACT, AX = mybir.AluOpType, mybir.ActivationFunctionType, mybir.AxisListType
    ctx = ExitStack()
    with ctx:
        def sb(name, shape, dt=fp32):
            return ctx.enter_context(nc.sbuf_tensor(name, shape, dt))

        made = {}

        def sem(name):
            if name not in made:
                made[name] = ctx.enter_context(nc.semaphore(name.replace(".", "_")))
            return made[name]

        def on_act(i):
            return i % 8 in (1, 3, 6)

        def act_evacuations(n):
            return sum(on_act(i) for i in range(n))

        narrow = {k: B * h for k, (h, _, _) in NARROW.items()}
        COUNTS = {n: [("a0", c("a0")), ("a2", c("a2")), ("a3", c("a3"))] for n, c in {
            **dict.fromkeys(("k", "kt", "v", "va", "q", "qt", "qp"), lambda k: 2), "kp": lambda k: 1,
            **dict.fromkeys(("S", "nm", "e", "T", "pv"), lambda k: narrow[k]),
            "pte": lambda k: narrow[k] - act_evacuations(narrow[k]), "pta": lambda k: act_evacuations(narrow[k]),
            **dict.fromkeys(("oe", "ot", "att"), lambda k: narrow[k] // 4),
            **dict.fromkeys(("attT", "ate", "out"), lambda k: B)}.items()}
        COUNTS |= {n: [(k, c(k)) for k in ("f0", "f1", "f2", "f3")] for n, c in {
            **dict.fromkeys(("lg", "lgc", "comb"), lambda k: 2), **dict.fromkeys(("d", "ex"), lambda k: 2 * int(FFN[k][1] == 2)),
            **dict.fromkeys(("up", "h"), lambda k: 2 * FC * FFN[k][0]), **dict.fromkeys(("down", "acc", "wp"), lambda k: 2 * FFN[k][0]), "np": lambda k: 2,
            **dict.fromkeys(("cT", "cTe", "b2", "b2a"), lambda k: 0 if k == "f2" else 2)}.items()}
        halves = lambda keys: [f"{k}.{hf}" for k in keys for hf in range(2)]
        inner = lambda keys: [f"{k}.{hf}" for hf in range(2) for k in keys]
        norms = halves(("a0", "f0", "a1")) + inner(("f1", "f1b", "f1c")) + halves(("a2", "f2", "a3", "f3"))
        COUNTS |= {"mv": [(k, 1) for k in norms], "rstd": [(k, 1) for k in norms], "xn": [(k, 4) for k in norms]}
        turns = halves(("ctx", "a0", "f0", "a1")) + inner(("f1", "f1n")) + halves(("a2", "f2", "a3", "f3"))
        COUNTS |= {n: [(k, 1) for k in turns] for n in ("tr", "nT")}
        COUNTS["x"] = [("a0", B), ("a1", NT), ("a2", B), ("a3", B)]

        def at(key, name, v):
            base = 0
            for k, total in COUNTS[name]:
                if k == key:
                    assert 0 < v <= total, (key, name, v)
                    return sem(name), base + v
                base += total
            raise KeyError(key)

        def probs_in_sbuf(key, i):
            n = act_evacuations(i + 1)
            return at(key, "pta", n) if on_act(i) else at(key, "pte", i + 1 - n)

        arena = -(-nc.sbuf_base // 32) * 32
        sb("arena", [128, 4096])

        def place(name, at_byte, shape, dt=fp32):
            return nc.alloc_sbuf_tensor_at(name, shape, dt, offset=arena + at_byte)

        x = sb("x_res", [128, NT, D])
        xn = place("xn", 0, [128, NT, D])
        xm = sb("xm", [128, NT, D])
        nT = [place("nT0", 4096, [128, TOK]), sb("nT1", [128, TOK])]
        cx = sb("cx", [128, NT, D])
        cT = sb("cT", [128, TOK])
        W = sb("W", [128, 9, 2 * F])
        aw = sb("aw", [128, 12, D])
        big = sb("big", [128, 18432])
        late = sb("late", [128, 8192])
        P = [place(f"P{i}", 8192 + 2048 * i, [128, 2, S]) for i in range(2)]
        PTs = [place(f"PTs{i}", 12288 + 2048 * i, [128, 2, S]) for i in range(2)]
        ident = sb("ident", [128, 128])
        identb = sb("identb", [128, 128], bf16)
        lowert = sb("lowert", [128, E, E])
        half = sb("half", [128, NT])
        stats = sb("stats", [128, NT, 6])
        mv = sb("mv", [128, NT, 2])
        rstd = sb("rstd", [128, NT])
        negmax = sb("negmax", [128, 4, 2])
        QT = sb("QT", [128, TOK])
        KT = sb("KT", [128, TOK])
        Os = [sb("Os0", [128, S]), sb("Os1", [128, S])]
        att = [sb("att0", [128, 2, D]), sb("att1", [128, 2, D])]
        attT = [sb("attT0", [128, S]), sb("attT1", [128, S])]
        rc = sb("rc", [128, 2, 4])
        madd2 = sb("madd2", [128, 2, S], bf16)
        leni = sb("leni", [128, B], i32)
        lenf = sb("lenf", [128, B])
        qpos = sb("qpos", [128, NT])
        qmask = sb("qmask", [128, NT])
        m1u = sb("m1u", [128, 2 * B], u8)
        m1f = sb("m1f", [128, 2 * B])
        qkb = sb("qkb", [128, 2])
        rows = sb("rows", [128, 7, D])
        rb = sb("rb", [128, 2, E])
        rw = sb("rw", [128, 4, E])
        b1 = sb("b1", [128, 3, 9 * FC])
        b2 = sb("b2", [9, 3, D])
        mixw = sb("mixw", [128, D])
        lg = sb("lg", [128, NT, E])
        sel = sb("sel", [128, NT, E])
        ex = sb("ex", [128, NT, E])
        tmax = sb("tmax", [128, NT])
        tsum = sb("tsum", [128, NT])
        comb = sb("comb", [128, NT, 9])
        bub = sb("bub", [128, 2, H1])
        bst = sb("bst", [128, 2, H1])
        r1 = sb("r1", [128, 4])
        r2 = sb("r2", [128, 4])

        warm = sb("warm", [128, 8])

        keyrow = big[:, 17920:18176]
        combT = KT[0:9, :]
        m2i = xm[:, 0:4, :].rearrange("p t d -> p (t d)").bitcast(i32).rearrange("p (t k) -> p t k", t=2)
        cmp_a, cmp_b = (QT[:, 512 * i:512 * (i + 1)].rearrange("p (t e f) -> p t e f", t=NT, e=E) for i in range(2))
        Qs, Ks = (big[:, 8192 * i:8192 * (i + 1)].bitcast(bf16).rearrange("p (h t) -> p h t", h=16) for i in range(2))
        parts = big[:, 16384:17920].bitcast(bf16).rearrange("p (c t) -> p c t", c=3)
        T1 = big[:, 0:4096].rearrange("p (q n) -> p q n", n=BH1)
        Q1 = [big[:, 4096 + 2048 * i:6144 + 2048 * i].bitcast(bf16).rearrange("p (q n) -> p q n", n=BH1)
              for i in range(3)]
        Q1all = big[:, 4096:10240].bitcast(bf16).rearrange("p (i q n) -> p i q n", i=3, n=BH1)
        ST = big[:, 10240:18432].rearrange("p (c n q) -> p c n q", c=2, n=BH1)
        Va = late[:, 0:4096].rearrange("p (t h w) -> p t h w", t=NT, w=32)
        hid = [late[:, 4096 + 2048 * i:6144 + 2048 * i].rearrange("p (c t) -> p c t", c=FC) for i in range(2)]
        PTs.append(late[:, 4096:4608].rearrange("p (c q) -> p c q", c=2))
        wide = late[:, :].rearrange("p (w h m) -> p w h m", w=8, h=H1)
        WQT, WKT, WVT, WO = (wide[:, i] for i in range(4))
        AQK, CVO = WQT, WVT
        WQ = xm
        QF = late[:, 7168:8192].rearrange("p (s t) -> p s t", s=2)
        PWf = QT
        PW = [KT[:, 256 * i:256 * (i + 1)].bitcast(bf16) for i in range(3)]
        QR = [Os[i][:, :] for i in range(2)]
        GT = [att[i][:, 0, :] for i in range(2)]

        nL, nH = (place(n, 4096 * i, [128, TOK], fp32r) for i, n in enumerate(("nL", "nH")))
        wH, wL = ([place(f"{n}{i}", o + 2048 * i, [128, F], fp32r) for i in range(2)] for n, o in (("wH", 8192), ("wL", 12288)))

        scratch = nc.dram_tensor("parts_scratch", [2, 128, 3, TOK], bf16, kind="Internal").ap()

        bank = [ctx.enter_context(nc.psum_tensor(f"bank{i}", [128, 512], fp32)) for i in range(8)]
        M = [6, 7]
        PVB = [4, 5, M[1]]

        def bank_of(name, usual):
            return 7 if name in ("f1.0", "f1n.0") else M[usual]

        def out_bank(qh, b):
            return 6 if qh else 6 + b % 2

        block = ctx.enter_context(nc.Block())

        SMALL = 16 * 15
        ORDER = ["a0", "f0", "a1", "f1", "a2", "f2", "a3", "f3"]
        NEXT = {"f1": "a2", "f2": "a3"}
        KV_STEP = {"f1": 8, "f2": 5}

        def bias_step(key, hf):
            return 5 if (key, hf) == ("f1", 0) else 3

        AFTER = dict(zip(ORDER, ORDER[1:]))
        SLOTLOAD = {"f0": 1, "f1": 2, "f2": 3, "f3": 4}

        def x_ready(eng, key, hf=1):
            n = len(ORDER) if key == "out" else ORDER.index(key)
            if n == 0:
                eng.wait_ge(sem("ld.x"), 16)
            elif ORDER[n - 1] in FFN:
                eng.wait_ge(*at(ORDER[n - 1], "acc", (hf + 1) * FFN[ORDER[n - 1]][0]))
            elif ORDER[n - 1] == "a1":
                eng.wait_ge(*at("a1", "x", B + 2 * (hf + 1)))
            else:
                eng.wait_ge(*at(ORDER[n - 1], "x", 2 * (hf + 1)))


        @block.sync
        def _(sp):
            sp.dma_start(cx[:, :, :], A["ctx"].rearrange("(t p) d -> p t d", p=128)).then_inc(sem("ld.ctx"), 16)
            sp.dma_start(aw[:, 0:4, :], A["aw"][0:4].rearrange("w i o -> i w o")).then_inc(sem("ld.aw"), 16)
            sp.dma_start(x[:, :, :], A["x"].rearrange("(t p) d -> p t d", p=128)).then_inc(sem("ld.x"), 16)
            sp.dma_start(leni[:, :], bass.AP(A["lens"].tensor, 0, [[0, 128], [1, B]])).then_inc(sem("ld.lens"), 16)

            def expert(key, e):
                prev = {"f1": "f0", "f2": "f1", "f3": "f2"}.get(key)
                if prev and e < FFN[prev][0]:
                    sp.wait_ge(*at(prev, "down", FFN[prev][0] + e + 1))
                sp.dma_start(W[:, e, 0:F], A[f"{key}.w1"][e]).then_inc(sem(f"w.slot{e}"), 16)
                sp.dma_start(W[:, e, F:2 * F].rearrange("p (c d) -> p c d", c=FC),
                             A[f"{key}.w2"][e].rearrange("(c p) d -> p c d", p=128)).then_inc(sem(f"w.slot{e}"), 16)

            small = [(m2i[:, :, :], A["mask2"].rearrange("(t p) k -> p t k", p=128)),
                     (m1u[:, :], A["mask1"]),
                     (qkb[:, :], A["qkb"]),
                     (rows[:, :, :], bass.AP(A["rows"].tensor, 0, [[0, 128], [D, 7], [1, D]])),
                     (rb[:, :, :], bass.AP(A["rb"].tensor, 0, [[0, 128], [E, 2], [1, E]])),
                     (rw[:, :, :], A["rw"].rearrange("l d e -> d l e")),
                     (b1[:, 0, :], A["f0.b1"]),
                     (b1[:, 1, 0:8 * FC], A["f1.b1"]),
                     (b1[:, 2, 0:8 * FC], A["f3.b1"]),
                     (b2[:, 0, :], A["f0.b2"]), (b2[0:8, 1, :], A["f1.b2"]), (b2[0:8, 2, :], A["f3.b2"]),
                     (mixw[:, :], A["mixw"]),
                     (bub[:, 0, :], A["bu"]), (bub[:, 1, :], A["bv"])]
            for dst, src in small:
                sp.dma_start(dst, src).then_inc(sem("ld.small"), 16)
            sp.dma_start(aw[:, 4:12, :], A["aw"][4:12].rearrange("w i o -> i w o")).then_inc(sem("ld.aw2"), 16)

            def stack(key, side, half=None):
                H, d, _ = NARROW[key]
                n = LAYER_OF[key]
                cols = slice(0, TOK) if half is None else slice(512 * half, 512 * (half + 1))
                dst = (Qs, Ks)[side]
                if side:
                    sp.wait_ge(*at(key, "kp", 1))
                    if key == "a3":
                        sp.wait_ge(*at("a2", "S", narrow["a2"]))
                    elif key == "a2":
                        sp.wait_ge(sem("c.zero"), 1)
                else:
                    sp.wait_ge(*at(key, "qp", half + 1))
                done = 16 * (3 * n + (1 if side else 2 + half))
                sp.dma_start(scratch[side, :, :, cols], parts[:, :, cols]).then_inc(sem("st.w"), 16)
                sp.wait_ge(sem("st.w"), done)
                src = scratch[side].rearrange("(h i) c t -> i h c t", i=d)
                for r, pair in enumerate(PAIRS):
                    sp.dma_start(dst[r * d:(r + 1) * d, 0:H, cols], src[:, :, pair[side], cols])\
                      .then_inc(sem("st.k" if side else f"st.q{half}"), 16)

            stack("a0", 1)
            sp.wait_ge(sem("c.maskrow"), 1)
            sp.dma_start(Ks[MASK_ROW:MASK_ROW + 1, 1:8, :], Ks[MASK_ROW:MASK_ROW + 1, 0:1, :].broadcast_to([1, 7, TOK]))\
              .then_inc(sem("ld.mask"), 16)
            stack("a0", 0, 0)
            stack("a0", 0, 1)
            for e in range(9):
                expert("f0", e)
            sp.wait_ge(*at("a0", "pv", narrow["a0"]))
            sp.wait_ge(sem("c.masks"), 1)
            for i, n in enumerate(("wqT", "wkT", "wvT", "wo")):
                sp.dma_start(wide[:, i], A[f"a1.{n}"]).then_inc(sem("ld.wide"), 16)
            sp.dma_start(WQ[:, :, :], A["a1.wq"]).then_inc(sem("ld.wide"), 16)
            sp.wait_ge(*at("f0", "comb", 2))
            sp.dma_start(PWf[:, 0:WIN], A["a1.pos"]).then_inc(sem("ld.pos"), 16)
            for e in range(8):
                expert("f1", e)
            for key, nxt in (("a2", "f2"), ("a3", "f3")):
                stack(key, 1)
                for e in range(8):
                    if e == 4:
                        stack(key, 0, 0)
                    expert(nxt, e)
                stack(key, 0, 1)
            x_ready(sp, "out")
            sp.dma_start(out.rearrange("(t p) d -> p t d", p=128), x[:, :, :]).then_inc(sem("stored"), 16)
            sp.wait_ge(sem("stored"), 16)

        @block.gpsimd
        def _(pool):
            chain = [0]

            def link(ins):
                chain[0] += 1
                ins.then_inc(sem("pool.chain"), 1)
                pool.wait_ge(sem("pool.chain"), chain[0])

            link(pool.memset(ident[:, :], 0.0))
            link(pool.affine_select(out=ident[:, :], in_=ident[:, :], compare_op=ALU.not_equal, fill=1.0, base=0,
                                    pattern=[[-1, 128]], channel_multiplier=1))
            pool.tensor_copy(identb[:, :], ident[:, :]).then_inc(sem("c.ident"), 1)
            pool.wait_ge(sem("c.ident"), 1)
            link(pool.memset(half[:, :], -0.5))
            pool.iota(keyrow[:, :], pattern=[[1, S]], base=0, channel_multiplier=0, allow_small_or_imprecise_dtypes=True)\
                .then_inc(sem("c.keyrow"), 1)
            pool.wait_ge(sem("c.keyrow"), 1)
            link(pool.iota(qpos[:, :].rearrange("p (b t) -> p b t", t=2), pattern=[[0, B], [128, 2]], base=0,
                           channel_multiplier=1, allow_small_or_imprecise_dtypes=True))
            link(pool.memset(lowert[:, :, :], 1.0))
            pool.affine_select(out=lowert[:, :, :], in_=lowert[:, :, :], compare_op=ALU.is_gt, fill=0.0, base=0,
                               pattern=[[1, E], [-1, E]], channel_multiplier=0).then_inc(sem("c.rest"), 1)
            pool.wait_ge(sem("c.rest"), 1)
            link(pool.memset(comb[:, :, :], 1.0))
            pool.memset(Va[:, :, :, :], 0.0).then_inc(sem("c.Va"), 1)

            def layer_norm_rstd(name):
                ts = slice(4 * int(name[-1]), 4 * int(name[-1]) + 4)
                pool.wait_ge(*at(name, "mv", 1))
                link(pool.tensor_scalar(rstd[:, ts], mv[:, ts, 1], LN_EPS, None, ALU.add))
                pool.tensor_tensor(rstd[:, ts], rstd[:, ts], half[:, ts], ALU.pow).then_inc(sem("rstd"), 1)
                pool.wait_ge(*at(name, "rstd", 1))

            for name in norms:
                layer_norm_rstd(name)
                if name == "a0.0":
                    pool.memset(Qs[96:128, 0:8, :], 1.0).then_inc(sem("c.rows"), 1)
                    pool.wait_ge(sem("c.rows"), 1)
                if name == "f1c.1":
                    pool.wait_ge(sem("a1.o"), 2 * BH1)
                    link(pool.memset(Va[:, :, :, :], 0.0))
                    pool.memset(big[:, 0:16384], 0.0).then_inc(sem("c.zero"), 1)
                    pool.wait_ge(sem("c.zero"), 1)

        @block.vector
        def _(dve):
            chain = [0]
            v = nc.vector

            def link(ins):
                chain[0] += 1
                ins.then_inc(sem("dve.chain"), 1)
                dve.wait_ge(sem("dve.chain"), chain[0])

            def norm_stats(key, hf, src):
                n = norms.index(f"{key}.{hf}")
                if n:
                    dve.wait_ge(*at(norms[n - 1], "xn", 4))
                for t in range(4 * hf, 4 * hf + 4):
                    ins = v.bn_stats(stats[:, t, :], src[:, t, :])
                link(ins)
                for t in range(4 * hf, 4 * hf + 4):
                    ins = v.bn_aggr(mv[:, t, :], stats[:, t, :])
                ins.then_inc(sem("mv"), 1)

            def norm_apply(key, hf, src, dst):
                dve.wait_ge(*at(f"{key}.{hf}", "rstd", 1))
                for t in range(4 * hf, 4 * hf + 4):
                    v.tensor_scalar(dst[:, t, :], src[:, t, :], mv[:, t, 0:1], rstd[:, t:t + 1],
                                    ALU.subtract, ALU.mult).then_inc(sem("xn"), 1)

            def query_parts(key, hf):
                dve.wait_ge(sem("st.w"), 16 * (3 * LAYER_OF[key] + 1))
                dve.wait_ge(*at(key, "qt", hf + 1))
                split(QT, slice(512 * hf, 512 * (hf + 1)), "qp")

            def row(i, n=NT):
                return rows[:, i:i + 1, :].broadcast_to([128, n, D])

            def mask_row():
                dve.wait_ge(sem("ld.lens"), 16)
                dve.wait_ge(sem("c.keyrow"), 1)
                link(v.tensor_copy(lenf[:, :], leni[:, :]))
                r = MASK_ROW
                for b in range(B):
                    ins = v.tensor_scalar(Ks[r:r + 1, 0, S * b:S * (b + 1)], keyrow[r:r + 1, :], lenf[r:r + 1, b:b + 1], L0_NEG,
                                          ALU.is_ge, ALU.mult)
                ins.then_inc(sem("c.maskrow"), 1)

            def masks():
                dve.wait_ge(sem("ld.small"), SMALL)
                dve.wait_ge(sem("c.rest"), 1)
                v.tensor_scalar(madd2[:, :, :], m2i[:, :, :], 0.0, BIG_NEG, ALU.is_equal, ALU.mult)
                for b in range(B):
                    v.tensor_scalar(qmask[:, 2 * b:2 * b + 2], qpos[:, 2 * b:2 * b + 2], lenf[:, b:b + 1], None, ALU.is_lt)
                link(v.tensor_copy(m1f[:, :], m1u[:, :]))
                link(v.tensor_scalar(m1f[:, :], m1f[:, :], 1.0, -L1_NEG, ALU.subtract, ALU.mult))
                link(v.tensor_scalar(bst[:, 1, :], bub[:, 1, :], float(D) ** -0.5, None, ALU.mult))
                v.memset(r1[:, :], 0.0).then_inc(sem("c.masks"), 1)

            link(v.memset(Ks[96:128, 0:8, :], 0.0))

            def split(src, cols, done):
                f, (p0, p1, p2) = src[:, cols], (parts[:, c, cols] for c in range(3))
                link(v.tensor_copy(p0, f))
                link(v.tensor_tensor(f, f, p0, ALU.subtract))
                link(v.tensor_copy(p1, f))
                v.tensor_tensor(p2, f, p1, ALU.subtract).then_inc(sem(done), 1)

            def keys_parts(key):
                n = LAYER_OF[key]
                dve.wait_ge(*at(key, "kt", 2))
                if n:
                    dve.wait_ge(sem("st.w"), 16 * 3 * n)
                split(KT, slice(0, TOK), "kp")

            def values(key):
                H, d, _ = NARROW[key]
                dve.wait_ge(*((sem("c.Va"), 1) if key == "a0" else (sem("c.zero"), 1)))
                Vk = Va[:, :, 0:H, :]
                v.memset(Vk[:, :, :, d:d + 1], 1.0)
                for c in range(2):
                    dve.wait_ge(*at(key, "v", c + 1))
                    src = bank[M[c]][:, :].rearrange("p (t h w) -> p t h w", t=4, w=d)
                    dst = Vk[:, 4 * c:4 * c + 4, :, 0:d]
                    for t in range(4):
                        if key == "a3":
                            ins = v.tensor_tensor(dst[:, t], src[:, t], rows[:, 5, :].rearrange("p (h w) -> p h w", w=d), ALU.add)
                        else:
                            ins = v.tensor_copy(dst[:, t], src[:, t])
                    ins.then_inc(sem("va"), 1)

            def attention(key):
                H, d, _ = NARROW[key]
                G = H // 4
                n = B * H
                if key == "a0":
                    x_ready(dve, key, 0)
                    norm_stats(key, 0, x)
                    norm_apply(key, 0, x, xn)
                    keys_parts(key)
                    mask_row()
                    values(key)
                    query_parts(key, 0)
                    masks()
                ffn_key = AFTER[key]

                def evacuate(i):
                    dve.wait_ge(*at(key, "T", i + 1))
                    if i >= 3:
                        dve.wait_ge(*at(key, "pv", i - 2))
                    v.tensor_copy(PTs[i % 3][:, :, :], bank[2 + i % 2][:, :].rearrange("p (c q) -> p c q", c=2))\
                        .then_inc(sem("pte"), 1)

                def normalise(g):
                    b, j = g // G, g % G
                    src = bank[PVB[g % 3]][:, 256:512].rearrange("p (t h w) -> p t h w", t=2, w=32)
                    dve.wait_ge(*at(key, "ot", g + 1))
                    if g:
                        dve.wait_ge(*at(key, "att", g))
                    link(v.reciprocal(rc[:, :, :], src[:, :, :, d]))
                    if key == "a0":
                        link(v.tensor_tensor(rc[:, :, :], rc[:, :, :],
                                             qmask[:, 2 * b:2 * b + 2].unsqueeze(2).broadcast_to([128, 2, 4]), ALU.mult))
                    for t in range(2):
                        if t == 0 and b >= 2 and j == 0:
                            dve.wait_ge(*at(key, "attT", b - 1))
                        ins = v.tensor_tensor(att[b % 2][:, t, 4 * d * j:4 * d * (j + 1)].rearrange("p (h w) -> p h w", w=d),
                                              src[:, t, :, 0:d], rc[:, t, :].unsqueeze(2).broadcast_to([128, 4, d]), ALU.mult)
                    ins.then_inc(sem("att"), 1)

                def residual(b):
                    dve.wait_ge(*at(key, "out", b + 1))
                    xs = x[:, 2 * b:2 * b + 2, :]
                    ins = v.tensor_tensor(xs, xs, bank[M[0]][:, 0:256].rearrange("p (t d) -> p t d", t=2), ALU.add)
                    if key == "a3":
                        link(ins)
                        ins = v.tensor_tensor(xs, xs, row(6, 2), ALU.add)
                    ins.then_inc(sem("x"), 1)

                for i in range(n + 17):
                    if i < n:
                        dve.wait_ge(*at(key, "S", i + 1))
                        v.tensor_reduce(negmax[:, i % 4, :], bank[i % 2][:, :].rearrange("p (t k) -> p t k", t=2),
                                        AX.X, ALU.max, negate=True).then_inc(sem("nm"), 1)
                    if 2 <= i <= n + 1 and not on_act(i - 2):
                        evacuate(i - 2)
                    if i >= 11 and (i - 11) % 4 == 0 and (i - 11) // 4 < n // 4:
                        normalise((i - 11) // 4)
                    if i >= H + 12 and (i - H - 12) % H == 0 and (i - H - 12) // H < B:
                        residual((i - H - 12) // H)
                    if i == 1:
                        x_ready(dve, key, 1)
                        norm_stats(key, 1, x)
                    if i == 3:
                        norm_apply(key, 1, x, xn)
                    if i == 9:
                        query_parts(key, 1)
                    if i in (n + 6, n + 8):
                        split_weights(ffn_key, (i - n - 6) // 2)
                    if i == 2 * H + 13:
                        x_ready(dve, ffn_key, 0)
                        norm_stats(ffn_key, 0, x)
                    if i == 2 * H + 14:
                        norm_apply(ffn_key, 0, x, xn)
                    if i == 2 * H + 18:
                        split_input(ffn_key, 0)
                    if i == n + 16:
                        router(ffn_key, 0)

            def split_input(key, hf):
                cols = slice(512 * hf, 512 * (hf + 1))
                dve.wait_ge(*at(f"{'f1n' if key == 'f1' else key}.{hf}", "nT", 1))
                link(v.tensor_copy(nH[:, cols], nT[1][:, cols]))
                v.tensor_tensor(nL[:, cols], nT[1][:, cols], nH[:, cols].bitcast(fp32), ALU.subtract).then_inc(sem("np"), 1)

            def split_weights(key, u):
                e = u % FFN[key][0]
                if u >= 2:
                    dve.wait_ge(*at(key, "up", FC * (u - 1)))
                elif key == "f1":
                    dve.wait_ge(sem("a1.o"), 2 * BH1)
                else:
                    before = ORDER[ORDER.index(key) - 1]
                    dve.wait_ge(*at(before, "pv", narrow[before]))
                dve.wait_ge(sem(f"w.slot{e}"), 32 * SLOTLOAD[key] if e < 8 else 32)
                link(v.tensor_copy(wH[u % 2][:, :], W[:, e, 0:F]))
                v.tensor_tensor(wL[u % 2][:, :], W[:, e, 0:F], wH[u % 2][:, :].bitcast(fp32), ALU.subtract).then_inc(sem("wp"), 1)

            def router(key, hf):
                nE, keep = FFN[key]
                ts = slice(4 * hf, 4 * hf + 4)
                n = [4, E]
                lgh, exh, selh, combh = lg[:, ts, :], ex[:, ts, :], sel[:, ts, :], comb[:, ts, 0:E]
                tmaxh, tsumh = tmax[:, ts], tsum[:, ts]
                ca, cb = cmp_a[:, ts], cmp_b[:, ts]
                dve.wait_ge(*at(key, "lg", hf + 1))
                src = bank[bank_of(f"{key}.{hf}", 0)][:, 0:4 * E].rearrange("p (t e) -> p t e", e=E)
                if key in ("f0", "f3"):
                    r = int(key == "f3")
                    v.tensor_tensor(lgh, src, rb[:, r:r + 1, :].broadcast_to([128, 4, E]), ALU.add).then_inc(sem("lgc"), 1)
                else:
                    v.tensor_copy(lgh, src).then_inc(sem("lgc"), 1)
                dve.wait_ge(*at(key, "lgc", hf + 1))
                if keep == 2:
                    link(v.tensor_reduce(tmaxh, lgh, AX.X, ALU.max))
                    v.tensor_tensor(exh, lgh, tmaxh.unsqueeze(2).broadcast_to([128, 4, E]), ALU.subtract).then_inc(sem("d"), 1)
                other = lgh.unsqueeze(2).broadcast_to([128, 4, E, E])
                own = lgh.unsqueeze(3).broadcast_to([128, 4, E, E])
                v.tensor_tensor(ca, other, own, ALU.is_gt)
                link(v.tensor_tensor(cb, other, own, ALU.is_equal))
                link(v.tensor_tensor(cb, cb, lowert[:, :, :].unsqueeze(1).broadcast_to([128, 4, E, E]), ALU.mult))
                link(v.tensor_tensor(ca, ca, cb, ALU.add))
                link(v.tensor_reduce(selh, ca, AX.X, ALU.add))
                if keep == 1:
                    v.tensor_scalar(combh, selh, float(keep), None, ALU.is_lt).then_inc(sem("comb"), 1)
                    return
                link(v.tensor_scalar(selh, selh, float(keep), None, ALU.is_lt))
                dve.wait_ge(*at(key, "ex", hf + 1))
                if key == "f1":
                    link(v.tensor_reduce(tsumh, exh, AX.X, ALU.add))
                link(v.tensor_tensor(selh, selh, exh, ALU.mult))
                if key != "f1":
                    link(v.tensor_reduce(tsumh, selh, AX.X, ALU.add))
                link(v.reciprocal(tsumh, tsumh))
                v.tensor_tensor(combh, selh, tsumh.unsqueeze(2).broadcast_to([128, 4, E]), ALU.mult).then_inc(sem("comb"), 1)

            def position_windows():
                dve.wait_ge(sem("ld.pos"), 16)
                pw = PWf[:, 0:WIN]
                res = big[:, 10240:10240 + WIN]
                link(v.tensor_copy(PW[0][:, 0:WIN], pw))
                link(v.tensor_tensor(res, pw, PW[0][:, 0:WIN], ALU.subtract))
                link(v.tensor_copy(PW[1][:, 0:WIN], res))
                v.tensor_tensor(PW[2][:, 0:WIN], res, PW[1][:, 0:WIN], ALU.subtract).then_inc(sem("a1.pw"), 1)

            def ffn(key):
                nE, keep = FFN[key]
                nxt = AFTER.get(key)
                if key == "f1":
                    split_weights(key, 0)
                    split_input(key, 0)
                    split_weights(key, 1)
                    router(key, 0)
                for u in range(2 * nE):
                    hf, e = divmod(u, nE)
                    if u + 2 < 2 * nE:
                        split_weights(key, u + 2)
                    if u == 0 and key != "f1":
                        x_ready(dve, key, 1)
                        norm_stats(key, 1, x)
                        norm_apply(key, 1, x, xn)
                    if key == "f1" and u in (0, 1, 2, 4, 5):
                        inner_layer(1, (0, 1, 2, 4, 5).index(u))
                    if u == (6 if key == "f1" else 3):
                        split_input(key, 1)
                    if u == (7 if key == "f1" else 2):
                        router(key, 1)
                    dve.wait_ge(*at(key, "comb", hf + 1))
                    dve.wait_ge(*at(key, "down", u + 1))
                    if u:
                        dve.wait_ge(*at(key, "acc", u))
                    if e == bias_step(key, hf) + 2 and key != "f2":
                        dve.wait_ge(*at(key, "b2a", hf + 1))
                    for i in range(4):
                        t = 4 * hf + i
                        ins = v.scalar_tensor_tensor(x[:, t, :], bank[4 + u % 2][:, 128 * i:128 * (i + 1)], comb[:, t, e:e + 1],
                                                     x[:, t, :], ALU.mult, ALU.add)
                    ins.then_inc(sem("acc"), 1)
                    if e == bias_step(key, hf) + 1 and key != "f2":
                        dve.wait_ge(*at(key, "acc", u + 1))
                        dve.wait_ge(*at(key, "b2", hf + 1))
                        xs = x[:, 4 * hf:4 * hf + 4, :]
                        v.tensor_tensor(xs, xs, bank[M[1]][:, :].rearrange("p (t d) -> p t d", t=4), ALU.add)\
                            .then_inc(sem("b2a"), 1)
                    if key == "f0" and u == 2 * nE - 3:
                        position_windows()
                    if u == KV_STEP.get(key, 99) + 1:
                        keys_parts(NEXT[key])
                    if u == KV_STEP.get(key, 99) + 2:
                        values(NEXT[key])
                    if u == nE and nxt:
                        x_ready(dve, nxt, 0)
                        norm_stats(nxt, 0, x)
                    if u == nE + 1 and nxt:
                        norm_apply(nxt, 0, x, xn)
                    if u == nE + 4 and nxt in NARROW:
                        query_parts(nxt, 0)

            def wide_attention():
                x_ready(dve, "a1", 1)
                norm_stats("a1", 1, x)
                norm_apply("a1", 1, x, xn)
                for qh in range(2):
                    for h in range(H1):
                        k = qh * H1 + h
                        dve.wait_ge(sem("a1.qf"), k + 1)
                        parts = [q.rearrange("p q (b h) -> p b q h", h=H1)[:, :, :, h] for q in Q1]
                        qs = QF[:, k % 2, :].rearrange("p (b q) -> p b q", b=B)
                        rs = P[k % 2][:, :, :].rearrange("p c (b q) -> p (c b) q", q=128)
                        link(v.tensor_tensor(rs, qs, parts[0], ALU.subtract))
                        link(v.tensor_copy(parts[1], rs))
                        v.tensor_tensor(parts[2], rs, parts[1], ALU.subtract).then_inc(sem("a1.q"), 1)
                    for u in range(16):
                        n = qh * 16 + u
                        qb, c = divmod(u, 2)
                        tmp = PTs[n % 2][:, :, :].rearrange("p c (q n) -> p (c q) n", n=BH1)
                        if n >= 2:
                            dve.wait_ge(sem("a1.st"), n - 1)
                        for g in range(4):
                            m = 4 * n + g
                            dve.wait_ge(sem("a1.S"), m + 1)
                            v.tensor_reduce(tmp[:, 4 * g:4 * g + 4, :],
                                            bank[m % 6][:, 0:384].rearrange("p (q g n) -> p q n g", q=4, g=3), AX.X, ALU.add)\
                                .then_inc(sem("a1.sr"), 1)
                        dve.wait_ge(sem("a1.sr"), 4 * n + 4)
                        dve.wait_ge(sem("a1.cs"), n + 1)
                        dst = ST[:, c, :, 16 * qb:16 * qb + 16].rearrange("p n q -> p q n")
                        v.tensor_tensor(dst, dst, tmp, ALU.add).then_inc(sem("a1.st"), 1)

                    def head_max(i):
                        dve.wait_ge(sem("a1.T0"), i + 1)
                        v.tensor_reduce(r1[:, i % 4:i % 4 + 1], bank[i % 2][:, 0:256], AX.X, ALU.max, negate=True)\
                            .then_inc(sem("a1.nm"), 1)

                    def head_scale(i):
                        dve.wait_ge(sem("a1.e"), i + 1)
                        link(v.reciprocal(r2[:, i % 4:i % 4 + 1], r2[:, i % 4:i % 4 + 1]))
                        p = P[i % 2][:, 0, :]
                        v.tensor_scalar(p, p, r2[:, i % 4:i % 4 + 1], None, ALU.mult).then_inc(sem("a1.p"), 1)

                    def head_out(i):
                        dve.wait_ge(sem("a1.G"), i + 1)
                        if i >= 2:
                            dve.wait_ge(sem("a1.o"), i - 1)
                        v.tensor_copy(GT[i % 2], bank[4 + i % 2][:, 0:128]).then_inc(sem("a1.g"), 1)

                    i0 = qh * 32
                    for i in range(32 + 5):
                        if i < 32:
                            head_max(i0 + i)
                        if 1 <= i <= 32:
                            head_scale(i0 + i - 1)
                        if 3 <= i <= 34:
                            head_out(i0 + i - 3)
                        if i >= 11 + 1 and (i - 12) % 8 == 0 and (i - 12) // 8 < B:
                            b = (i - 12) // 8
                            dve.wait_ge(sem("a1.o"), i0 + 8 * b + 8)
                            t = 2 * b + qh
                            v.tensor_tensor(x[:, t, :], x[:, t, :], bank[out_bank(qh, b)][:, 0:128], ALU.add).then_inc(sem("x"), 1)
                        if qh and i in (21, 23, 25, 30, 32):
                            inner_layer(0, (21, 23, 25, 30, 32).index(i))

            def inner_layer(hf, stage):
                ts = slice(4 * hf, 4 * hf + 4)
                if stage == 0:
                    x_ready(dve, "f1", hf)
                    norm_stats("f1", hf, x)
                elif stage == 1:
                    norm_apply("f1", hf, x, xn)
                    dve.wait_ge(*at(f"f1.{hf}", "xn", 4))
                    norm_stats("f1b", hf, xn)
                elif stage == 2:
                    norm_apply("f1b", hf, xn, xm)
                    dve.wait_ge(*at(f"f1b.{hf}", "xn", 4))
                    link(v.tensor_tensor(xm[:, ts, :], xm[:, ts, :], row(0, 4), ALU.mult))
                    v.tensor_tensor(xm[:, ts, :], xm[:, ts, :], row(1, 4), ALU.add).then_inc(sem("f1.n"), 1)
                    dve.wait_ge(sem("f1.n"), hf + 1)
                    link(v.tensor_tensor(xn[:, ts, :], xn[:, ts, :], xm[:, ts, :], ALU.add))
                    link(v.tensor_tensor(xn[:, ts, :], xn[:, ts, :], row(2, 4), ALU.add))
                elif stage == 3:
                    dve.wait_ge(sem("f1.mix"), hf + 1)
                    v.tensor_tensor(xm[:, ts, :], xn[:, ts, :], bank[bank_of(f"f1.{hf}", 1)][:, :].rearrange("p (t d) -> p t d", t=4), ALU.add)\
                        .then_inc(sem("f1.m"), 1)
                    dve.wait_ge(sem("f1.m"), hf + 1)
                    norm_stats("f1c", hf, xm)
                    link(v.tensor_tensor(x[:, ts, :], x[:, ts, :], xm[:, ts, :], ALU.add))
                elif stage == 4:
                    norm_apply("f1c", hf, xm, xn)
                    dve.wait_ge(*at(f"f1c.{hf}", "xn", 4))
                    link(v.tensor_tensor(xn[:, ts, :], xn[:, ts, :], row(3, 4), ALU.mult))
                    v.tensor_tensor(xn[:, ts, :], xn[:, ts, :], row(4, 4), ALU.add).then_inc(sem("f1.n2"), 1)

            for key in ORDER:
                if key in NARROW:
                    attention(key)
                elif key == "a1":
                    wide_attention()
                else:
                    ffn(key)

        @block.scalar
        def _(act):
            a = nc.scalar

            def load_table(key, func):
                i = ORDER.index(key)
                act.wait_ge(sem("c.rest"), 1)
                a.activation(warm[:, i:i + 1], half[:, 0:1], func)

            def copy_T(key, hf, dst):
                act.wait_ge(*at(f"{key}.{hf}", "tr", 1))
                a.activation(dst[:, 512 * hf:512 * (hf + 1)], bank[bank_of(f"{key}.{hf}", hf if key == "ctx" else 0)][:, :], ACT.Copy).then_inc(sem("nT"), 1)

            def queries(key, hf):
                scale = NARROW[key][2]
                act.wait_ge(*at(key, "q", hf + 1))
                qt = QT[:, 512 * hf:512 * (hf + 1)]
                if key == "a3":
                    ins = a.activation(qt, bank[M[1 - hf]][:, :], ACT.Identity, bias=qkb[:, 0:1])
                else:
                    ins = a.activation(qt, bank[M[1 - hf]][:, :], ACT.Copy, scale=scale)
                ins.then_inc(sem("qt"), 1)

            def router(key, hf):
                if FFN[key][1] == 2:
                    act.wait_ge(*at(key, "d", hf + 1))
                    exh = ex[:, 4 * hf:4 * hf + 4, :]
                    a.activation(exh, exh, ACT.Exp).then_inc(sem("ex"), 1)

            copy_T("ctx", 0, cT)
            copy_T("ctx", 1, cT)

            def project(key):
                for c in range(2):
                    act.wait_ge(*at(key, "k", c + 1))
                    kt = KT[:, 512 * c:512 * (c + 1)]
                    if key == "a3":
                        ins = a.activation(kt, bank[M[c]][:, :], ACT.Identity, bias=qkb[:, 1:2])
                    else:
                        ins = a.activation(kt, bank[M[c]][:, :], ACT.Copy)
                    ins.then_inc(sem("kt"), 1)

            def attention(key):
                H, d, scale = NARROW[key]
                n = B * H
                if key == "a0":
                    project(key)
                    copy_T(key, 0, nT[0])
                    queries(key, 0)
                ffn_key = AFTER[key]
                load_table(key, ACT.Exp)
                for i in range(n + 17):
                    if i < n:
                        act.wait_ge(*at(key, "nm", i + 1))
                        if i >= 2:
                            act.wait_ge(*at(key, "T", i - 1))
                        for t in range(2):
                            ins = a.activation(P[i % 2][:, t, :], bank[i % 2][:, 256 * t:256 * (t + 1)], ACT.Exp,
                                               bias=negmax[:, i % 4, t:t + 1])
                        ins.then_inc(sem("e"), 1)
                    if 2 <= i <= n + 1 and on_act(i - 2):
                        act.wait_ge(*at(key, "T", i - 1))
                        if i >= 5:
                            act.wait_ge(*at(key, "pv", i - 4))
                        a.activation(PTs[(i - 2) % 3][:, :, :], bank[2 + i % 2][:, :].rearrange("p (c q) -> p c q", c=2), ACT.Copy)\
                            .then_inc(sem("pta"), 1)
                    if i >= 8 and (i - 8) % 4 == 0 and (i - 8) // 4 < n // 4:
                        g = (i - 8) // 4
                        act.wait_ge(*at(key, "pv", 4 * g + 4))
                        if g >= 2:
                            act.wait_ge(*at(key, "ot", g - 1))
                        a.activation(Os[g % 2][:, :], bank[PVB[g % 3]][:, 0:256], ACT.Copy).then_inc(sem("oe"), 1)
                    if i >= H + 10 and (i - H - 10) % H == 0 and (i - H - 10) // H < B:
                        b = (i - H - 10) // H
                        act.wait_ge(*at(key, "attT", b + 1))
                        if b >= 2:
                            act.wait_ge(*at(key, "out", b - 1))
                        a.activation(attT[b % 2][:, :], bank[6][:, 0:256], ACT.Copy).then_inc(sem("ate"), 1)
                    if i == 6:
                        copy_T(key, 1, nT[0])
                    if i == 8:
                        queries(key, 1)
                    if i == 2 * H + 17:
                        copy_T(ffn_key, 0, nT[1])

            def wide_weights(i):
                act.wait_ge(sem("a1.pre"), i + 1)
                if i < 4:
                    dst = (AQK, CVO)[i // 2][:, 4 * (i % 2):4 * (i % 2) + 4, :]
                    ins = a.activation(dst, bank[M[i % 2]][:, :].rearrange("p (h m) -> p h m", h=4), ACT.Copy)
                else:
                    ins = a.activation(bst[:, 0, :], bank[M[0]][:, 0:H1], ACT.Copy, scale=float(D) ** -0.5)
                ins.then_inc(sem("a1.w"), 1)

            def ffn(key, nTk):
                nE, keep = FFN[key]
                bi = {"f0": 0, "f1": 1, "f3": 2}.get(key)
                func = {"f0": ACT.Gelu_apprx_tanh, "f1": ACT.Silu, "f2": ACT.Relu, "f3": ACT.Gelu}[key]
                act.wait_ge(sem("ld.small"), SMALL)
                load_table(key, func)
                nxt = AFTER.get(key)
                for u in range(2 * nE):
                    hf, e = divmod(u, nE)
                    for c in range(FC):
                        act.wait_ge(*at(key, "up", FC * u + c + 1))
                        if c == 0 and u >= 2:
                            act.wait_ge(*at(key, "down", u - 1))
                        dst = hid[u % 2][:, c, :]
                        if bi is None:
                            ins = a.activation(dst, bank[c][:, :], func)
                        else:
                            ins = a.activation(dst, bank[c][:, :], func, bias=b1[:, bi, FC * e + c:FC * e + c + 1])
                        ins.then_inc(sem("h"), 1)
                    if u == 0:
                        router(key, 0)
                    if key == "f1":
                        if u == 3:
                            copy_T("f1", 1, nT[0])
                        if u == 6:
                            copy_T("f1n", 1, nT[1])
                    elif u == 2:
                        copy_T(key, 1, nT[1])
                    if u == (7 if key == "f1" else 3):
                        router(key, 1)
                    if e == bias_step(key, hf) + 1 and key != "f2":
                        act.wait_ge(*at(key, "cT", hf + 1))
                        a.activation(combT[0:nE, 512 * hf:512 * (hf + 1)], bank[M[1]][0:nE, :], ACT.Copy)\
                            .then_inc(sem("cTe"), 1)
                    if key == "f0" and 6 <= u < 11:
                        wide_weights(u - 6)
                    if u == KV_STEP.get(key, 99) + 1:
                        project(NEXT[key])
                    if u == nE + 3 and nxt:
                        copy_T(nxt, 0, nT[0])
                    if u == nE + 4 and nxt in NARROW:
                        queries(nxt, 0)

            def wide_attention():
                scale = float(D) ** -0.5
                act.wait_ge(sem("a1.w"), 5)
                act.wait_ge(sem("c.masks"), 1)
                copy_T("a1", 1, nT[0])
                for qh in range(2):
                    for m in range(2 * H1):
                        h = m % H1
                        act.wait_ge(sem("a1.t"), 2 * H1 * qh + m + 1)
                        src = bank[4 + m % 4][:, :].rearrange("p (b q) -> p b q", b=B)
                        if m < H1:
                            k = qh * H1 + h
                            if k >= 2:
                                act.wait_ge(sem("a1.q"), k - 1)
                            if m == 0 and qh:
                                act.wait_ge(sem("a1.S"), 64)
                            a.activation(QF[:, k % 2, :], bank[4 + m % 4][:, :], ACT.Identity,
                                         bias=bst[:, 1, h:h + 1], scale=scale)
                            a.activation(Q1[0].rearrange("p q (b h) -> p b q h", h=H1)[:, :, :, h], src, ACT.Identity,
                                         bias=bst[:, 1, h:h + 1], scale=scale).then_inc(sem("a1.qf"), 1)
                        else:
                            a.activation(T1.rearrange("p q (b h) -> p b q h", h=H1)[:, :, :, h], src, ACT.Identity,
                                         bias=bst[:, 0, h:h + 1], scale=scale).then_inc(sem("a1.te"), 1)
                    for u in range(16):
                        n = qh * 16 + u
                        qb, c = divmod(u, 2)
                        act.wait_ge(sem("a1.C"), n + 1)
                        if u == 0 and qh:
                            act.wait_ge(sem("a1.T0"), 32)
                        for b in range(B):
                            ins = a.activation(ST[:, c, H1 * b:H1 * (b + 1), 16 * qb:16 * qb + 16].rearrange("p n q -> p q n"),
                                               bank[M[u % 2]][:, :].rearrange("p (q n) -> p q n", n=BH1)[:, :, H1 * b:H1 * (b + 1)],
                                               ACT.Identity, bias=m1f[:, 2 * b + c:2 * b + c + 1])
                        ins.then_inc(sem("a1.cs"), 1)
                    i0 = qh * 32
                    for j in range(33):
                        i = i0 + j
                        if j < 32:
                            act.wait_ge(sem("a1.nm"), i + 1)
                            if i >= 2:
                                act.wait_ge(sem("a1.T1"), i - 1)
                            elif i == 0:
                                act.wait_ge(sem("a1.q"), 8)
                            a.activation(P[i % 2][:, 0, :], bank[i % 2][:, 0:256], ACT.Exp, bias=r1[:, i % 4:i % 4 + 1],
                                         accum_out=r2[:, i % 4:i % 4 + 1]).then_inc(sem("a1.e"), 1)
                        if j >= 1:
                            k = i - 1
                            act.wait_ge(sem("a1.T1"), k + 1)
                            if k >= 2:
                                act.wait_ge(sem("a1.G"), k - 1)
                            a.activation(PTs[k % 2][:, 0, :], bank[2 + k % 2][:, 0:256], ACT.Copy).then_inc(sem("a1.pte"), 1)
                        if qh and j == 27:
                            copy_T("f1", 0, nT[0])

            for key in ORDER:
                if key in NARROW:
                    attention(key)
                elif key == "a1":
                    wide_attention()
                else:
                    if key == "f1":
                        copy_T("f1n", 0, nT[1])
                    ffn(key, nT[1])

        @block.tensor
        def _(pe):
            mm, tr = nc.tensor.matmul, nc.tensor.transpose
            reader = {}

            def take(k):
                if k in reader:
                    pe.wait_ge(*reader.pop(k))
                return bank[k]

            def turn(key, hf, src, ready):
                k = bank_of(f"{key}.{hf}", hf if key == "ctx" else 0)
                dst = take(k)
                for i in range(4):
                    t = 4 * hf + i
                    pe.wait_ge(*ready(t))
                    ins = tr(dst[:, 128 * i:128 * (i + 1)], src[:, t, :], ident[:, :])
                ins.then_inc(sem("tr"), 1)
                reader[k] = at(f"{key}.{hf}", "nT", 1)

            def turn_norm(key, hf):
                turn(key, hf, xn, lambda t: at(f"{key}.{hf}", "xn", t - 4 * hf + 1))

            def queries(key, hf):
                pe.wait_ge(*at(f"{key}.{hf}", "nT", 1))
                dst = take(M[1 - hf])
                mm(dst[:, :], aw[:, 4 * LAYER_OF[key], :], nT[0][:, 512 * hf:512 * (hf + 1)], start=True, stop=True).then_inc(sem("q"), 1)
                reader[M[1 - hf]] = at(key, "qt", hf + 1)

            def logits(key, hf):
                nTk = nT[1]
                pe.wait_ge(sem("ld.small"), SMALL)
                pe.wait_ge(*at(f"{'f1n' if key == 'f1' else key}.{hf}", "nT", 1))
                k = bank_of(f"{key}.{hf}", 0)
                dst = take(k)
                for i in range(4):
                    t = 4 * hf + i
                    ins = mm(dst[:, E * i:E * (i + 1)], nTk[:, 128 * t:128 * (t + 1)], rw[:, int(key[1]), :], start=True, stop=True)
                ins.then_inc(sem("lg"), 1)
                reader[k] = at(key, "lgc", hf + 1)

            pe.wait_ge(sem("c.ident"), 1)
            turn("ctx", 0, cx, lambda t: (sem("ld.ctx"), 16))
            turn("ctx", 1, cx, lambda t: (sem("ld.ctx"), 16))
            pe.wait_ge(sem("ld.aw"), 16)
            pe.wait_ge(*at("ctx.1", "nT", 1))

            def keys(key):
                w = 4 * LAYER_OF[key]
                for c in range(2):
                    dst = take(M[c])
                    mm(dst[:, :], aw[:, w + 1, :], cT[:, 512 * c:512 * (c + 1)], start=True, stop=True).then_inc(sem("k"), 1)
                    reader[M[c]] = at(key, "kt", c + 1)

            def values(key):
                w = 4 * LAYER_OF[key]
                for c in range(2):
                    dst = take(M[c])
                    for i in range(4):
                        t = 4 * c + i
                        ins = mm(dst[:, 128 * i:128 * (i + 1)], cT[:, 128 * t:128 * (t + 1)], aw[:, w + 2, :], start=True, stop=True)
                    ins.then_inc(sem("v"), 1)
                    reader[M[c]] = at(key, "va", c + 1)

            def up(key, u):
                nE = FFN[key][0]
                hf, e = divmod(u, nE)
                if e == 0:
                    pe.wait_ge(*at(key, "np", hf + 1))
                pe.wait_ge(*at(key, "wp", u + 1))
                for c in range(FC):
                    dst = take(c)
                    for n, (w, act_in) in enumerate(((wH, nH), (wH, nL), (wL, nH))):
                        ins = mm(dst[:, :], w[u % 2][:, 128 * c:128 * (c + 1)], act_in[:, 512 * hf:512 * (hf + 1)],
                                 start=n == 0, stop=n == 2)
                    ins.then_inc(sem("up"), 1)
                    reader[c] = at(key, "h", FC * u + c + 1)

            def attention(key):
                H, d, _ = NARROW[key]
                G = H // 4
                n = B * H
                w = 4 * LAYER_OF[key]
                R = ROWS[key]
                if key == "a0":
                    keys(key)
                    values(key)
                    turn_norm(key, 0)
                    queries(key, 0)
                ffn_key = AFTER[key]
                pe.wait_ge(sem("st.k"), 16 * len(PAIRS) * (LAYER_OF[key] + 1))
                if key == "a0":
                    pe.wait_ge(sem("c.rows"), 1)
                    pe.wait_ge(sem("ld.mask"), 16)
                    pe.wait_ge(sem("ld.aw2"), 16)
                else:
                    pe.wait_ge(sem("c.masks"), 1)

                def scores(i):
                    b, h = divmod(i, H)
                    if h == 0 and b % 2 == 0:
                        pe.wait_ge(sem(f"st.q{b // 2}"), 16 * len(PAIRS) * (LAYER_OF[key] + 1))
                    dst = take(i % 2)
                    for t in range(2):
                        o = dst[:, 256 * t:256 * (t + 1)]
                        ins = mm(o, Qs[0:R, h, S * b + 128 * t:S * b + 128 * (t + 1)], Ks[0:R, h, S * b:S * (b + 1)],
                                 start=True, stop=key != "a2")
                        if key == "a2":
                            ins = mm(o, identb[:, :], madd2[:, t, :], start=False, stop=True)
                    ins.then_inc(sem("S"), 1)
                    reader[i % 2] = at(key, "e", i + 1)

                def transpose_p(i):
                    pe.wait_ge(*at(key, "e", i + 1))
                    dst = take(2 + i % 2)
                    for c in range(2):
                        for t in range(2):
                            ins = tr(dst[:, 256 * c + 128 * t:256 * c + 128 * (t + 1)], P[i % 2][:, t, 128 * c:128 * (c + 1)], ident[:, :])
                    ins.then_inc(sem("T"), 1)
                    reader[2 + i % 2] = probs_in_sbuf(key, i)

                def probs_v(i):
                    b, h = divmod(i, H)
                    g, j = divmod(i, 4)
                    pe.wait_ge(*probs_in_sbuf(key, i))
                    if i == 0:
                        pe.wait_ge(*at(key, "va", 2))
                    dst = take(PVB[g % 3]) if j == 0 else bank[PVB[g % 3]]
                    for c in range(2):
                        ins = mm(dst[32 * j:32 * (j + 1), 0:256], Va[:, 2 * b + c, h, :], PTs[i % 3][:, c, :],
                                 start=c == 0, stop=c == 1)
                    ins.then_inc(sem("pv"), 1)

                def token_major(g):
                    pe.wait_ge(*at(key, "oe", g + 1))
                    for t in range(2):
                        ins = tr(bank[PVB[g % 3]][:, 256 + 128 * t:384 + 128 * t], Os[g % 2][:, 128 * t:128 * (t + 1)], ident[:, :])
                    ins.then_inc(sem("ot"), 1)
                    reader[PVB[g % 3]] = at(key, "att", g + 1)

                def out_transpose(b):
                    pe.wait_ge(*at(key, "att", G * (b + 1)))
                    dst = take(M[0])
                    for t in range(2):
                        ins = tr(dst[:, 128 * t:128 * (t + 1)], att[b % 2][:, t, :], ident[:, :])
                    ins.then_inc(sem("attT"), 1)
                    reader[M[0]] = at(key, "ate", b + 1)

                def out_project(b):
                    pe.wait_ge(*at(key, "ate", b + 1))
                    dst = take(M[0])
                    for t in range(2):
                        ins = mm(dst[:, 128 * t:128 * (t + 1)], attT[b % 2][:, 128 * t:128 * (t + 1)], aw[:, w + 3, :], start=True, stop=True)
                    ins.then_inc(sem("out"), 1)
                    reader[M[0]] = at(key, "x", b + 1)

                for i in range(n + 17):
                    if i < n:
                        scores(i)
                    if 2 <= i <= n + 1:
                        transpose_p(i - 2)
                    if 4 <= i <= n + 3:
                        probs_v(i - 4)
                    if i >= 10 and (i - 10) % 4 == 0 and (i - 10) // 4 < n // 4:
                        token_major((i - 10) // 4)
                    if i >= H + 9 and (i - H - 9) % H == 0 and (i - H - 9) // H < B:
                        out_transpose((i - H - 9) // H)
                    if i >= H + 11 and (i - H - 11) % H == 0 and (i - H - 11) // H < B:
                        out_project((i - H - 11) // H)
                    if i == 6:
                        turn_norm(key, 1)
                    if i == 8:
                        queries(key, 1)
                    if i == n + 9:
                        up(ffn_key, 0)
                    if i == 2 * H + 16:
                        turn_norm(ffn_key, 0)
                    if i == n + 16:
                        logits(ffn_key, 0)

            def wide_weights(i):
                pe.wait_ge(sem("ld.wide"), 16 * 5)
                dst = take(M[i % 2])
                if i < 4:
                    l, r = ((WQT, WKT), (WVT, WO))[i // 2]
                    for j in range(4):
                        h = 4 * (i % 2) + j
                        ins = mm(dst[:, 128 * j:128 * (j + 1)], l[:, h, :], r[:, h, :], start=True, stop=True)
                else:
                    for h in range(H1):
                        ins = mm(dst[:, h:h + 1], WKT[:, h, :], bub[:, 0, h:h + 1], start=True, stop=True)
                ins.then_inc(sem("a1.pre"), 1)
                reader[M[i % 2]] = (sem("a1.w"), i + 1)

            def ffn(key, nTk):
                nE, keep = FFN[key]
                nxt = AFTER.get(key)

                def down(u):
                    e = u % nE
                    if u < nE:
                        pe.wait_ge(sem(f"w.slot{e}"), 32 * SLOTLOAD[key] if e < 8 else 32)
                    pe.wait_ge(*at(key, "h", FC * (u + 1)))
                    dst = take(4 + u % 2)
                    for i in range(4):
                        for c in range(FC):
                            ins = mm(dst[:, 128 * i:128 * (i + 1)], hid[u % 2][:, c, 128 * i:128 * (i + 1)],
                                     W[:, e, F + 128 * c:F + 128 * (c + 1)], start=c == 0, stop=c == FC - 1)
                    ins.then_inc(sem("down"), 1)
                    reader[4 + u % 2] = at(key, "acc", u + 1)

                def weights_turned(hf):
                    pe.wait_ge(*at(key, "comb", hf + 1))
                    dst = take(M[1])
                    for i in range(4):
                        ins = tr(dst[0:nE, 128 * i:128 * (i + 1)], comb[:, 4 * hf + i, 0:nE], ident[:, :])
                    ins.then_inc(sem("cT"), 1)
                    reader[M[1]] = at(key, "cTe", hf + 1)

                def biases(hf):
                    dst = take(M[1])
                    for i in range(4):
                        t = 4 * hf + i
                        ins = mm(dst[:, 128 * i:128 * (i + 1)], combT[0:nE, 128 * t:128 * (t + 1)],
                                 b2[0:nE, {"f0": 0, "f1": 1, "f3": 2}[key], :], start=True, stop=True)
                    ins.then_inc(sem("b2"), 1)
                    reader[M[1]] = at(key, "b2a", hf + 1)

                if key == "f1":
                    up(key, 0)
                for u in range(2 * nE):
                    hf, e = divmod(u, nE)
                    if u + 1 < 2 * nE:
                        up(key, u + 1)
                    down(u)
                    if key == "f1" and u in (2, 3, 5):
                        inner_layer(1, (2, 3, 5).index(u))
                    if key != "f1" and u == 1:
                        turn_norm(key, 1)
                    if u == (6 if key == "f1" else 2):
                        logits(key, 1)
                    if e == bias_step(key, hf) and key != "f2":
                        weights_turned(hf)
                    if e == bias_step(key, hf) + 1 and key != "f2":
                        biases(hf)
                    if key == "f0" and 5 <= u < 10:
                        wide_weights(u - 5)
                    if u == KV_STEP.get(key, 99):
                        keys(NEXT[key])
                    if u == KV_STEP.get(key, 99) + 1:
                        values(NEXT[key])
                    if u == nE + 2 and nxt:
                        turn_norm(nxt, 0)
                    if u == nE + 3 and nxt in NARROW:
                        queries(nxt, 0)

            def inner_layer(hf, stage):
                if stage == 0:
                    turn("f1", hf, xm, lambda t: (sem("f1.n"), hf + 1))
                elif stage == 1:
                    pe.wait_ge(*at(f"f1.{hf}", "nT", 1))
                    k = bank_of(f"f1.{hf}", 1)
                    dst = take(k)
                    for i in range(4):
                        t = 4 * hf + i
                        ins = mm(dst[:, 128 * i:128 * (i + 1)], nT[0][:, 128 * t:128 * (t + 1)], mixw[:, :], start=True, stop=True)
                    ins.then_inc(sem("f1.mix"), 1)
                    reader[k] = (sem("f1.m"), hf + 1)
                else:
                    turn("f1n", hf, xn, lambda t: (sem("f1.n2"), hf + 1))

            def wide_attention():
                turn_norm("a1", 1)
                pe.wait_ge(*at("a1.1", "nT", 1))
                xq = nT[0][:, :].rearrange("p (b s q) -> p b s q", b=B, s=2)
                for qh in range(2):
                    for m in range(2 * H1):
                        h = m % H1
                        k = qh * H1 + h
                        kb = 4 + m % 4
                        dst = take(kb)
                        mm(dst[:, :].rearrange("p (b q) -> p b q", b=B), (WQ, AQK)[m // H1][:, h, :], xq[:, :, qh, :],
                           start=True, stop=True).then_inc(sem("a1.t"), 1)
                        reader[kb] = (sem("a1.te" if m >= H1 else "a1.qf"), k + 1)
                    pe.wait_ge(sem("a1.te"), 8 * (qh + 1))

                    def content(u):
                        qb, c = divmod(u, 2)
                        dst = take(M[u % 2])[:, :].rearrange("p (q n) -> p q n", n=BH1)
                        for b in range(B):
                            ins = mm(dst[:, :, H1 * b:H1 * (b + 1)], cT[:, S * b + 128 * c:S * b + 128 * (c + 1)],
                                     T1[:, 16 * qb:16 * qb + 16, H1 * b:H1 * (b + 1)], start=True, stop=True)
                        ins.then_inc(sem("a1.C"), 1)
                        reader[M[u % 2]] = (sem("a1.cs"), qh * 16 + u + 1)

                    def position(u, g):
                        qb, c = divmod(u, 2)
                        m = 64 * qh + 4 * u + g
                        dst = take(m % 6)
                        for j in range(4):
                            q = 16 * qb + 4 * g + j
                            off = S - 1 - (128 * qh + q) + 128 * c
                            for part in range(3):
                                ins = mm(dst[:, 96 * j + 32 * part:96 * (j + 1)].rearrange("p (i n) -> p i n", n=BH1),
                                         PW[part][:, off:off + 128], Q1all[:, 0:3 - part, q, :],
                                         start=j == 0 and part == 0, stop=j == 3 and part == 2, skip_group_check=True)
                        ins.then_inc(sem("a1.S"), 1)
                        reader[m % 6] = (sem("a1.sr"), m + 1)

                    for u in range(2):
                        content(u)
                    pe.wait_ge(sem("a1.q"), 8 * (qh + 1))
                    pe.wait_ge(sem("a1.pw"), 1)
                    for u in range(16):
                        for g in range(4):
                            position(u, g)
                        if u + 2 < 16:
                            content(u + 2)
                    pe.wait_ge(sem("a1.st"), 16 * (qh + 1))

                    def scores_q(i, j):
                        b, h = divmod(j, H1)
                        dst = take(i % 2)
                        for c in range(2):
                            ins = tr(dst[:, 128 * c:128 * (c + 1)], ST[:, c, j, :], ident[:, :])
                        ins.then_inc(sem("a1.T0"), 1)
                        reader[i % 2] = (sem("a1.e"), i + 1)

                    def probs_t(i, j):
                        pe.wait_ge(sem("a1.p"), i + 1)
                        dst = take(2 + i % 2)
                        for c in range(2):
                            ins = tr(dst[:, 128 * c:128 * (c + 1)], P[i % 2][:, 0, 128 * c:128 * (c + 1)], ident[:, :])
                        ins.then_inc(sem("a1.T1"), 1)
                        reader[2 + i % 2] = (sem("a1.pte"), i + 1)

                    def probs_ctx(i, j):
                        b = j // H1
                        pe.wait_ge(sem("a1.pte"), i + 1)
                        dst = take(4 + i % 2)
                        for c in range(2):
                            ins = mm(dst[:, 0:128], cx[:, 2 * b + c, :], PTs[i % 2][:, 0, 128 * c:128 * (c + 1)], start=c == 0, stop=c == 1)
                        ins.then_inc(sem("a1.G"), 1)
                        reader[4 + i % 2] = (sem("a1.g"), i + 1)

                    def out_head(i, j):
                        b, h = divmod(j, H1)
                        pe.wait_ge(sem("a1.g"), i + 1)
                        dst = take(out_bank(qh, b)) if h == 0 else bank[out_bank(qh, b)]
                        mm(dst[:, 0:128], GT[i % 2], CVO[:, h, :], start=h == 0, stop=h == H1 - 1).then_inc(sem("a1.o"), 1)
                        if h == H1 - 1:
                            reader[out_bank(qh, b)] = at("a1", "x", B * qh + b + 1)

                    i0 = qh * 32
                    for j in range(32 + 4):
                        if j < 32:
                            scores_q(i0 + j, j)
                        if 2 <= j <= 33:
                            probs_t(i0 + j - 2, j - 2)
                        if 3 <= j <= 34:
                            probs_ctx(i0 + j - 3, j - 3)
                        if 4 <= j <= 35:
                            out_head(i0 + j - 4, j - 4)
                        if qh and j in (26, 29, 33):
                            inner_layer(0, (26, 29, 33).index(j))

            for key in ORDER:
                if key in NARROW:
                    attention(key)
                elif key == "a1":
                    wide_attention()
                else:
                    if key == "f1":
                        logits(key, 0)
                    ffn(key, nT[1])


def kernel(**inputs):
    import numpy as np
    import concourse.bacc as bacc
    from concourse.bass_utils import run_bass_kernel_spmd

    g = {k: np.asarray(v) for k, v in inputs.items()}
    T = lambda a, *p: np.ascontiguousarray(np.transpose(a, p or None))
    row = np.arange(WIN) - (S - 1) + POS // 2
    row = np.clip(np.where(row < 0, row + POS, row), 0, POS - 1)
    cols = lambda a: np.ascontiguousarray(a.reshape(-1, 128).T)
    aw = []
    for n in ("L0_xattn_W_", "L2_xattn_w_", "L3_xattn_W"):
        aw += [T(g[n + s]) for s in "qkvo"]
    a = {
        "x": g["x"].reshape(TOK, D), "ctx": g["ctx_1024"].reshape(TOK, D), "lens": g["_lenS2"],
        "mask1": np.ascontiguousarray(g["mask_BxS2_bf1"].reshape(2 * B, 128).T).view(np.uint8),
        "mask2": g["mask_1x1xSxS2_if1"].reshape(S, S),
        "aw": np.stack(aw),
        "qkb": T(np.stack([g["L3_xattn_bq"], g["L3_xattn_bk"]])),
        "rows": np.stack([g["L1_ffn_g1"], g["L1_ffn_be1"], g["L1_ffn_mix_b"], g["L1_ffn_g2"], g["L1_ffn_be2"],
                          g["L3_xattn_bv"], g["L3_xattn_bo"]]),
        "rb": np.stack([g["L0_ffn_router_b"], g["L3_ffn_br"]]),
        "rw": np.stack([T(g["L0_ffn_router_w"]), g["L1_ffn_router_w"], g["L2_ffn_Wr"], g["L3_ffn_wr"]]),
        "mixw": g["L1_ffn_mix_w"],
        "bu": g["L1_xattn_bu"], "bv": g["L1_xattn_bv"],
        "a1.wqT": T(g["L1_xattn_wq"], 1, 2, 0), "a1.wkT": T(g["L1_xattn_wk"], 1, 2, 0),
        "a1.wvT": T(g["L1_xattn_wv"], 1, 2, 0), "a1.wo": g["L1_xattn_wo"], "a1.wq": T(g["L1_xattn_wq"], 0, 2, 1),
        "a1.pos": T(g["L1_xattn_pos_w"][row]),
        "f0.w1": np.concatenate([T(g["L0_ffn_spec_w1"], 0, 2, 1), T(g["L0_ffn_shared_w1"])[None]]),
        "f0.w2": np.concatenate([T(g["L0_ffn_spec_w2"], 0, 2, 1), T(g["L0_ffn_shared_w2"])[None]]),
        "f0.b1": cols(np.concatenate([g["L0_ffn_spec_b1"], g["L0_ffn_shared_b1"][None]])),
        "f0.b2": np.concatenate([g["L0_ffn_spec_b2"], g["L0_ffn_shared_b2"][None]]),
        "f1.w1": g["L1_ffn_w1"], "f1.w2": g["L1_ffn_w2"], "f1.b1": cols(g["L1_ffn_b1"]), "f1.b2": g["L1_ffn_b2"],
        "f2.w1": g["L2_ffn_W1"], "f2.w2": g["L2_ffn_W2"],
        "f3.w1": g["L3_ffn_w1"], "f3.w2": g["L3_ffn_w2"], "f3.b1": cols(g["L3_ffn_b1"]), "f3.b2": g["L3_ffn_b2"],
    }
    nc = bacc.Bacc("TRN2", target_bir_lowering=False, num_devices=1)
    arrays, handles = {}, {}
    for name, v in a.items():
        dram = "in_" + name.replace(".", "_")
        arrays[dram] = np.ascontiguousarray(v)
        handles[name] = nc.dram_tensor(dram, v.shape, mybir.dt.from_np(v.dtype), kind="ExternalInput").ap()
    o = nc.dram_tensor("out_x", (TOK, D), mybir.dt.float32, kind="ExternalOutput").ap()
    build(nc, handles, o)
    r = run_bass_kernel_spmd(nc, [arrays], core_ids=[0])
    return r.results[0]["out_x"].reshape(B, S, D)
```
